# Optimizing a Trainium2 kernel written in Bass

```python
import numpy as np
import jax
import jax.numpy as jnp

def _softmax(x, axis=-1):
    return jax.nn.softmax(x, axis=axis)

def _gelu(x):
    return jax.nn.gelu(x, approximate=True)

def _silu(x):
    return jax.nn.silu(x)

def _sigmoid(x):
    return jax.nn.sigmoid(x)

def _layernorm(x, axis=-1, eps=1e-05):
    m = jnp.mean(x, axis=axis, keepdims=True)
    v = jnp.var(x, axis=axis, keepdims=True)
    return (x - m) / jnp.sqrt(v + eps)

def _scatter_add(tgt, idx, src, axis=0):
    return tgt.at[idx].add(src)

def _segment_sum(src, seg, n):
    return jax.ops.segment_sum(src, seg, n)
kernel_name = 'mk_xattn_seq_d2_seqx_r4_f9066c'

def setup_inputs(seed: int=0):
    np.random.seed(seed)
    _w = jnp.asarray

    def _rec_inputs():
        import jax
        import jax.numpy as jnp
        _rk = jax.random.key(seed)
        x = 7.22e-05 + 1 * jax.random.normal(jax.random.fold_in(_rk, 1), (16, 100, 512), jnp.float32)
        _lenS = 100 - jax.random.randint(jax.random.fold_in(_rk, 7), (16,), 0, max(1, 100 // 4) + 1, jnp.int32)
        _lenS2 = 361 - jax.random.randint(jax.random.fold_in(_rk, 8), (16,), 0, max(1, 361 // 4) + 1, jnp.int32)
        _ctx_2048P = jax.random.normal(jax.random.fold_in(_rk, 11), (16, 16, 512), jnp.float32)
        _ctx_2048c = jax.random.dirichlet(jax.random.fold_in(_rk, 511), 0.3 * jnp.ones((16,), jnp.float32), (16, 361))
        _ctx_2048t = jnp.einsum('bsk,bkd->bsd', _ctx_2048c, _ctx_2048P)
        _ctx_2048t = _ctx_2048t * jax.lax.rsqrt(jnp.mean(jnp.square(_ctx_2048t)) + 1e-12) * 0.953939
        ctx_2048 = 3.03215e-05 + 0.0999827 * (_ctx_2048t + 0.3 * jax.random.normal(jax.random.fold_in(_rk, 611), (16, 361, 512), jnp.float32))
        _validS = jnp.arange(100)[None, :] < _lenS[:, None]
        _validS2 = jnp.arange(361)[None, :] < _lenS2[:, None]
        _causal = jnp.tril(jnp.ones((100, 100), dtype=bool))
        mask_BxS2_ik0 = jnp.where(jnp.broadcast_to(_validS2[:, :], (16, 361)), 0, 1).astype(jnp.int32)
        return (x, ctx_2048, mask_BxS2_ik0)
    x, ctx_2048, mask_BxS2_ik0 = _rec_inputs()

    def _L0_xattn_setup():
        import jax, jax.numpy as jnp
        import numpy as np
        N_HEAD = 32
        EPS = 1e-05

        def _ln(x, w, b):
            m = jnp.mean(x, axis=-1, keepdims=True)
            v = jnp.mean((x - m) ** 2, axis=-1, keepdims=True)
            return (x - m) * jax.lax.rsqrt(v + EPS) * w + b

        def _forward(x, state, i, ln1_w, ln1_b, ln2_w, ln2_b, maa_x, maa_w, maa_k, maa_v, maa_r, maa_g, maa_w1, maa_w2, time_decay, decay_w1, decay_w2, faaaa, Wr, Wk, Wv, Wg, Wo, gn_w, gn_b, fmaa_k, fmaa_r, fWk, fWr, fWv):
            B, L, C = x.shape
            H = N_HEAD
            S = C // H
            i0 = (2 + S) * i
            xa = _ln(x, ln1_w, ln1_b)
            sx = jnp.concatenate([state[:, i0 + 1][:, None], xa[:, :-1]], axis=1) - xa
            xxx = xa + sx * maa_x
            t = jnp.tanh(xxx @ maa_w1).reshape(B, L, 5, -1)
            m = jnp.einsum('blfd,fdc->blfc', t, maa_w2)
            mw, mk, mv, mr, mg = (m[:, :, j] for j in range(5))
            xw = xa + sx * (maa_w + mw)
            xk = xa + sx * (maa_k + mk)
            xv = xa + sx * (maa_v + mv)
            xr = xa + sx * (maa_r + mr)
            xg = xa + sx * (maa_g + mg)
            w = time_decay + jnp.tanh(xw @ decay_w1) @ decay_w2
            w = jnp.exp(-jnp.exp(w)).reshape(B, L, H, S)
            r = (xr @ Wr.T).reshape(B, L, H, S)
            k = (xk @ Wk.T).reshape(B, L, H, S)
            v = (xv @ Wv.T).reshape(B, L, H, S)
            g = jax.nn.silu(xg @ Wg.T)
            s0 = state[:, i0 + 2:i0 + 2 + S].reshape(B, H, S, S)

            def step(s, inp):
                k_l, v_l, w_l, r_l = inp
                a = k_l[..., :, None] * v_l[..., None, :]
                out = jnp.einsum('bhs,bhst->bht', r_l, faaaa * a + s)
                s_new = a + w_l[..., None] * s
                return (s_new, out)
            seq = tuple((z.transpose(1, 0, 2, 3) for z in (k, v, w, r)))
            _, outs = jax.lax.scan(step, s0, seq)
            y = outs.transpose(1, 0, 2, 3)
            gm = jnp.mean(y, axis=-1, keepdims=True)
            gv = jnp.mean((y - gm) ** 2, axis=-1, keepdims=True)
            y = ((y - gm) * jax.lax.rsqrt(gv + EPS)).reshape(B, L, C) * gn_w + gn_b
            x = x + y * g @ Wo.T
            xc = _ln(x, ln2_w, ln2_b)
            sxc = jnp.concatenate([state[:, i0][:, None], xc[:, :-1]], axis=1) - xc
            xk2 = xc + sxc * fmaa_k
            xr2 = xc + sxc * fmaa_r
            rr = jax.nn.sigmoid(xr2 @ fWr.T)
            kk = jnp.square(jax.nn.relu(xk2 @ fWk.T))
            x = x + rr * (kk @ fWv.T)
            return x
        key = jax.random.key(seed)
        B, L, C, H = (8, 128, 512, N_HEAD)
        S = C // H
        DM, DD = (32, 64)
        ks = jax.random.split(key, 32)
        n = lambda k, shp, s=1.0: jax.random.normal(k, shp, dtype=jnp.float32) * s
        u = lambda k, shp: jax.random.uniform(k, shp, dtype=jnp.float32)
        inp = {'x': n(ks[0], (B, L, C)), 'state': n(ks[1], (B, 2 + S, C), 0.1), 'i': 0, 'ln1_w': jnp.ones((C,), jnp.float32), 'ln1_b': jnp.zeros((C,), jnp.float32), 'ln2_w': jnp.ones((C,), jnp.float32), 'ln2_b': jnp.zeros((C,), jnp.float32), 'maa_x': u(ks[2], (C,)), 'maa_w': u(ks[3], (C,)), 'maa_k': u(ks[4], (C,)), 'maa_v': u(ks[5], (C,)), 'maa_r': u(ks[6], (C,)), 'maa_g': u(ks[7], (C,)), 'maa_w1': n(ks[8], (C, 5 * DM), 0.02), 'maa_w2': n(ks[9], (5, DM, C), 0.02), 'time_decay': n(ks[10], (C,), 0.5), 'decay_w1': n(ks[11], (C, DD), 0.02), 'decay_w2': n(ks[12], (DD, C), 0.02), 'faaaa': n(ks[13], (H, S, 1), 0.1), 'Wr': n(ks[14], (C, C), 0.02), 'Wk': n(ks[15], (C, C), 0.02), 'Wv': n(ks[16], (C, C), 0.02), 'Wg': n(ks[17], (C, C), 0.02), 'Wo': n(ks[18], (C, C), 0.02), 'gn_w': jnp.ones((C,), jnp.float32), 'gn_b': jnp.zeros((C,), jnp.float32), 'fmaa_k': u(ks[19], (C,)), 'fmaa_r': u(ks[20], (C,)), 'fWk': n(ks[21], (C, C), 0.02), 'fWr': n(ks[22], (C, C), 0.02), 'fWv': n(ks[23], (C, C), 0.02)}
        return inp
    _L0_xattn_all = _L0_xattn_setup()
    _L0_xattn_in = {k: v for k, v in _L0_xattn_all.items() if k in ('ln1_w', 'ln1_b', 'ln2_w', 'ln2_b', 'maa_x', 'maa_w', 'maa_k', 'maa_v', 'maa_r', 'maa_g', 'maa_w1', 'maa_w2', 'time_decay', 'decay_w1', 'decay_w2', 'faaaa', 'Wr', 'Wk', 'Wv', 'Wg', 'Wo', 'gn_w', 'gn_b', 'fmaa_k', 'fmaa_r', 'fWk', 'fWr', 'fWv')}
    del _L0_xattn_all

    def _L1_xattn_setup():
        import jax, jax.numpy as jnp
        import numpy as np
        B, P, K, H, NH = (4, 512, 64, 512, 16)
        DH = H // NH
        EPS = 1e-06

        def rmsnorm(x, w):
            var = jnp.mean(jnp.square(x), axis=-1, keepdims=True)
            return x * jax.lax.rsqrt(var + EPS) * w
        key = jax.random.key(seed)
        ks = jax.random.split(key, 12)
        s = 0.02
        return {'x': jax.random.normal(ks[0], (B, P, H), jnp.float32), 'latents': jax.random.normal(ks[1], (B, K, H), jnp.float32), 'attention_mask': jax.random.randint(ks[2], (B, P), 0, 2, jnp.int32), 'q_w': s * jax.random.normal(ks[3], (H, H), jnp.float32), 'q_b': jnp.zeros((H,), jnp.float32), 'kv_w': s * jax.random.normal(ks[4], (H, 2 * H), jnp.float32), 'kv_b': jnp.zeros((2 * H,), jnp.float32), 'out_w': s * jax.random.normal(ks[5], (H, H), jnp.float32), 'out_b': jnp.zeros((H,), jnp.float32), 'postnorm_w': jnp.ones((H,), jnp.float32), 'mlp_w1': s * jax.random.normal(ks[6], (H, 4 * H), jnp.float32), 'mlp_b1': jnp.zeros((4 * H,), jnp.float32), 'mlp_w2': s * jax.random.normal(ks[7], (4 * H, H), jnp.float32), 'mlp_b2': jnp.zeros((H,), jnp.float32)}
    _L1_xattn_all = _L1_xattn_setup()
    _L1_xattn_in = {k: v for k, v in _L1_xattn_all.items() if k in ('q_w', 'q_b', 'kv_w', 'kv_b', 'out_w', 'out_b', 'postnorm_w', 'mlp_w1', 'mlp_b1', 'mlp_w2', 'mlp_b2')}
    del _L1_xattn_all
    return {'x': x, 'ctx_2048': ctx_2048, 'mask_BxS2_ik0': mask_BxS2_ik0, 'L0_xattn_ln1_w': _L0_xattn_in['ln1_w'], 'L0_xattn_ln1_b': _L0_xattn_in['ln1_b'], 'L0_xattn_ln2_w': _L0_xattn_in['ln2_w'], 'L0_xattn_ln2_b': _L0_xattn_in['ln2_b'], 'L0_xattn_maa_x': _L0_xattn_in['maa_x'], 'L0_xattn_maa_w': _L0_xattn_in['maa_w'], 'L0_xattn_maa_k': _L0_xattn_in['maa_k'], 'L0_xattn_maa_v': _L0_xattn_in['maa_v'], 'L0_xattn_maa_r': _L0_xattn_in['maa_r'], 'L0_xattn_maa_g': _L0_xattn_in['maa_g'], 'L0_xattn_maa_w1': _L0_xattn_in['maa_w1'], 'L0_xattn_maa_w2': _L0_xattn_in['maa_w2'], 'L0_xattn_time_decay': _L0_xattn_in['time_decay'], 'L0_xattn_decay_w1': _L0_xattn_in['decay_w1'], 'L0_xattn_decay_w2': _L0_xattn_in['decay_w2'], 'L0_xattn_faaaa': _L0_xattn_in['faaaa'], 'L0_xattn_Wr': _L0_xattn_in['Wr'], 'L0_xattn_Wk': _L0_xattn_in['Wk'], 'L0_xattn_Wv': _L0_xattn_in['Wv'], 'L0_xattn_Wg': _L0_xattn_in['Wg'], 'L0_xattn_Wo': _L0_xattn_in['Wo'], 'L0_xattn_gn_w': _L0_xattn_in['gn_w'], 'L0_xattn_gn_b': _L0_xattn_in['gn_b'], 'L0_xattn_fmaa_k': _L0_xattn_in['fmaa_k'], 'L0_xattn_fmaa_r': _L0_xattn_in['fmaa_r'], 'L0_xattn_fWk': _L0_xattn_in['fWk'], 'L0_xattn_fWr': _L0_xattn_in['fWr'], 'L0_xattn_fWv': _L0_xattn_in['fWv'], 'L1_xattn_q_w': _L1_xattn_in['q_w'], 'L1_xattn_q_b': _L1_xattn_in['q_b'], 'L1_xattn_kv_w': _L1_xattn_in['kv_w'], 'L1_xattn_kv_b': _L1_xattn_in['kv_b'], 'L1_xattn_out_w': _L1_xattn_in['out_w'], 'L1_xattn_out_b': _L1_xattn_in['out_b'], 'L1_xattn_postnorm_w': _L1_xattn_in['postnorm_w'], 'L1_xattn_mlp_w1': _L1_xattn_in['mlp_w1'], 'L1_xattn_mlp_b1': _L1_xattn_in['mlp_b1'], 'L1_xattn_mlp_w2': _L1_xattn_in['mlp_w2'], 'L1_xattn_mlp_b2': _L1_xattn_in['mlp_b2']}

def reference(x, ctx_2048, mask_BxS2_ik0, L0_xattn_ln1_w, L0_xattn_ln1_b, L0_xattn_ln2_w, L0_xattn_ln2_b, L0_xattn_maa_x, L0_xattn_maa_w, L0_xattn_maa_k, L0_xattn_maa_v, L0_xattn_maa_r, L0_xattn_maa_g, L0_xattn_maa_w1, L0_xattn_maa_w2, L0_xattn_time_decay, L0_xattn_decay_w1, L0_xattn_decay_w2, L0_xattn_faaaa, L0_xattn_Wr, L0_xattn_Wk, L0_xattn_Wv, L0_xattn_Wg, L0_xattn_Wo, L0_xattn_gn_w, L0_xattn_gn_b, L0_xattn_fmaa_k, L0_xattn_fmaa_r, L0_xattn_fWk, L0_xattn_fWr, L0_xattn_fWv, L1_xattn_q_w, L1_xattn_q_b, L1_xattn_kv_w, L1_xattn_kv_b, L1_xattn_out_w, L1_xattn_out_b, L1_xattn_postnorm_w, L1_xattn_mlp_w1, L1_xattn_mlp_b1, L1_xattn_mlp_w2, L1_xattn_mlp_b2):
    import jax
    import jax.numpy as jnp

    def _L0_xattn_ref(x, state, i, ln1_w, ln1_b, ln2_w, ln2_b, maa_x, maa_w, maa_k, maa_v, maa_r, maa_g, maa_w1, maa_w2, time_decay, decay_w1, decay_w2, faaaa, Wr, Wk, Wv, Wg, Wo, gn_w, gn_b, fmaa_k, fmaa_r, fWk, fWr, fWv):
        import jax, jax.numpy as jnp
        import numpy as np
        N_HEAD = 32
        EPS = 1e-05

        def _ln(x, w, b):
            m = jnp.mean(x, axis=-1, keepdims=True)
            v = jnp.mean((x - m) ** 2, axis=-1, keepdims=True)
            return (x - m) * jax.lax.rsqrt(v + EPS) * w + b

        def _forward(x, state, i, ln1_w, ln1_b, ln2_w, ln2_b, maa_x, maa_w, maa_k, maa_v, maa_r, maa_g, maa_w1, maa_w2, time_decay, decay_w1, decay_w2, faaaa, Wr, Wk, Wv, Wg, Wo, gn_w, gn_b, fmaa_k, fmaa_r, fWk, fWr, fWv):
            B, L, C = x.shape
            H = N_HEAD
            S = C // H
            i0 = (2 + S) * i
            xa = _ln(x, ln1_w, ln1_b)
            sx = jnp.concatenate([state[:, i0 + 1][:, None], xa[:, :-1]], axis=1) - xa
            xxx = xa + sx * maa_x
            t = jnp.tanh(xxx @ maa_w1).reshape(B, L, 5, -1)
            m = jnp.einsum('blfd,fdc->blfc', t, maa_w2)
            mw, mk, mv, mr, mg = (m[:, :, j] for j in range(5))
            xw = xa + sx * (maa_w + mw)
            xk = xa + sx * (maa_k + mk)
            xv = xa + sx * (maa_v + mv)
            xr = xa + sx * (maa_r + mr)
            xg = xa + sx * (maa_g + mg)
            w = time_decay + jnp.tanh(xw @ decay_w1) @ decay_w2
            w = jnp.exp(-jnp.exp(w)).reshape(B, L, H, S)
            r = (xr @ Wr.T).reshape(B, L, H, S)
            k = (xk @ Wk.T).reshape(B, L, H, S)
            v = (xv @ Wv.T).reshape(B, L, H, S)
            g = jax.nn.silu(xg @ Wg.T)
            s0 = state[:, i0 + 2:i0 + 2 + S].reshape(B, H, S, S)

            def step(s, inp):
                k_l, v_l, w_l, r_l = inp
                a = k_l[..., :, None] * v_l[..., None, :]
                out = jnp.einsum('bhs,bhst->bht', r_l, faaaa * a + s)
                s_new = a + w_l[..., None] * s
                return (s_new, out)
            seq = tuple((z.transpose(1, 0, 2, 3) for z in (k, v, w, r)))
            _, outs = jax.lax.scan(step, s0, seq)
            y = outs.transpose(1, 0, 2, 3)
            gm = jnp.mean(y, axis=-1, keepdims=True)
            gv = jnp.mean((y - gm) ** 2, axis=-1, keepdims=True)
            y = ((y - gm) * jax.lax.rsqrt(gv + EPS)).reshape(B, L, C) * gn_w + gn_b
            x = x + y * g @ Wo.T
            xc = _ln(x, ln2_w, ln2_b)
            sxc = jnp.concatenate([state[:, i0][:, None], xc[:, :-1]], axis=1) - xc
            xk2 = xc + sxc * fmaa_k
            xr2 = xc + sxc * fmaa_r
            rr = jax.nn.sigmoid(xr2 @ fWr.T)
            kk = jnp.square(jax.nn.relu(xk2 @ fWk.T))
            x = x + rr * (kk @ fWv.T)
            return x
        return _forward(x, state, i, ln1_w, ln1_b, ln2_w, ln2_b, maa_x, maa_w, maa_k, maa_v, maa_r, maa_g, maa_w1, maa_w2, time_decay, decay_w1, decay_w2, faaaa, Wr, Wk, Wv, Wg, Wo, gn_w, gn_b, fmaa_k, fmaa_r, fWk, fWr, fWv)

    def _L1_xattn_ref(x, latents, attention_mask, q_w, q_b, kv_w, kv_b, out_w, out_b, postnorm_w, mlp_w1, mlp_b1, mlp_w2, mlp_b2):
        import jax, jax.numpy as jnp
        import numpy as np
        B, P, K, H, NH = (4, 512, 64, 512, 16)
        DH = H // NH
        EPS = 1e-06

        def rmsnorm(x, w):
            var = jnp.mean(jnp.square(x), axis=-1, keepdims=True)
            return x * jax.lax.rsqrt(var + EPS) * w
        b, p, _ = x.shape
        k_len = latents.shape[1]
        residual = latents
        h = jnp.concatenate([x, latents], axis=1)
        q = (latents @ q_w + q_b).reshape(b, k_len, NH, DH)
        kv = (h @ kv_w + kv_b).reshape(b, p + k_len, NH, DH, 2)
        kmat, v = (kv[..., 0], kv[..., 1])
        attn = jnp.einsum('bkhd,bnhd->bhkn', q, kmat) / DH
        full_mask = jnp.concatenate([attention_mask.astype(bool), jnp.ones((b, k_len), bool)], axis=-1)
        attn = jnp.where(full_mask[:, None, None, :], attn, -jnp.inf)
        attn = jax.nn.softmax(attn.astype(jnp.float32), axis=-1).astype(q.dtype)
        attn_out = jnp.einsum('bhkn,bnhd->bkhd', attn, v).reshape(b, k_len, H)
        attn_out = attn_out @ out_w + out_b + residual
        out = rmsnorm(attn_out, postnorm_w)
        out = jax.nn.gelu(out @ mlp_w1 + mlp_b1) @ mlp_w2 + mlp_b2
        return out + residual
    x = _L0_xattn_ref(x, ctx_2048, 0, L0_xattn_ln1_w, L0_xattn_ln1_b, L0_xattn_ln2_w, L0_xattn_ln2_b, L0_xattn_maa_x, L0_xattn_maa_w, L0_xattn_maa_k, L0_xattn_maa_v, L0_xattn_maa_r, L0_xattn_maa_g, L0_xattn_maa_w1, L0_xattn_maa_w2, L0_xattn_time_decay, L0_xattn_decay_w1, L0_xattn_decay_w2, L0_xattn_faaaa, L0_xattn_Wr, L0_xattn_Wk, L0_xattn_Wv, L0_xattn_Wg, L0_xattn_Wo, L0_xattn_gn_w, L0_xattn_gn_b, L0_xattn_fmaa_k, L0_xattn_fmaa_r, L0_xattn_fWk, L0_xattn_fWr, L0_xattn_fWv)
    x = _L1_xattn_ref(ctx_2048, x, mask_BxS2_ik0, L1_xattn_q_w, L1_xattn_q_b, L1_xattn_kv_w, L1_xattn_kv_b, L1_xattn_out_w, L1_xattn_out_b, L1_xattn_postnorm_w, L1_xattn_mlp_w1, L1_xattn_mlp_b1, L1_xattn_mlp_w2, L1_xattn_mlp_b2)
    return x

_drawn_inputs = setup_inputs


def setup_inputs(seed=0):
    import zlib

    import numpy as np

    out = dict(_drawn_inputs(seed))
    spreads = {'L0_xattn_ln1_w': (1.0, 0.2),
     'L0_xattn_ln1_b': (0.0, 0.1),
     'L0_xattn_ln2_w': (1.0, 0.6),
     'L0_xattn_ln2_b': (0.0, 0.8),
     'L0_xattn_gn_w': (1.0, 0.6),
     'L0_xattn_gn_b': (0.0, 0.8),
     'L1_xattn_q_b': (0.0, 0.8),
     'L1_xattn_kv_b': (0.0, 0.775),
     'L1_xattn_out_b': (0.0, 1.549),
     'L1_xattn_postnorm_w': (1.0, 0.2),
     'L1_xattn_mlp_b1': (0.0, 0.1),
     'L1_xattn_mlp_b2': (0.0, 0.1)}
    factors = {'ctx_2048': 5.784,
     'L0_xattn_maa_x': 6.572,
     'L0_xattn_maa_w': 8.0,
     'L0_xattn_maa_w1': 3.43,
     'L0_xattn_maa_w2': 3.448,
     'L0_xattn_decay_w1': 8.0,
     'L0_xattn_decay_w2': 8.0,
     'L0_xattn_faaaa': 3.716,
     'L0_xattn_fmaa_r': 8.0,
     'L0_xattn_fWr': 7.554,
     'L1_xattn_q_w': 8.0,
     'L1_xattn_kv_w': 8.0,
     'L1_xattn_out_w': 5.214}
    for name, (base, spread) in spreads.items():
        noise = np.random.default_rng([zlib.crc32(name.encode()), seed]).standard_normal(out[name].shape)
        drawn = base * np.exp(spread * noise) if base else spread * noise
        out[name] = jnp.asarray(drawn.astype(out[name].dtype))
    for name, factor in factors.items():
        out[name] = (out[name] * factor).astype(out[name].dtype)
    return out
```

```python
from contextlib import ExitStack

import numpy as np

import concourse.bass as bass
from concourse import mybir

F32 = mybir.dt.float32
I32 = mybir.dt.int32
ALU = mybir.AluOpType
ACT = mybir.ActivationFunctionType

P = 128
SEQS, LEN, C = 16, 100, 512
CTX = 361
CT = C // P
GROUPS = 4
GB = SEQS // GROUPS
GT = GB * LEN
TOK = SEQS * LEN
RH, RS = 32, 16
HPT = P // RS
MIX, MIXR = 5, 32
DECR = 64
AH, AD = 16, 32
KEYS = CTX + LEN
KT_N = 4
KT_W = 116
KPAD = KT_N * KT_W
FF = 4 * C
FT = FF // P
QUADS = RS // 4
UNITS = CT * QUADS
RING = 4
LN_EPS, RMS_EPS = 1e-5, 1e-6
MASKED = -3.0e38
ARENA = 27300

VECS = ["ln1_w", "ln1_b", "ln2_w", "ln2_b", "maa_x", "maa_w", "maa_k", "maa_v", "maa_r", "maa_g",
        "time_decay", "faaaa", "gn_w", "gn_b", "fmaa_k", "fmaa_r", "q_b", "k_b", "v_b", "out_b",
        "postnorm_w", "mlp_b2"]
NVEC = len(VECS) * CT + FT


def spread(ap, axis, n):
    a = ap.unsqueeze(axis)
    return a.broadcast_to(list(a.shape[:axis]) + [n] + list(a.shape[axis + 1:]))


class Signal:

    def __init__(self, nc, ctx, name, per=1):
        self.sem, self.per = ctx.enter_context(nc.semaphore(name)), per

    def at(self, turn, k=None):
        k = self.per if k is None else k
        return turn * self.per + k


class Results:

    def __init__(self, nc, ctx, name, banks, readers):
        self.banks, self.readers = banks, list(readers.values())
        self.order = {key: i for i, key in enumerate(readers)}
        n = len(banks)
        self.full = [Signal(nc, ctx, f"{name}{b}_full", len(self.readers[b::n])) for b in range(n)]

    def claim(self, eng, turn, key):
        i, n = self.order[key], len(self.banks)
        if i >= n:
            signal, k = self.readers[i - n]
            eng.wait_ge(signal.sem, signal.at(turn, k))
        else:
            signal, _ = self.readers[i::n][-1]
            eng.wait_ge(signal.sem, signal.at(turn, 0))
        return self.banks[i % n]

    def filled(self, ins, key):
        ins.then_inc(self.full[self.order[key] % len(self.banks)].sem, 1)

    def take(self, eng, turn, key):
        i, n = self.order[key], len(self.banks)
        full = self.full[i % n]
        eng.wait_ge(full.sem, full.at(turn, i // n + 1))
        return self.banks[i % n]


def rwkv_perceiver(nc, xT, ctxT, mask, edgeT, s0T, vecs, w_mix1, w_mix2, w_dec1, w_dec2, w_rkvg,
                   w_off, w_q, w_kv, w_out, w_mlp1, w_mlp2, heads, heads_sum, heads_back, out):
    with ExitStack() as ctx:
        def sb(name, shape, dt=F32):
            return ctx.enter_context(nc.sbuf_tensor(name, shape, dt))

        vec = sb("vec", [P, NVEC])
        heads_sb = sb("heads_sb", [P, 6 * P + 2 * P - HPT])
        ident = heads_sb[:, 0:P]
        block_ones = heads_sb[:, P:2 * P]
        pick = heads_sb[:, 2 * P:6 * P].rearrange("p (i n) -> p i n", i=4)
        window = heads_sb[:, 6 * P:]
        heads_sum_sb = sb("heads_sum_sb", [P, CT, RH])
        heads_back_sb = sb("heads_back_sb", [RH, CT, P])
        mean_ones = sb("mean_ones", [P, P])
        eps = sb("eps", [P, 2])
        mix1 = sb("mix1", [P, CT, MIX * MIXR])
        mix2a = sb("mix2a", [P, C])
        mix2b = sb("mix2b", [MIXR, C])
        dec1 = sb("dec1", [P, CT, DECR])
        dec2 = sb("dec2", [DECR, C])
        wq = sb("wq", [P, CT, C])
        region1 = sb("region1", [P, 4, CT, C])
        region2 = sb("region2", [P, 4, CT, C])
        arena = sb("arena", [P, ARENA])
        cursor = [0]

        def cut(words):
            a = cursor[0]
            cursor[0] = a + words
            assert cursor[0] <= ARENA, cursor[0]
            return arena[:, a:a + words]

        def tile_ct(words=GT):
            return cut(CT * words).rearrange("p (c n) -> p c n", c=CT)

        wr, wk, wv, wg = (region1[:, i] for i in range(4))
        wo, fwr, fwk, fwv = (region2[:, i] for i in range(4))
        w_k, w_v, w_o = region1[:, 0], region1[:, 1], region1[:, 2]
        w_1 = region2.rearrange("p m c n -> p (m c n)").rearrange("p (c n) -> p c n", c=CT)

        mixed = [tile_ct() for _ in range(MIX)]
        ring = [m.rearrange("p c n -> p (c n)").rearrange("p (j n) -> p j n", j=4) for m in mixed[:RING]]
        xa = tile_ct()
        centred, square, scratch = tile_ct(), tile_ct(), tile_ct()
        shift = tile_ct()
        k_sb, v_sb, r_sb, w_sb, g_sb = (tile_ct() for _ in range(5))
        rk = tile_ct()
        ext = cut(CT * GB * (LEN + 1)).rearrange("p (c b l) -> p c b l", c=CT, b=GB)
        edge_sb = sb("edge_sb", [P, 2, CT, GB])
        s0_sb = sb("s0_sb", [P, CT, QUADS, 4, GB])
        std = sb("std", [P, GT])
        rstd = sb("rstd", [P, GT])
        mix_t4 = sb("mix_t4", [P, GT])
        mix_t1 = sb("mix_t1", [MIXR, GT])
        dec_t = sb("dec_t", [DECR, GT])

        cursor[0] = 0
        w_2 = cut(FT * C).rearrange("p (f n) -> p f n", f=FT)
        hT = [tile_ct(KPAD) for _ in range(2)]
        kT = [tile_ct(KPAD) for _ in range(2)]
        v_tok = [cut(KT_N * C).rearrange("p (k n) -> p k n", k=KT_N) for _ in range(2)]
        qT = [tile_ct(LEN) for _ in range(2)]
        mask_i = [cut(CTX).bitcast(I32) for _ in range(2)]
        mask_f = [cut(KEYS) for _ in range(2)]
        probs = [cut(KPAD) for _ in range(4)]
        probsT = [cut(KT_N * LEN).rearrange("p (k n) -> p k n", k=KT_N) for _ in range(2)]
        row_max, row_sum, row_inv = cut(AH), cut(AH), cut(AH)
        tick = sb("tick", [1, 1])
        o_tok = cut(C)
        o_T = tile_ct(LEN)
        cursor[0] = FT * C
        attn, res, mid, sq_c, out_sb = (tile_ct() for _ in range(5))
        hidden = cut(FT * GT).rearrange("p (f n) -> p f n", f=FT)

        x_mid = nc.dram_tensor("x_mid", [CT, P, TOK], F32, kind="Internal").ap()
        q_mid = nc.dram_tensor("q_mid", [CT, P, TOK], F32, kind="Internal").ap()
        o_mid = nc.dram_tensor("o_mid", [CT, P, TOK], F32, kind="Internal").ap()

        ps_all = ctx.enter_context(nc.psum_tensor("ps_all", [P, 8, 512], F32))
        bank = [ps_all[:, i, :] for i in range(8)]
        ps_v = ps_all[:, 0:4, 0:GT]
        ps_y = ps_all[:, 4, 0:GT]

        def vcol(name, ct):
            i = VECS.index(name) * CT + ct
            return vec[:, i:i + 1]

        def bias1(m):
            return vec[:, len(VECS) * CT + m:len(VECS) * CT + m + 1]

        def by_seq(ap):
            return ap.rearrange("p (b l) -> p b l", b=GB)

        def group_cols(dram, g):
            return dram[:, :, bass.ds(g * GT, GT)].rearrange("c p n -> p c n")

        def sig(name, per=1):
            return Signal(nc, ctx, name, per)

        loaded = sig("loaded")
        consts_set = sig("consts_set", 5)
        group_in = sig("group_in")
        centred_ready = sig("centred_ready", 2)
        square_ready = sig("square_ready", 2)
        std_ready = sig("std_ready", 3)
        rstd_ready = sig("rstd_ready", 3)
        normed = sig("normed", 2)
        ext_ready = sig("ext_ready", 2 * CT)
        edge_ready = sig("edge_ready", 2)
        shift_ready = sig("shift_ready", 2)
        mixx_ready = sig("mixx_ready", CT)
        mix_rank = sig("mix_rank", 2)
        mix_scaled = sig("mix_scaled", MIX * CT)
        mixed_ready = sig("mixed_ready", MIX)
        dec_rank = sig("dec_rank")
        dec_exp = sig("dec_exp", CT)
        w_ready = sig("w_ready", CT)
        k_ready = sig("k_ready", CT)
        v_ready = sig("v_ready", CT)
        r_ready = sig("r_ready", CT)
        g_ready = sig("g_ready", CT)
        rku_ready = sig("rku_ready", CT)
        bonus_ready = sig("bonus_ready", CT)
        vals_full = sig("vals_full", UNITS)
        start_state = sig("start_state", UNITS)
        outer_ready = sig("outer_ready", UNITS)
        scanned = sig("scanned", UNITS)
        weighed = sig("weighed", UNITS)
        summed = sig("summed", UNITS)
        y_copied = sig("y_copied", CT)
        y_added = sig("y_added")
        y_centred = sig("y_centred", CT)
        y_square = sig("y_square", CT)
        y_scaled = sig("y_scaled", CT)
        y_affine = sig("y_affine", CT)
        y_gated = sig("y_gated")
        x2_ready = sig("x2_ready", CT)
        ffk_ready = sig("ffk_ready", CT)
        ffr_ready = sig("ffr_ready", CT)
        rr_ready = sig("rr_ready", CT)
        relu_ready = sig("relu_ready", CT)
        kk_ready = sig("kk_ready", CT)
        ff_ready = sig("ff_ready", CT)
        x3_ready = sig("x3_ready")
        q_ready = sig("q_ready", CT)
        group_out = sig("group_out")

        readers = {"mean1": (centred_ready, 1), "var1": (std_ready, 1), "rank4": (mix_rank, 1), "rank1": (mix_rank, 2)}
        readers |= {("mix", j, ct): (mix_scaled, j * CT + ct + 1) for j in range(MIX) for ct in range(CT)}
        readers |= {"dec1": (dec_rank, 1)} | {("dec2", ct): (dec_exp, ct + 1) for ct in range(CT)}
        readers |= {(n, ct): (s, ct + 1) for n, s in (("k", k_ready), ("v", v_ready), ("r", r_ready)) for ct in range(CT)}
        readers |= {(n, ct): (s, ct + 1) for ct in range(CT) for n, s in (("g", g_ready), ("bonus", bonus_ready))}
        readers |= {("ymean", ct): (y_centred, ct + 1) for ct in range(CT)} | {"yvar": (std_ready, 2)}
        readers |= {("yback", ct): (y_scaled, ct + 1) for ct in range(CT)}
        readers |= {("o", ct): (x2_ready, ct + 1) for ct in range(CT)}
        readers |= {"mean2": (centred_ready, 2), "var2": (std_ready, 3)}
        readers |= {(n, ct): (s, ct + 1) for n, s in (("fr", rr_ready), ("fk", relu_ready), ("fv", ff_ready), ("q", q_ready))
                    for ct in range(CT)}
        ra = Results(nc, ctx, "ra", bank[5:8], readers)

        weights_b = sig("weights_b")
        weights_c = sig("weights_c")
        pads_set = sig("pads_set", 8)
        seq_in = [sig(f"seq_in{p}") for p in range(2)]
        mask_ready = sig("mask_ready", 2)
        kv_full = sig("kv_full", 16)
        k_done = sig("k_done", 2 * CT)
        v_done = sig("v_done", 2 * KT_N)
        s_full = sig("s_full", 2 * AH)
        s_masked = sig("s_masked", 2 * AH)
        p_ready = sig("p_ready", 2 * AH)
        pT_full = sig("pT_full", 2 * AH)
        pT_ready = sig("pT_ready", 2 * AH)
        pv_done = sig("pv_done", 2 * AH)
        inv_ready = sig("inv_ready", 2)
        o_ready = sig("o_ready", 2)
        oT_full = sig("oT_full", 2)
        oT_ready = sig("oT_ready", 2)
        o_stored = sig("o_stored")

        c_in = sig("c_in")
        resid_ready = sig("resid_ready", CT)
        sq_ready = sig("sq_ready")
        cstd_ready = sig("cstd_ready")
        crstd_ready = sig("crstd_ready")
        h_ready = sig("h_ready", CT)
        hid_ready = sig("hid_ready", FT)
        out_ready = sig("out_ready", CT)
        c_out = sig("c_out")
        readers_c = {("o", ct): (resid_ready, ct + 1) for ct in range(CT)} | {"ms": (cstd_ready, 1)}
        readers_c |= {("h", m): (hid_ready, m + 1) for m in range(FT)} | {("y", ct): (out_ready, ct + 1) for ct in range(CT)}
        rc = Results(nc, ctx, "rc", bank[0:4], readers_c)

        block = ctx.enter_context(nc.Block())

        def rows(w):
            return w.rearrange("(c p) n -> p c n", p=P)

        loads = [
            (vec[:, :], vecs), (heads_sb[:, :], heads), (mix1[:, :, :], rows(w_mix1)),
            (mix2a[:, :], w_mix2[0:P, :]), (mix2b[:, :], w_mix2[P:MIX * MIXR, :]),
            (dec1[:, :, :], rows(w_dec1)), (dec2[:, :], w_dec2),
            (heads_sum_sb[:, :, :], heads_sum), (heads_back_sb[:, :, :], heads_back),
            (region1[:, :, :, :], w_rkvg.rearrange("m (c p) n -> p m c n", p=P)),
            (region2[:, :, :, :], w_off.rearrange("m (c p) n -> p m c n", p=P)),
            (wq[:, :, :], rows(w_q)),
        ]
        ALL_LOADED = 16 * len(loads)
        PAIRS = SEQS // 2

        @block.sync
        def _(sp):
            with sp.Fori(0, GROUPS) as g:
                sp.wait_ge(group_out.sem, 32 * g)
                sp.dma_start(xa, group_cols(xT, g)).then_inc(group_in.sem, 16)
                sp.dma_start(edge_sb[:, :, :, :], edgeT[bass.ds(g, 1)].rearrange("o p r c b -> (o p) r c b")).then_inc(group_in.sem, 16)
                sp.dma_start(s0_sb[:, :, :, :], s0T[bass.ds(g, 1)].rearrange("o p c q i b -> (o p) c q i b")).then_inc(group_in.sem, 16)
                sp.wait_ge(x3_ready.sem, x3_ready.at(g))
                sp.dma_start(group_cols(x_mid, g), xa).then_inc(group_out.sem, 16)
                sp.wait_ge(q_ready.sem, q_ready.at(g))
                sp.dma_start(group_cols(q_mid, g), mixed[4]).then_inc(group_out.sem, 16)

            sp.wait_ge(group_out.sem, 32 * GROUPS)
            sp.dma_start(region1[:, 0:2, :, :], w_kv.rearrange("m (c p) n -> p m c n", p=P)).then_inc(weights_b.sem, 16)

            def load_seq(b, p):
                cols = bass.ds(b * LEN, LEN)
                sp.dma_start(hT[p][:, :, 0:CTX], ctxT[bass.ds(b, 1)].rearrange("o c p n -> (o p) c n")).then_inc(seq_in[p].sem, 16)
                sp.dma_start(hT[p][:, :, CTX:KEYS], x_mid[:, :, cols].rearrange("c p n -> p c n")).then_inc(seq_in[p].sem, 16)
                sp.dma_start(qT[p], q_mid[:, :, cols].rearrange("c p n -> p c n")).then_inc(seq_in[p].sem, 16)
                sp.dma_start(mask_i[p][0:LEN, :], mask[bass.ds(b, 1), :].broadcast_to([LEN, CTX])).then_inc(seq_in[p].sem, 16)

            load_seq(0, 0)
            load_seq(1, 1)
            sp.dma_start(region1[:, 2, :, :], rows(w_out)).then_inc(weights_c.sem, 16)
            sp.dma_start(w_1, rows(w_mlp1)).then_inc(weights_c.sem, 16)
            sp.dma_start(w_2, w_mlp2.rearrange("(f p) n -> p f n", p=P)).then_inc(weights_c.sem, 16)

            def pair_io(i, last):
                for p in range(2):
                    if not last:
                        sp.wait_ge(s_full.sem, s_full.at(i, (p + 1) * AH))
                        load_seq(i * 2 + p + 2, p)
                    sp.wait_ge(oT_ready.sem, oT_ready.at(i, p + 1))
                    sp.dma_start(o_mid[:, :, bass.ds((i * 2 + p) * LEN, LEN)].rearrange("c p n -> p c n"), o_T).then_inc(o_stored.sem, 16)

            with sp.Fori(0, PAIRS - 1) as i:
                pair_io(i, False)
            pair_io(PAIRS - 1, True)
            sp.wait_ge(o_stored.sem, 16 * SEQS)

            with sp.Fori(0, GROUPS) as g:
                sp.wait_ge(c_out.sem, 16 * g)
                sp.dma_start(attn, group_cols(o_mid, g)).then_inc(c_in.sem, 16)
                sp.dma_start(res, group_cols(x_mid, g)).then_inc(c_in.sem, 16)
                sp.wait_ge(out_ready.sem, out_ready.at(g))
                sp.dma_start(group_cols(out, g), out_sb).then_inc(c_out.sem, 16)
            sp.wait_ge(c_out.sem, 16 * GROUPS)

        @block.tensor
        def _(pe):
            mm = nc.tensor.matmul
            pe.wait_ge(loaded.sem, ALL_LOADED)
            pe.wait_ge(consts_set.sem, consts_set.per)

            def sum_channels(g, key, src):
                ps = ra.claim(pe, g, key)
                for kt in range(CT):
                    last = mm(ps[:, 0:GT], mean_ones[:, :], src[:, kt, :], start=kt == 0, stop=kt == CT - 1)
                ra.filled(last, key)

            def project(g, key, w, ct, src):
                ps = ra.claim(pe, g, key)
                for kt in range(CT):
                    last = mm(ps[:, 0:GT], w[:, kt, ct * P:(ct + 1) * P], src[:, kt, :], start=kt == 0, stop=kt == CT - 1)
                ra.filled(last, key)

            with pe.Fori(0, GROUPS) as g:
                pe.wait_ge(group_in.sem, 48 * g + 48)
                sum_channels(g, "mean1", xa)
                pe.wait_ge(square_ready.sem, square_ready.at(g, 1))
                sum_channels(g, "var1", square)
                pe.wait_ge(mixx_ready.sem, mixx_ready.at(g))
                for key, lo, hi in (("rank4", 0, P), ("rank1", P, MIX * MIXR)):
                    ps = ra.claim(pe, g, key)
                    for kt in range(CT):
                        last = mm(ps[0:hi - lo, 0:GT], mix1[:, kt, lo:hi], scratch[:, kt, :], start=kt == 0, stop=kt == CT - 1)
                    ra.filled(last, key)
                pe.wait_ge(mix_rank.sem, mix_rank.at(g))
                for j in range(MIX):
                    lo = MIXR * (j % 4)
                    w, t = (mix2a, mix_t4) if j < 4 else (mix2b, mix_t1)
                    for ct in range(CT):
                        ps = ra.claim(pe, g, ("mix", j, ct))
                        ra.filled(mm(ps[:, 0:GT], w[lo:lo + MIXR, ct * P:(ct + 1) * P], t[lo:lo + MIXR, :], start=True, stop=True),
                                  ("mix", j, ct))
                pe.wait_ge(mixed_ready.sem, mixed_ready.at(g, 1))
                ps = ra.claim(pe, g, "dec1")
                for kt in range(CT):
                    last = mm(ps[0:DECR, 0:GT], dec1[:, kt, :], mixed[0][:, kt, :], start=kt == 0, stop=kt == CT - 1)
                ra.filled(last, "dec1")
                pe.wait_ge(dec_rank.sem, dec_rank.at(g))
                for ct in range(CT):
                    ps = ra.claim(pe, g, ("dec2", ct))
                    ra.filled(mm(ps[:, 0:GT], dec2[:, ct * P:(ct + 1) * P], dec_t[:, :], start=True, stop=True), ("dec2", ct))
                for n, w, j in (("k", wk, 1), ("v", wv, 2), ("r", wr, 3)):
                    pe.wait_ge(mixed_ready.sem, mixed_ready.at(g, j + 1))
                    for ct in range(CT):
                        project(g, (n, ct), w, ct, mixed[j])
                pe.wait_ge(mixed_ready.sem, mixed_ready.at(g))

                def broadcast_values(u):
                    ct, q = divmod(u, QUADS)
                    pe.wait_ge(v_ready.sem, v_ready.at(g, ct + 1))
                    pe.wait_ge(outer_ready.sem, outer_ready.at(g, u))
                    for i in range(4):
                        rows_i = slice(32 * i, 32 * i + 32)
                        last = mm(ps_v[:, i, :], pick[rows_i, q, :], v_sb[rows_i, ct, :], start=True, stop=True)
                    last.then_inc(vals_full.sem, 1)

                def sum_rows(u):
                    ct, q = divmod(u, QUADS)
                    pe.wait_ge(weighed.sem, weighed.at(g, u + 1))
                    if q == 0:
                        pe.wait_ge(y_copied.sem, y_copied.at(g, ct))
                    for i in range(4):
                        first = P - HPT - HPT * (4 * i + q)
                        last = mm(ps_y, window[:, first:first + P], ring[u % RING][:, i, :], start=q == 0 and i == 0, stop=q == 3 and i == 3)
                    last.then_inc(summed.sem, 1)

                for u in range(UNITS + 2):
                    if u < UNITS:
                        broadcast_values(u)
                    if u >= 2:
                        sum_rows(u - 2)
                    if 1 <= u <= CT:
                        project(g, ("g", u - 1), wg, u - 1, mixed[4])
                        pe.wait_ge(rku_ready.sem, rku_ready.at(g, u))
                        ps = ra.claim(pe, g, ("bonus", u - 1))
                        ra.filled(mm(ps[:, 0:GT], block_ones, rk[:, u - 1, :], start=True, stop=True), ("bonus", u - 1))

                pe.wait_ge(y_added.sem, y_added.at(g))
                for ct in range(CT):
                    ps = ra.claim(pe, g, ("ymean", ct))
                    ra.filled(mm(ps[:, 0:GT], block_ones, shift[:, ct, :], start=True, stop=True), ("ymean", ct))
                ps = ra.claim(pe, g, "yvar")
                for ct in range(CT):
                    pe.wait_ge(y_square.sem, y_square.at(g, ct + 1))
                    last = mm(ps[0:RH, 0:GT], heads_sum_sb[:, ct, :], square[:, ct, :], start=ct == 0, stop=ct == CT - 1)
                ra.filled(last, "yvar")
                pe.wait_ge(rstd_ready.sem, rstd_ready.at(g, 2))
                for ct in range(CT):
                    ps = ra.claim(pe, g, ("yback", ct))
                    ra.filled(mm(ps[:, 0:GT], heads_back_sb[:, ct, :], rstd[0:RH, :], start=True, stop=True), ("yback", ct))
                pe.wait_ge(y_gated.sem, y_gated.at(g))
                for ct in range(CT):
                    project(g, ("o", ct), wo, ct, shift)
                pe.wait_ge(x2_ready.sem, x2_ready.at(g))
                sum_channels(g, "mean2", xa)
                pe.wait_ge(square_ready.sem, square_ready.at(g, 2))
                sum_channels(g, "var2", square)
                pe.wait_ge(ffr_ready.sem, ffr_ready.at(g))
                for ct in range(CT):
                    project(g, ("fr", ct), fwr, ct, rk)
                pe.wait_ge(ffk_ready.sem, ffk_ready.at(g))
                for ct in range(CT):
                    project(g, ("fk", ct), fwk, ct, scratch)
                pe.wait_ge(kk_ready.sem, kk_ready.at(g))
                for ct in range(CT):
                    project(g, ("fv", ct), fwv, ct, k_sb)
                pe.wait_ge(x3_ready.sem, x3_ready.at(g))
                for ct in range(CT):
                    project(g, ("q", ct), wq, ct, xa)

            pe.wait_ge(weights_b.sem, 16)
            pe.wait_ge(pads_set.sem, pads_set.per)

            def make_kv(i, p, n):
                if n < 2:
                    pe.wait_ge(v_done.sem, v_done.at(i, p * KT_N))
                elif n < 2 + CT:
                    pe.wait_ge(k_done.sem, k_done.at(i, p * CT + n - 1))
                else:
                    pe.wait_ge(v_done.sem, v_done.at(i, p * KT_N + n - 1 - CT))
                ps = bank[6 + n % 2]
                for kt in range(CT):
                    if n < CT:
                        last = mm(ps[:, 0:KPAD], w_k[:, kt, n * P:(n + 1) * P], hT[p][:, kt, :], start=kt == 0, stop=kt == CT - 1)
                    else:
                        m = (n - CT) * KT_W
                        last = mm(ps[0:KT_W, :], hT[p][:, kt, m:m + KT_W], w_v[:, kt, :], start=kt == 0, stop=kt == CT - 1)
                last.then_inc(kv_full.sem, 1)

            def make_next_kv(i, p, n):
                if n == 0:
                    pe.wait_ge(seq_in[1 - p].sem, 64 * (i + p) + 64)
                make_kv(i + p, 1 - p, n)

            pe.wait_ge(seq_in[0].sem, 64)
            for n in range(8):
                make_kv(0, 0, n)

            def attend(i, p, last_seq):
                base = p * AH
                pe.wait_ge(k_done.sem, k_done.at(i, (p + 1) * CT))
                for h in range(AH + 3):
                    if h < AH:
                        t = base + h
                        ct, r = h // 4, AD * (h % 4)
                        pe.wait_ge(s_masked.sem, s_masked.at(i, max(t - 2, 0)))
                        mm(bank[t % 3][0:LEN, 0:KEYS], qT[p][r:r + AD, ct, :], kT[p][r:r + AD, ct, 0:KEYS],
                           start=True, stop=True).then_inc(s_full.sem, 1)
                    if 2 <= h < AH + 2:
                        t = base + h - 2
                        pe.wait_ge(p_ready.sem, p_ready.at(i, t + 1))
                        pe.wait_ge(pT_ready.sem, pT_ready.at(i, max(t - 1, 0)))
                        if h == 2:
                            pe.wait_ge(oT_ready.sem, oT_ready.at(i, p))
                        for k in range(KT_N):
                            last = nc.tensor.transpose(bank[3 + t % 2][0:KT_W, k * LEN:(k + 1) * LEN],
                                                       probs[t % 4][0:LEN, k * KT_W:(k + 1) * KT_W], ident[0:LEN, 0:LEN])
                        last.then_inc(pT_full.sem, 1)
                    if h >= 3:
                        t, c = base + h - 3, (h - 3) * AD
                        pe.wait_ge(pT_ready.sem, pT_ready.at(i, t + 1))
                        if h == 3:
                            pe.wait_ge(v_done.sem, v_done.at(i, (p + 1) * KT_N))
                            pe.wait_ge(o_ready.sem, o_ready.at(i, p))
                        for k in range(KT_N):
                            last = mm(bank[5][0:LEN, c:c + AD], probsT[t % 2][0:KT_W, k, :], v_tok[p][0:KT_W, k, c:c + AD],
                                      start=k == 0, stop=k == KT_N - 1)
                        last.then_inc(pv_done.sem, 1)
                    if h % 2 == 1 and h // 2 < 7 and not last_seq:
                        make_next_kv(i, p, h // 2)
                if not last_seq:
                    make_next_kv(i, p, 7)
                pe.wait_ge(o_ready.sem, o_ready.at(i, p + 1))
                pe.wait_ge(pT_ready.sem, pT_ready.at(i, base + AH))
                for ct in range(CT):
                    last = nc.tensor.transpose(bank[3][:, ct * LEN:(ct + 1) * LEN], o_tok[0:LEN, ct * P:(ct + 1) * P], ident[0:LEN, 0:LEN])
                last.then_inc(oT_full.sem, 1)

            with pe.Fori(0, PAIRS - 1) as i:
                attend(i, 0, False)
                attend(i, 1, False)
            attend(PAIRS - 1, 0, False)
            attend(PAIRS - 1, 1, True)

            pe.wait_ge(weights_c.sem, 48)
            pe.wait_ge(oT_ready.sem, SEQS)
            with pe.Fori(0, GROUPS) as g:
                pe.wait_ge(c_in.sem, 32 * g + 32)
                for ct in range(CT):
                    ps = rc.claim(pe, g, ("o", ct))
                    for kt in range(CT):
                        last = mm(ps[:, 0:GT], w_o[:, kt, ct * P:(ct + 1) * P], attn[:, kt, :], start=kt == 0, stop=kt == CT - 1)
                    rc.filled(last, ("o", ct))
                pe.wait_ge(sq_ready.sem, sq_ready.at(g))
                ps = rc.claim(pe, g, "ms")
                for kt in range(CT):
                    last = mm(ps[:, 0:GT], mean_ones[:, :], sq_c[:, kt, :], start=kt == 0, stop=kt == CT - 1)
                rc.filled(last, "ms")
                pe.wait_ge(h_ready.sem, h_ready.at(g))
                for m in range(FT):
                    ps = rc.claim(pe, g, ("h", m))
                    for kt in range(CT):
                        last = mm(ps[:, 0:GT], w_1[:, kt, m * P:(m + 1) * P], mid[:, kt, :], start=kt == 0, stop=kt == CT - 1)
                    rc.filled(last, ("h", m))
                for ct in range(CT):
                    ps = rc.claim(pe, g, ("y", ct))
                    for f in range(FT):
                        if ct == 0:
                            pe.wait_ge(hid_ready.sem, hid_ready.at(g, f + 1))
                        last = mm(ps[:, 0:GT], w_2[:, f, ct * P:(ct + 1) * P], hidden[:, f, :], start=f == 0, stop=f == FT - 1)
                    rc.filled(last, ("y", ct))

        @block.scalar
        def _(act):
            af = nc.scalar.activation
            for dst, src in loads:
                act.dma_start(dst, src).then_inc(loaded.sem, 16)
            act.wait_ge(loaded.sem, ALL_LOADED)
            act.wait_ge(consts_set.sem, consts_set.per)

            def affine(g, k, w, b):
                act.wait_ge(normed.sem, normed.at(g, k))
                for ct in range(CT):
                    af(ext[:, ct, :, 1:LEN + 1], by_seq(centred[:, ct, :]), ACT.Identity,
                       bias=vcol(b, ct), scale=vcol(w, ct)).then_inc(ext_ready.sem, 1)

            with act.Fori(0, GROUPS) as g:
                act.wait_ge(group_in.sem, 48 * g + 48)
                af(ext[:, :, :, 0], edge_sb[:, 1, :, :], ACT.Copy).then_inc(edge_ready.sem, 1)
                act.wait_ge(centred_ready.sem, centred_ready.at(g, 1))
                af(square, centred, ACT.Square).then_inc(square_ready.sem, 1)
                ps = ra.take(act, g, "var1")
                af(std[:, :], ps[:, 0:GT], ACT.Sqrt, bias=eps[:, 0:1]).then_inc(std_ready.sem, 1)
                affine(g, 1, "ln1_w", "ln1_b")
                ps = ra.take(act, g, "rank4")
                af(mix_t4[:, :], ps[:, 0:GT], ACT.Tanh).then_inc(mix_rank.sem, 1)
                ps = ra.take(act, g, "rank1")
                af(mix_t1[:, :], ps[0:MIXR, 0:GT], ACT.Tanh).then_inc(mix_rank.sem, 1)
                ps = ra.take(act, g, "dec1")
                af(dec_t[:, :], ps[0:DECR, 0:GT], ACT.Tanh).then_inc(dec_rank.sem, 1)
                for ct in range(CT):
                    ps = ra.take(act, g, ("dec2", ct))
                    af(scratch[:, ct, :], ps[:, 0:GT], ACT.Exp, bias=vcol("time_decay", ct)).then_inc(dec_exp.sem, 1)
                for ct in range(CT):
                    act.wait_ge(dec_exp.sem, dec_exp.at(g, ct + 1))
                    af(by_seq(w_sb[:, ct, :])[:, :, 1:LEN], by_seq(scratch[:, ct, :])[:, :, 0:LEN - 1],
                       ACT.Exp, scale=-1.0).then_inc(w_ready.sem, 1)
                for n, dst, done in (("k", k_sb, k_ready), ("v", v_sb, v_ready), ("r", r_sb, r_ready)):
                    for ct in range(CT):
                        ps = ra.take(act, g, (n, ct))
                        af(dst[:, ct, :], ps[:, 0:GT], ACT.Copy).then_inc(done.sem, 1)
                act.wait_ge(mixx_ready.sem, mixx_ready.at(g))
                act.wait_ge(mixed_ready.sem, mixed_ready.at(g))
                af(ext[:, :, :, 0], edge_sb[:, 0, :, :], ACT.Copy).then_inc(edge_ready.sem, 1)
                act.wait_ge(r_ready.sem, r_ready.at(g))
                for u in range(UNITS + 2):
                    if u < UNITS:
                        ct, q = divmod(u, QUADS)
                        act.wait_ge(summed.sem, summed.at(g, max(u - RING + 1, 0)))
                        states = ring[u % RING].rearrange("p j (b l) -> p j b l", b=GB)
                        af(states[:, :, :, 0], s0_sb[:, ct, q, :, :], ACT.Copy).then_inc(start_state.sem, 1)
                    if 1 <= u <= CT:
                        ps = ra.take(act, g, ("g", u - 1))
                        af(g_sb[:, u - 1, :], ps[:, 0:GT], ACT.Silu).then_inc(g_ready.sem, 1)
                    if u >= QUADS + 1 and (u - QUADS - 1) % QUADS == 0:
                        ct = (u - QUADS - 1) // QUADS
                        act.wait_ge(summed.sem, summed.at(g, (ct + 1) * QUADS))
                        af(shift[:, ct, :], ps_y, ACT.Copy).then_inc(y_copied.sem, 1)
                for ct in range(CT):
                    act.wait_ge(y_centred.sem, y_centred.at(g, ct + 1))
                    af(square[:, ct, :], shift[:, ct, :], ACT.Square).then_inc(y_square.sem, 1)
                ps = ra.take(act, g, "yvar")
                af(std[0:RH, :], ps[0:RH, 0:GT], ACT.Sqrt, bias=eps[0:RH, 0:1], scale=1.0 / RS).then_inc(std_ready.sem, 1)
                act.wait_ge(centred_ready.sem, centred_ready.at(g, 2))
                af(square, centred, ACT.Square).then_inc(square_ready.sem, 1)
                ps = ra.take(act, g, "var2")
                af(std[:, :], ps[:, 0:GT], ACT.Sqrt, bias=eps[:, 0:1]).then_inc(std_ready.sem, 1)
                affine(g, 2, "ln2_w", "ln2_b")
                for ct in range(CT):
                    ps = ra.take(act, g, ("fr", ct))
                    af(g_sb[:, ct, :], ps[:, 0:GT], ACT.Sigmoid).then_inc(rr_ready.sem, 1)
                for ct in range(CT):
                    ps = ra.take(act, g, ("fk", ct))
                    af(k_sb[:, ct, :], ps[:, 0:GT], ACT.Relu).then_inc(relu_ready.sem, 1)
                for ct in range(CT):
                    ps = ra.take(act, g, ("q", ct))
                    af(mixed[4][:, ct, :], ps[:, 0:GT], ACT.Identity, bias=vcol("q_b", ct)).then_inc(q_ready.sem, 1)

            def copy_kv(i, p, n):
                act.wait_ge(kv_full.sem, kv_full.at(i, p * 8 + n + 1))
                ps = bank[6 + n % 2]
                if n < CT:
                    af(kT[p][:, n, :], ps[:, 0:KPAD], ACT.Identity, bias=vcol("k_b", n)).then_inc(k_done.sem, 1)
                else:
                    af(v_tok[p][0:KT_W, n - CT, :], ps[0:KT_W, :], ACT.Copy).then_inc(v_done.sem, 1)

            def attend(i, p, last_seq):
                base = p * AH
                act.wait_ge(inv_ready.sem, inv_ready.at(i, p))
                act.wait_ge(s_full.sem, s_full.at(i, base))
                act.wait_ge(pv_done.sem, pv_done.at(i, base))
                for h in range(AH):
                    t = base + h
                    act.wait_ge(s_masked.sem, s_masked.at(i, t + 1))
                    af(probs[t % 4][0:LEN, 0:KEYS], probs[t % 4][0:LEN, 0:KEYS], ACT.Exp, bias=row_max[0:LEN, h:h + 1], scale=-1.0,
                       accum_out=row_sum[0:LEN, h:h + 1]).then_inc(p_ready.sem, 1)
                    if h % 2 == 1 and h // 2 < 7 and not last_seq:
                        copy_kv(i + p, 1 - p, h // 2)
                if not last_seq:
                    copy_kv(i + p, 1 - p, 7)
                act.wait_ge(oT_full.sem, oT_full.at(i, p + 1))
                act.wait_ge(o_stored.sem, 32 * i + 16 * p)
                for ct in range(CT):
                    last = af(o_T[:, ct, :], bank[3][:, ct * LEN:(ct + 1) * LEN], ACT.Identity, bias=vcol("v_b", ct))
                last.then_inc(oT_ready.sem, 1)

            for n in range(8):
                copy_kv(0, 0, n)
            with act.Fori(0, PAIRS - 1) as i:
                attend(i, 0, False)
                attend(i, 1, False)
            attend(PAIRS - 1, 0, False)
            attend(PAIRS - 1, 1, True)

            with act.Fori(0, GROUPS) as g:
                act.wait_ge(resid_ready.sem, resid_ready.at(g))
                af(sq_c, mid, ACT.Square).then_inc(sq_ready.sem, 1)
                ps = rc.take(act, g, "ms")
                af(std[:, :], ps[:, 0:GT], ACT.Sqrt, bias=eps[:, 1:2]).then_inc(cstd_ready.sem, 1)
                for m in range(FT):
                    ps = rc.take(act, g, ("h", m))
                    af(hidden[:, m, :], ps[:, 0:GT], ACT.Gelu_apprx_tanh, bias=bias1(m)).then_inc(hid_ready.sem, 1)

        @block.gpsimd
        def _(pool):
            tt = nc.gpsimd.tensor_tensor
            with pool.Fori(0, GROUPS) as g:
                for j in range(MIX):
                    pool.wait_ge(mix_scaled.sem, mix_scaled.at(g, (j + 1) * CT))
                    m = mixed[j].rearrange("p c (b l) -> p c b l", b=GB)
                    tt(m, m, ext[:, :, :, 1:LEN + 1], ALU.add).then_inc(mixed_ready.sem, 1)
                pool.wait_ge(r_ready.sem, r_ready.at(g))
                for u in range(UNITS):
                    pool.wait_ge(scanned.sem, scanned.at(g, u + 1))
                    states = ring[u % RING]
                    tt(states, states, spread(r_sb[:, u // QUADS, :], 1, 4), ALU.mult).then_inc(weighed.sem, 1)
                for ct in range(CT):
                    pool.wait_ge(relu_ready.sem, relu_ready.at(g, ct + 1))
                    tt(k_sb[:, ct, :], k_sb[:, ct, :], k_sb[:, ct, :], ALU.mult).then_inc(kk_ready.sem, 1)

        @block.vector
        def _(dve):
            v = nc.vector
            v.memset(mean_ones[:, :], 1.0 / C).then_inc(consts_set.sem, 1)
            v.memset(eps[:, 0:1], LN_EPS).then_inc(consts_set.sem, 1)
            v.memset(eps[:, 1:2], RMS_EPS).then_inc(consts_set.sem, 1)
            v.memset(w_sb, 0.0).then_inc(consts_set.sem, 1)
            v.memset(ext, 0.0).then_inc(consts_set.sem, 1)
            dve.wait_ge(loaded.sem, ALL_LOADED)

            def normalise(g, k, mean, kr):
                ps = ra.take(dve, g, mean)
                v.tensor_tensor(centred, xa, spread(ps[:, 0:GT], 1, CT), ALU.subtract).then_inc(centred_ready.sem, 1)
                dve.wait_ge(std_ready.sem, std_ready.at(g, kr))
                v.reciprocal(rstd[:, :], std[:, :]).then_inc(rstd_ready.sem, 1)
                dve.wait_ge(rstd_ready.sem, rstd_ready.at(g, kr))
                v.tensor_tensor(centred, centred, spread(rstd[:, :], 1, CT), ALU.mult).then_inc(normed.sem, 1)

            def token_shift(g, k):
                dve.wait_ge(ext_ready.sem, ext_ready.at(g, k * CT))
                dve.wait_ge(edge_ready.sem, edge_ready.at(g, k))
                v.tensor_tensor(shift.rearrange("p c (b l) -> p c b l", b=GB), ext[:, :, :, 0:LEN], ext[:, :, :, 1:LEN + 1],
                                ALU.subtract).then_inc(shift_ready.sem, 1)
                dve.wait_ge(shift_ready.sem, shift_ready.at(g, k))

            def mix_in(dst, w, done):
                for ct in range(CT):
                    v.scalar_tensor_tensor(by_seq(dst[:, ct, :]), by_seq(shift[:, ct, :]), vcol(w, ct), ext[:, ct, :, 1:LEN + 1],
                                           ALU.mult, ALU.add).then_inc(done.sem, 1)

            with dve.Fori(0, GROUPS) as g:
                dve.wait_ge(group_in.sem, 48 * g + 48)
                normalise(g, 1, "mean1", 1)
                token_shift(g, 1)
                mix_in(scratch, "maa_x", mixx_ready)
                for j, name in enumerate(("maa_w", "maa_k", "maa_v", "maa_r", "maa_g")):
                    for ct in range(CT):
                        ps = ra.take(dve, g, ("mix", j, ct))
                        v.scalar_tensor_tensor(mixed[j][:, ct, :], ps[:, 0:GT], vcol(name, ct), shift[:, ct, :],
                                               ALU.add, ALU.mult).then_inc(mix_scaled.sem, 1)
                for ct in range(CT):
                    dve.wait_ge(r_ready.sem, r_ready.at(g, ct + 1))
                    v.scalar_tensor_tensor(rk[:, ct, :], r_sb[:, ct, :], vcol("faaaa", ct), k_sb[:, ct, :],
                                           ALU.mult, ALU.mult).then_inc(rku_ready.sem, 1)
                for u in range(UNITS):
                    ct = u // QUADS
                    states = ring[u % RING].rearrange("p j (b l) -> p j b l", b=GB)
                    dve.wait_ge(vals_full.sem, vals_full.at(g, u + 1))
                    dve.wait_ge(summed.sem, summed.at(g, max(u - RING + 1, 0)))
                    v.tensor_tensor(states[:, :, :, 1:LEN], spread(by_seq(k_sb[:, ct, :])[:, :, 0:LEN - 1], 1, 4),
                                    ps_v.rearrange("p j (b l) -> p j b l", b=GB)[:, :, :, 0:LEN - 1], ALU.mult).then_inc(outer_ready.sem, 1)
                    dve.wait_ge(outer_ready.sem, outer_ready.at(g, u + 1))
                    dve.wait_ge(start_state.sem, start_state.at(g, u + 1))
                    dve.wait_ge(w_ready.sem, w_ready.at(g, ct + 1))
                    for i in range(4):
                        row = ring[u % RING][:, i, :]
                        last = v.tensor_tensor_scan(row, w_sb[:, ct, :], row, 0.0, ALU.mult, ALU.add)
                    last.then_inc(scanned.sem, 1)
                    if 2 <= u < 2 + CT:
                        c = u - 2
                        ps = ra.take(dve, g, ("bonus", c))
                        v.tensor_tensor(rk[:, c, :], ps[:, 0:GT], v_sb[:, c, :], ALU.mult).then_inc(bonus_ready.sem, 1)
                dve.wait_ge(y_copied.sem, y_copied.at(g))
                dve.wait_ge(bonus_ready.sem, bonus_ready.at(g))
                v.tensor_tensor(shift, shift, rk, ALU.add).then_inc(y_added.sem, 1)
                dve.wait_ge(y_added.sem, y_added.at(g))
                for ct in range(CT):
                    ps = ra.take(dve, g, ("ymean", ct))
                    v.scalar_tensor_tensor(shift[:, ct, :], ps[:, 0:GT], -1.0 / RS, shift[:, ct, :], ALU.mult, ALU.add).then_inc(y_centred.sem, 1)
                dve.wait_ge(std_ready.sem, std_ready.at(g, 2))
                v.reciprocal(rstd[0:RH, :], std[0:RH, :]).then_inc(rstd_ready.sem, 1)
                for ct in range(CT):
                    ps = ra.take(dve, g, ("yback", ct))
                    v.tensor_tensor(shift[:, ct, :], ps[:, 0:GT], shift[:, ct, :], ALU.mult).then_inc(y_scaled.sem, 1)
                for ct in range(CT):
                    dve.wait_ge(y_scaled.sem, y_scaled.at(g, ct + 1))
                    v.tensor_scalar(shift[:, ct, :], shift[:, ct, :], vcol("gn_w", ct), vcol("gn_b", ct), ALU.mult, ALU.add).then_inc(y_affine.sem, 1)
                dve.wait_ge(y_affine.sem, y_affine.at(g))
                dve.wait_ge(g_ready.sem, g_ready.at(g))
                v.tensor_tensor(shift, shift, g_sb, ALU.mult).then_inc(y_gated.sem, 1)
                for ct in range(CT):
                    ps = ra.take(dve, g, ("o", ct))
                    v.tensor_tensor(xa[:, ct, :], ps[:, 0:GT], xa[:, ct, :], ALU.add).then_inc(x2_ready.sem, 1)
                dve.wait_ge(x2_ready.sem, x2_ready.at(g))
                normalise(g, 2, "mean2", 3)
                token_shift(g, 2)
                mix_in(rk, "fmaa_r", ffr_ready)
                mix_in(scratch, "fmaa_k", ffk_ready)
                for ct in range(CT):
                    ps = ra.take(dve, g, ("fv", ct))
                    dve.wait_ge(rr_ready.sem, rr_ready.at(g, ct + 1))
                    v.tensor_tensor(r_sb[:, ct, :], ps[:, 0:GT], g_sb[:, ct, :], ALU.mult).then_inc(ff_ready.sem, 1)
                dve.wait_ge(ff_ready.sem, ff_ready.at(g))
                v.tensor_tensor(xa, xa, r_sb, ALU.add).then_inc(x3_ready.sem, 1)

            dve.wait_ge(group_out.sem, 32 * GROUPS)
            for p in range(2):
                v.memset(hT[p][:, :, KEYS:KPAD], 0.0).then_inc(pads_set.sem, 1)
                v.memset(mask_f[p][:, CTX:KEYS], 0.0).then_inc(pads_set.sem, 1)
            for t in range(4):
                v.memset(probs[t][:, KEYS:KPAD], 0.0).then_inc(pads_set.sem, 1)
            dve.wait_ge(pads_set.sem, pads_set.per)

            def attend(i, p):
                base = p * AH
                dve.wait_ge(seq_in[p].sem, 64 * i + 64)
                dve.wait_ge(s_masked.sem, s_masked.at(i, base))
                v.tensor_scalar(mask_f[p][0:LEN, 0:CTX], mask_i[p][0:LEN, :], 0.0, MASKED, ALU.is_equal, ALU.mult).then_inc(mask_ready.sem, 1)
                dve.wait_ge(mask_ready.sem, mask_ready.at(i, p + 1))
                dve.wait_ge(p_ready.sem, p_ready.at(i, base))
                dve.wait_ge(s_full.sem, s_full.at(i, base + 2))
                dve.wait_ge(pT_full.sem, pT_full.at(i, base))
                v.tensor_copy(tick[:, :], eps[0:1, 0:1])
                for h in range(AH + 2):
                    if h >= 2:
                        t = base + h - 2
                        if h < AH:
                            dve.wait_ge(s_full.sem, s_full.at(i, base + h + 1))
                        dve.wait_ge(pT_full.sem, pT_full.at(i, t + 1))
                        dve.wait_ge(pv_done.sem, pv_done.at(i, max(t - 1, 0)))
                        v.tensor_copy(probsT[t % 2][0:KT_W, :, :], bank[3 + t % 2][0:KT_W, 0:KT_N * LEN].rearrange("p (k n) -> p k n", k=KT_N)).then_inc(pT_ready.sem, 1)
                    if h < AH:
                        t = base + h
                        v.tensor_tensor_reduce(out=probs[t % 4][0:LEN, 0:KEYS], in0=bank[t % 3][0:LEN, 0:KEYS], in1=mask_f[p][0:LEN, :],
                                               scale=-1.0 / AD, scalar=3.0e38, op0=ALU.add, op1=ALU.min,
                                               accum_out=row_max[0:LEN, h:h + 1]).then_inc(s_masked.sem, 1)
                dve.wait_ge(p_ready.sem, p_ready.at(i, base + AH))
                v.reciprocal(row_inv[0:LEN, :], row_sum[0:LEN, :]).then_inc(inv_ready.sem, 1)
                dve.wait_ge(inv_ready.sem, inv_ready.at(i, p + 1))
                dve.wait_ge(pv_done.sem, pv_done.at(i, base + AH))
                dve.wait_ge(oT_full.sem, oT_full.at(i, p))
                v.tensor_tensor(o_tok[0:LEN, :].rearrange("p (h d) -> p h d", h=AH), bank[5][0:LEN, :].rearrange("p (h d) -> p h d", h=AH),
                                spread(row_inv[0:LEN, :], 2, AD), ALU.mult).then_inc(o_ready.sem, 1)

            with dve.Fori(0, PAIRS) as i:
                attend(i, 0)
                attend(i, 1)

            with dve.Fori(0, GROUPS) as g:
                dve.wait_ge(c_in.sem, 32 * g + 32)
                for ct in range(CT):
                    ps = rc.take(dve, g, ("o", ct))
                    v.scalar_tensor_tensor(mid[:, ct, :], ps[:, 0:GT], vcol("out_b", ct), res[:, ct, :], ALU.add, ALU.add).then_inc(resid_ready.sem, 1)
                dve.wait_ge(cstd_ready.sem, cstd_ready.at(g))
                v.reciprocal(rstd[:, :], std[:, :]).then_inc(crstd_ready.sem, 1)
                dve.wait_ge(crstd_ready.sem, crstd_ready.at(g))
                for ct in range(CT):
                    v.scalar_tensor_tensor(mid[:, ct, :], mid[:, ct, :], vcol("postnorm_w", ct), rstd[:, :], ALU.mult, ALU.mult).then_inc(h_ready.sem, 1)
                for ct in range(CT):
                    ps = rc.take(dve, g, ("y", ct))
                    v.scalar_tensor_tensor(out_sb[:, ct, :], ps[:, 0:GT], vcol("mlp_b2", ct), res[:, ct, :], ALU.add, ALU.add).then_inc(out_ready.sem, 1)


def head_constants():
    row = np.arange(P)
    head, chan = row % HPT, row // HPT
    same = (head[:, None] == head[None, :]).astype(np.float32)
    pick = (same[:, None, :] * (chan[:, None, None] % 4 == np.arange(4)[None, :, None])).astype(np.float32)
    window = np.zeros((P, 2 * P - HPT), np.float32)
    window[row, P - HPT + head] = 1
    heads = np.concatenate([np.eye(P, dtype=np.float32), same, pick.reshape(P, -1), window], 1)
    heads_sum = np.zeros((P, CT, RH), np.float32)
    for ct in range(CT):
        heads_sum[row, ct, ct * HPT + head] = 1
    heads_back = np.ascontiguousarray(heads_sum.transpose(2, 1, 0))
    return heads, heads_sum, heads_back


def kernel(**inputs):
    import concourse.bacc as bacc
    from concourse.bass_utils import run_bass_kernel_spmd

    a = {k: np.asarray(v) for k, v in inputs.items()}
    l0 = {k[len("L0_xattn_"):]: v for k, v in a.items() if k.startswith("L0_")}
    l1 = {k[len("L1_xattn_"):]: v for k, v in a.items() if k.startswith("L1_")}

    def channels(x):
        return x.transpose(2, 0, 1).reshape(CT, P, -1)

    def tiles(x):
        return x.reshape(-1, P).T

    ctx = a["ctx_2048"]
    kv_w = l1["kv_w"].reshape(C, C, 2)
    kv_b = l1["kv_b"].reshape(C, 2)

    def by_row(x, axis):
        x = np.moveaxis(x, axis, 0)
        x = x.reshape(CT, HPT, RS, -1).transpose(0, 2, 1, 3).reshape(x.shape)
        return np.moveaxis(x, 0, axis)

    named = {**l0, **l1, "k_b": kv_b[:, 0], "v_b": kv_b[:, 1], "faaaa": l0["faaaa"].reshape(C)}
    for n in ("time_decay", "faaaa", "gn_w", "gn_b"):
        named[n] = by_row(named[n], 0)
    heads, heads_sum, heads_back = head_constants()
    s0 = ctx[:, 2:2 + RS].reshape(GROUPS, GB, CT, HPT, RS, 4, 4).transpose(0, 4, 3, 2, 6, 5, 1).reshape(GROUPS, P, CT, QUADS, 4, GB)
    edge = ctx[:, 0:2].reshape(GROUPS, GB, 2, CT, P).transpose(0, 4, 2, 3, 1)
    arrays = {
        "xT": channels(a["x"]), "ctxT": ctx.transpose(0, 2, 1).reshape(SEQS, CT, P, CTX), "mask": a["mask_BxS2_ik0"],
        "edgeT": edge, "s0T": s0,
        "vecs": np.concatenate([tiles(named[n]) for n in VECS] + [tiles(l1["mlp_b1"])], 1),
        "w_mix1": l0["maa_w1"], "w_mix2": l0["maa_w2"].reshape(MIX * MIXR, C),
        "w_dec1": l0["decay_w1"], "w_dec2": by_row(l0["decay_w2"], 1),
        "w_rkvg": np.stack([by_row(l0[n].T, 1) for n in ("Wr", "Wk", "Wv", "Wg")]),
        "w_off": np.stack([by_row(l0["Wo"].T, 0)] + [l0[n].T for n in ("fWr", "fWk", "fWv")]),
        "w_q": l1["q_w"], "w_kv": kv_w.transpose(2, 0, 1), "w_out": l1["out_w"],
        "w_mlp1": l1["mlp_w1"], "w_mlp2": l1["mlp_w2"],
        "heads": heads, "heads_sum": heads_sum, "heads_back": heads_back,
    }
    arrays = {k: np.ascontiguousarray(v) for k, v in arrays.items()}
    nc = bacc.Bacc("TRN2", target_bir_lowering=False, num_devices=1)
    args = {k: nc.dram_tensor(k, v.shape, mybir.dt.from_np(v.dtype), kind="ExternalInput").ap() for k, v in arrays.items()}
    out = nc.dram_tensor("out", [CT, P, TOK], F32, kind="ExternalOutput").ap()
    rwkv_perceiver(nc, **args, out=out)
    r = run_bass_kernel_spmd(nc, [arrays], core_ids=[0])
    got = r.results[0]["out"]
    return np.ascontiguousarray(got.reshape(C, SEQS, LEN).transpose(1, 2, 0))
```

```python
from contextlib import ExitStack

import numpy as np

import concourse.bass as bass
from concourse import mybir

F32 = mybir.dt.float32
F32R = mybir.dt.float32r
I32 = mybir.dt.int32
ALU = mybir.AluOpType
ACT = mybir.ActivationFunctionType

P = 128
SEQS, LEN, C = 16, 100, 512
CTX = 361
CT = C // P
GROUPS = 4
GB = SEQS // GROUPS
GT = GB * LEN
TOK = SEQS * LEN
RH, RS = 32, 16
HPT = P // RS
MIX, MIXR = 5, 32
DECR = 64
AH, AD = 16, 32
KEYS = CTX + LEN
KT_N = 4
KT_W = 116
KPAD = KT_N * KT_W
FF = 4 * C
FT = FF // P
QUADS = RS // 4
UNITS = CT * QUADS
RING = 4
SUM_LAG = 3
REC_DRAIN = 4
MIX_ORDER = [1, 2, 3, 4, 0]
LN_EPS, RMS_EPS = 1e-5, 1e-6
MASKED = -3.0e38
MEM_AT = 16512
MEM_WORDS = 53200
PAIR = 2 * AH
T_LAG, HI_LAG, LO_LAG, PV_LAG = 2, 3, 3, 4
DRAIN = 7
W_CHUNKS = 4

VECS = ["ln1_w", "ln1_b", "ln2_w", "ln2_b", "maa_x", "maa_w", "maa_k", "maa_v", "maa_r", "maa_g",
        "time_decay", "faaaa", "gn_w", "gn_b", "fmaa_k", "fmaa_r", "q_b", "k_b", "v_b", "out_b",
        "postnorm_w", "mlp_b2"]
NVEC = len(VECS) * CT + FT


def spread(ap, axis, n):
    a = ap.unsqueeze(axis)
    return a.broadcast_to(list(a.shape[:axis]) + [n] + list(a.shape[axis + 1:]))


class Signal:

    def __init__(self, nc, ctx, name, per=1):
        self.sem, self.per = ctx.enter_context(nc.semaphore(name)), per

    def at(self, turn, k=None):
        k = self.per if k is None else k
        return turn * self.per + k


class Memory:

    def __init__(self, nc):
        self.nc, self.word = nc, 0

    def at(self, word):
        self.word = word

    def lay(self, name, shape, dt=F32):
        words = int(np.prod(shape[1:]))
        t = self.nc.alloc_sbuf_tensor_at(name, shape, dt, offset=MEM_AT + 4 * self.word)
        self.word += (words + 7) // 8 * 8
        assert self.word <= MEM_WORDS, (name, self.word)
        return t[tuple(slice(None) for _ in shape)]

    def split(self, name, shape):
        hi = self.lay(name + "_hi", shape, F32R)
        here = self.word
        lo = self.lay(name + "_lo", shape, F32R)
        self.at(here)
        return hi, lo, self.lay(name + "_raw", shape)


class Results:

    def __init__(self, nc, ctx, name, banks, readers):
        self.banks, self.readers = banks, list(readers.values())
        self.order = {key: i for i, key in enumerate(readers)}
        n = len(banks)
        self.full = [Signal(nc, ctx, f"{name}{b}_full", len(self.readers[b::n])) for b in range(n)]

    def bank(self, key):
        return self.banks[self.order[key] % len(self.banks)]

    def claim(self, eng, turn, key):
        i, n = self.order[key], len(self.banks)
        if i >= n:
            signal, k = self.readers[i - n]
            eng.wait_ge(signal.sem, signal.at(turn, k))
        else:
            signal, _ = self.readers[i::n][-1]
            eng.wait_ge(signal.sem, signal.at(turn, 0))
        return self.banks[i % n]

    def filled(self, ins, key):
        ins.then_inc(self.full[self.order[key] % len(self.banks)].sem, 1)

    def take(self, eng, turn, key):
        i, n = self.order[key], len(self.banks)
        full = self.full[i % n]
        eng.wait_ge(full.sem, full.at(turn, i // n + 1))
        return self.banks[i % n]


def rwkv_perceiver(nc, xT, ctxT, mask, edgeT, s0T, vecs, w_mix1, w_mix2, w_dec1, w_dec2, w_rkvg,
                   w_off, w_q, w_kv, w_out, w_mlp1, w_mlp2, heads, heads_sum, heads_back, out):
    with ExitStack() as ctx:
        mem = Memory(nc)
        sb = mem.lay

        vec = sb("vec", [P, NVEC])
        heads_sb = sb("heads_sb", [P, 6 * P + 2 * P - HPT])
        ident = heads_sb[:, 0:P]
        block_ones = heads_sb[:, P:2 * P]
        pick = heads_sb[:, 2 * P:6 * P].rearrange("p (i n) -> p i n", i=4)
        window = heads_sb[:, 6 * P:]
        heads_sum_sb = sb("heads_sum_sb", [P, CT, RH])
        heads_back_sb = sb("heads_back_sb", [RH, CT, P])
        mean_ones = sb("mean_ones", [P, P])
        eps = sb("eps", [P, 2])
        one = sb("one", [P, 1])
        std = sb("std", [P, GT])
        rstd = sb("rstd", [P, GT])
        tick = sb("tick", [1, PAIR])
        phase_at = mem.word


        def tile_ct(name, words=GT, dt=F32):
            return sb(name, [P, CT, words], dt)

        mix1 = sb("mix1", [P, CT, MIX * MIXR])
        mix2a = sb("mix2a", [P, C])
        mix2b = sb("mix2b", [MIXR, C])
        dec1 = sb("dec1", [P, CT, DECR])
        dec2 = sb("dec2", [DECR, C])
        w_rkvg_s = [mem.split(f"w_{n}", [P, CT, C]) for n in "rkvg"]
        xa = tile_ct("xa")
        scratch = tile_ct("scratch")
        shift = tile_ct("shift")
        ext = sb("ext", [P, CT, GB, LEN + 1])
        edge_sb = sb("edge_sb", [P, CT, GB])
        mixed_s = [mem.split(f"mixed{j}", [P, CT, GT]) for j in range(1, MIX)]
        mixed_w = tile_ct("mixed_w")
        rec_out = sb("rec_out", [P, MIX, CT, GT])
        k_sb, v_sb, r_sb, w_sb, g_sb = (rec_out[:, n] for n in range(MIX))
        mix_t4 = sb("mix_t4", [P, GT])
        mix_t1 = sb("mix_t1", [MIXR, GT])
        dec_t = sb("dec_t", [DECR, GT])

        mem.at(phase_at)
        x3_raw = tile_ct("x3_raw")
        y_s = mem.split("y", [P, CT, GT])
        squares = tile_ct("squares")
        gate = tile_ct("gate")
        x_in3 = tile_ct("x_in3")
        x2 = tile_ct("x2")
        ext3 = sb("ext3", [P, CT, GB, LEN + 1])
        edge3 = sb("edge3", [P, CT, GB])
        shift3 = tile_ct("shift3")
        xr_s, xk_s, kk_s = (mem.split(n, [P, CT, GT]) for n in ("xr", "xk", "kk"))
        rr = tile_ct("rr")
        q_out = tile_ct("q_out")
        w_off_s = [mem.split(f"w_{n}", [P, CT, C]) for n in ("o", "fr", "fk", "fv")] + [mem.split("w_q", [P, CT, C])]

        mem.at(phase_at)
        rec_in = [sb(f"rec_in{ct}", [P, 4, GT]) for ct in range(CT)]
        s0_in = [sb(f"s0_in{ct}", [P, QUADS, 4, GB]) for ct in range(CT)]
        v_hi2, v_lo2 = ([sb(f"{n}{p}", [P, GT], F32R) for p in range(2)] for n in ("v_hi2_", "v_lo2_"))
        ring = [sb(f"ring{n}", [P, 4, GT]) for n in range(RING)]
        rk2, bonus2, y_out = (sb(n, [P, 2, GT]) for n in ("rk2", "bonus2", "y_out"))
        pick_r = sb("pick_r", [P, 4, P], F32R)

        mem.at(phase_at)
        w_o = sb("w_o", [P, CT, C])
        b_at = mem.word
        w_k, w_v = (mem.split(n, [P, CT, C]) for n in ("w_k", "w_v"))
        h_raw = tile_ct("h_raw", KPAD)
        h_hi, h_lo, kT_hi, kT_lo = ([tile_ct(f"{n}{p}", KPAD, F32R) for p in range(2)] for n in ("h_hi", "h_lo", "kT_hi", "kT_lo"))
        v_all = [sb(f"v_all{p}", [P, KT_N, AH, 2, AD], F32R) for p in range(2)]
        q_raw = [tile_ct(f"q_raw{p}", LEN) for p in range(2)]
        q_hi, q_lo = ([tile_ct(f"{n}{p}", LEN, F32R) for p in range(2)] for n in ("q_hi", "q_lo"))
        mask_i = [sb(f"mask_i{p}", [P, CTX], I32) for p in range(2)]
        mask_f = [sb(f"mask_f{p}", [P, KPAD]) for p in range(2)]
        probs = [sb(f"probs{t}", [P, KPAD]) for t in range(4)]
        pT_hi, pT_lo = ([sb(f"{n}{t}", [P, KT_N, LEN], F32R) for t in range(4)] for n in ("pT_hi", "pT_lo"))
        row_max, row_inv = (sb(n, [P, AH]) for n in ("row_max", "row_inv"))
        row_sum = [sb(f"row_sum{p}", [P, AH]) for p in range(2)]
        o_tok = sb("o_tok", [P, C])
        o_T = tile_ct("o_T", LEN)

        mem.at(b_at)
        w_1 = [mem.split(f"w_1{c}", [P, CT, C]) for c in range(W_CHUNKS)]
        w_2 = [mem.split(f"w_2{c}", [P, FT // W_CHUNKS, C]) for c in range(W_CHUNKS)]
        attn = tile_ct("attn")
        square_c = attn
        res_in, res_out, mid = (tile_ct(n) for n in ("res_in", "res_out", "mid"))
        mid_hi, mid_lo = (tile_ct(n, GT, F32R) for n in ("mid_hi", "mid_lo"))
        hid = [sb(f"hid{t}", [P, GT]) for t in range(4)]
        hid_hi, hid_lo = ([sb(f"{n}{t}", [P, GT], F32R) for t in range(4)] for n in ("hid_hi", "hid_lo"))

        rec_mid = nc.dram_tensor("rec_mid", [4, CT, P, TOK], F32, kind="Internal").ap()
        g_mid = nc.dram_tensor("g_mid", [CT, P, TOK], F32, kind="Internal").ap()
        y_mid = nc.dram_tensor("y_mid", [CT, P, TOK], F32, kind="Internal").ap()
        x_mid = nc.dram_tensor("x_mid", [CT, P, TOK], F32, kind="Internal").ap()
        q_mid = nc.dram_tensor("q_mid", [CT, P, TOK], F32, kind="Internal").ap()
        o_mid = nc.dram_tensor("o_mid", [CT, P, TOK], F32, kind="Internal").ap()

        ps_all = ctx.enter_context(nc.psum_tensor("ps_all", [P, 8, 512], F32))
        bank = [ps_all[:, i, :] for i in range(8)]
        ps_v = ps_all[:, 0:4, 0:GT]

        def vcol(name, ct):
            i = VECS.index(name) * CT + ct
            return vec[:, i:i + 1]

        def bias1(m):
            return vec[:, len(VECS) * CT + m:len(VECS) * CT + m + 1]

        def by_seq(ap):
            return ap.rearrange("p (b l) -> p b l", b=GB)

        def group_cols(dram, g):
            return dram[:, :, bass.ds(g * GT, GT)].rearrange("c p n -> p c n")

        def sig(name, per=1):
            return Signal(nc, ctx, name, per)

        loaded = sig("loaded")
        weights_in = [sig(f"weights_in{n}") for n in range(2 * W_CHUNKS)]
        weights_due = {}
        for phase, number in (("rkvg", 4), ("off", 5), ("kv", 2), ("mlp", 2 * W_CHUNKS)):
            for n in range(number):
                weights_due[phase, n] = 16 + sum(16 for other, m in weights_due if m == n)

        def await_weights(eng, phase, n):
            eng.wait_ge(weights_in[n].sem, weights_due[phase, n])

        rkvg_hi, rkvg_lo = sig("rkvg_hi", 4), sig("rkvg_lo", 4)
        consts_set = sig("consts_set", 5)
        x_in = sig("x_in")
        mean_full, var_full = sig("mean_full"), sig("var_full")
        centred_ready = sig("centred_ready")
        square_ready = sig("square_ready")
        std_ready = sig("std_ready")
        rstd_ready = sig("rstd_ready")
        normed = sig("normed")
        ext_ready = sig("ext_ready", CT + 1)
        shift_ready = sig("shift_ready")
        mixx_ready = sig("mixx_ready", CT)
        mix_rank = sig("mix_rank", 2)
        mix_scaled = sig("mix_scaled", MIX * CT)
        mixed_ready = sig("mixed_ready", MIX)
        mixed_hi = sig("mixed_hi", MIX - 1)
        mixed_lo = sig("mixed_lo", MIX - 1)
        dec_rank = sig("dec_rank")
        dec_exp = sig("dec_exp", CT)
        k_ready, v_ready, r_ready, w_ready, g_ready = (sig(f"{n}_ready", CT) for n in "kvrwg")
        rec_stored = sig("rec_stored")

        readers = {"rank4": (mix_rank, 1), "rank1": (mix_rank, 2)}
        readers |= {("mix", j, ct): (mix_scaled, n * CT + ct + 1) for n, j in enumerate(MIX_ORDER) for ct in range(CT)}
        readers |= {("k", ct): (k_ready, ct + 1) for ct in range(CT)} | {("v", ct): (v_ready, ct + 1) for ct in range(CT)}
        readers |= {"dec1": (dec_rank, 1)} | {("r", ct): (r_ready, ct + 1) for ct in range(CT)}
        readers |= {("dec2", ct): (dec_exp, ct + 1) for ct in range(CT)} | {("g", ct): (g_ready, ct + 1) for ct in range(CT)}
        ra = Results(nc, ctx, "ra", bank[0:5], readers)

        pick_set = sig("pick_set")
        tile_in = [sig(f"tile_in{ct}") for ct in range(CT)]
        v_hi_set, v_lo_set = sig("v_hi_set", CT), sig("v_lo_set", CT)
        vals_full = sig("vals_full", UNITS)
        start_state = sig("start_state", UNITS)
        outer_ready = sig("outer_ready", UNITS)
        scanned = sig("scanned", UNITS)
        weighed = sig("weighed", UNITS)
        summed = sig("summed", UNITS)
        rk_ready = sig("rk_ready", CT)
        bonus_full = sig("bonus_full", CT)
        bonus_ready = sig("bonus_ready", CT)
        y_ready = sig("y_ready", CT)
        y_stored = [sig(f"y_stored{p}") for p in range(2)]

        off_hi, off_lo = sig("off_hi", 5), sig("off_lo", 5)
        yg_in = sig("yg_in")
        x3_in = sig("x3_in")
        y_centred = sig("y_centred", CT)
        y_square = sig("y_square", CT)
        y_std = sig("y_std")
        y_rstd = sig("y_rstd")
        y_scaled = sig("y_scaled", CT)
        y_gated = sig("y_gated", CT)
        y_hi_set, y_lo_set = sig("y_hi_set", CT), sig("y_lo_set", CT)
        x2_ready = sig("x2_ready", CT)
        centred3 = sig("centred3")
        square3 = sig("square3")
        std3 = sig("std3")
        rstd3 = sig("rstd3")
        normed3 = sig("normed3")
        ext3_ready = sig("ext3_ready", CT + 1)
        shift3_ready = sig("shift3_ready")
        xr_ready, xk_ready = sig("xr_ready", CT), sig("xk_ready", CT)
        xrk_hi, xrk_lo = sig("xrk_hi", 2), sig("xrk_lo", 2)
        rr_ready = sig("rr_ready", CT)
        relu_ready = sig("relu_ready", CT)
        kk_ready = sig("kk_ready", CT)
        kk_hi_set, kk_lo_set = sig("kk_hi_set", CT), sig("kk_lo_set", CT)
        ff_ready = sig("ff_ready", CT)
        x3_ready = sig("x3_ready", CT)
        x3_hi_set, x3_lo_set = sig("x3_hi_set"), sig("x3_lo_set")
        q_ready = sig("q_ready", CT)
        x3_stored, q_stored = sig("x3_stored"), sig("q_stored")

        readers = {("ymean", ct): (y_centred, ct + 1) for ct in range(CT)} | {"yvar": (y_std, 1)}
        readers |= {("yback", ct): (y_scaled, ct + 1) for ct in range(CT)}
        readers |= {("o", ct): (x2_ready, ct + 1) for ct in range(CT)}
        readers |= {"mean2": (centred3, 1), "var2": (std3, 1)}
        r1 = Results(nc, ctx, "r1_", bank[0:3], readers)
        readers = {(n, ct): (done, ct + 1) for n, done in (("fr", rr_ready), ("fk", relu_ready), ("fv", ff_ready), ("q", q_ready))
                   for ct in range(CT)}
        r2 = Results(nc, ctx, "r2_", bank[3:7], readers)

        kv_w_hi = sig("kv_w_hi", 2)
        kv_w_lo = sig("kv_w_lo", 2)
        o_w_in = sig("o_w_in")
        pads_set = sig("pads_set", 7)
        h_in = sig("h_in")
        q_in = [sig(f"q_in{p}") for p in range(2)]
        h_hi_set, h_lo_set, q_hi_set, q_lo_set = (sig(n, 2) for n in ("h_hi_set", "h_lo_set", "q_hi_set", "q_lo_set"))
        mask_ready = sig("mask_ready", 2)
        kv_full = sig("kv_full", 16)
        kv_hi_set = sig("kv_hi_set", 16)
        kv_done = sig("kv_done", 16)
        s_full = sig("s_full", 2 * AH)
        s_masked = sig("s_masked", 2 * AH)
        p_ready = sig("p_ready", 2 * AH)
        t_full = sig("t_full", 2 * AH)
        pT_hi_set = sig("pT_hi_set", 2 * AH)
        pT_ready = sig("pT_ready", 2 * AH)
        pv_done = sig("pv_done", 2 * AH)
        inv_ready = sig("inv_ready", 2)
        o_copied = sig("o_copied", 4)
        o_summed = sig("o_summed", 4)
        o_ready = sig("o_ready", 2)
        oT_full = sig("oT_full", 2)
        oT_ready = sig("oT_ready", 2)
        o_stored = sig("o_stored")

        mlp_w_hi = sig("mlp_w_hi", 2 * W_CHUNKS)
        mlp_w_lo = sig("mlp_w_lo", 2 * W_CHUNKS)
        attn_in = sig("attn_in")
        out_in = sig("out_in")
        resid_ready = sig("resid_ready", CT)
        sq_ready = sig("sq_ready")
        cstd_ready = sig("cstd_ready")
        crstd_ready = sig("crstd_ready")
        mid_ready = sig("mid_ready", CT)
        mid_hi_set = sig("mid_hi_set")
        mid_lo_set = sig("mid_lo_set")
        hid_full = sig("hid_full", FT)
        hid_ready = sig("hid_ready", FT)
        hid_hi_set = sig("hid_hi_set", FT)
        hid_lo_set = sig("hid_lo_set", FT)
        hid_used = sig("hid_used", FT)
        out_ready = sig("out_ready", CT)
        c_out = sig("c_out")
        front_c = {("o", ct): (resid_ready, ct + 1) for ct in range(CT)} | {"ms": (cstd_ready, 1)}
        rf = Results(nc, ctx, "rf", bank[6:8], front_c)

        def runs(x, first):
            return x < PAIR and (x >= 0 or not first)

        block = ctx.enter_context(nc.Block())

        def rows(w):
            return w.rearrange("(c p) n -> p c n", p=P)

        loads = [
            (vec, vecs), (mix1, rows(w_mix1)), (mix2a, w_mix2[0:P, :]), (mix2b, w_mix2[P:MIX * MIXR, :]),
            (dec1, rows(w_dec1)), (dec2, w_dec2), (heads_sb, heads), (heads_sum_sb, heads_sum), (heads_back_sb, heads_back),
        ]
        ALL_LOADED = 16 * len(loads)
        PAIRS = SEQS // 2

        @block.sync
        def _(sp):
            def load_x(g):
                sp.wait_ge(ext_ready.sem, ext_ready.at(g, 0))
                sp.dma_start(xa, group_cols(xT, g)).then_inc(x_in.sem, 16)
                sp.dma_start(edge_sb, edgeT[bass.ds(g, 1), :, 1].rearrange("o p c b -> (o p) c b")).then_inc(x_in.sem, 16)

            def store_rec(g):
                for n, ready in enumerate((k_ready, v_ready, r_ready, w_ready, g_ready)):
                    sp.wait_ge(ready.sem, ready.at(g))
                    dst = group_cols(rec_mid[n], g) if n < 4 else group_cols(g_mid, g)
                    sp.dma_start(dst, rec_out[:, n]).then_inc(rec_stored.sem, 16)

            load_x(0)
            for n in (1, 2, 0, 3):
                sp.dma_start(w_rkvg_s[n][2], rows(w_rkvg[n])).then_inc(weights_in[n].sem, 16)
            with sp.Fori(0, GROUPS - 1) as g:
                load_x(g + 1)
                store_rec(g)
            store_rec(GROUPS - 1)

            sp.wait_ge(rec_stored.sem, 80 * GROUPS)

            def load_tile(g, ct):
                sp.dma_start(rec_in[ct], rec_mid[:, ct, :, bass.ds(g * GT, GT)].rearrange("k p n -> p k n")).then_inc(tile_in[ct].sem, 16)
                sp.dma_start(s0_in[ct], s0T[bass.ds(g, 1), :, ct].rearrange("o p q i b -> (o p) q i b")).then_inc(tile_in[ct].sem, 16)

            def rec_io(g, last):
                for ct in range(CT):
                    sp.wait_ge(y_ready.sem, y_ready.at(g, ct + 1))
                    sp.dma_start(y_mid[ct, :, bass.ds(g * GT, GT)], y_out[:, ct % 2, :]).then_inc(y_stored[ct % 2].sem, 16)
                    if not last:
                        load_tile(g + 1, ct)

            for ct in range(CT):
                load_tile(0, ct)
            for n, src in enumerate([w_off[m] for m in range(4)] + [w_q]):
                sp.dma_start(w_off_s[n][2], rows(src)).then_inc(weights_in[n].sem, 16)
            with sp.Fori(0, GROUPS - 1) as g:
                rec_io(g, False)
            rec_io(GROUPS - 1, True)

            for p in range(2):
                sp.wait_ge(y_stored[p].sem, 16 * CT // 2 * GROUPS)

            def load_yg(g):
                sp.wait_ge(x2_ready.sem, x2_ready.at(g, 0))
                sp.dma_start(y_s[2], group_cols(y_mid, g)).then_inc(yg_in.sem, 16)
                sp.dma_start(gate, group_cols(g_mid, g)).then_inc(yg_in.sem, 16)

            def load_x3(g):
                sp.wait_ge(ext3_ready.sem, ext3_ready.at(g, 0))
                sp.dma_start(x_in3, group_cols(xT, g)).then_inc(x3_in.sem, 16)
                sp.dma_start(edge3, edgeT[bass.ds(g, 1), :, 0].rearrange("o p c b -> (o p) c b")).then_inc(x3_in.sem, 16)

            def store_xq(g):
                sp.wait_ge(x3_ready.sem, x3_ready.at(g))
                sp.dma_start(group_cols(x_mid, g), x3_raw).then_inc(x3_stored.sem, 16)
                sp.wait_ge(q_ready.sem, q_ready.at(g))
                sp.dma_start(group_cols(q_mid, g), q_out).then_inc(q_stored.sem, 16)

            load_yg(0)
            load_x3(0)
            with sp.Fori(0, GROUPS - 1) as g:
                load_yg(g + 1)
                load_x3(g + 1)
                store_xq(g)
            store_xq(GROUPS - 1)

            sp.wait_ge(x3_stored.sem, 16 * GROUPS)
            sp.wait_ge(q_stored.sem, 16 * GROUPS)
            sp.dma_start(w_k[2], rows(w_kv[0])).then_inc(weights_in[0].sem, 16)
            sp.dma_start(w_v[2], rows(w_kv[1])).then_inc(weights_in[1].sem, 16)

            def load_h(b):
                sp.dma_start(h_raw[:, :, 0:CTX], ctxT[bass.ds(b, 1)].rearrange("o c p n -> (o p) c n")).then_inc(h_in.sem, 16)
                sp.dma_start(h_raw[:, :, CTX:KEYS], x_mid[:, :, bass.ds(b * LEN, LEN)].rearrange("c p n -> p c n")).then_inc(h_in.sem, 16)

            def load_q(b, p):
                sp.dma_start(q_raw[p], q_mid[:, :, bass.ds(b * LEN, LEN)].rearrange("c p n -> p c n")).then_inc(q_in[p].sem, 16)
                sp.dma_start(mask_i[p][0:LEN, :], mask[bass.ds(b, 1), :].broadcast_to([LEN, CTX])).then_inc(q_in[p].sem, 16)

            load_h(0)
            load_q(0, 0)
            load_q(1, 1)
            sp.wait_ge(h_lo_set.sem, 1)
            load_h(1)
            sp.dma_start(w_o, rows(w_out)).then_inc(o_w_in.sem, 16)

            def store_o(b, turn, k):
                sp.wait_ge(oT_ready.sem, oT_ready.at(turn, k))
                sp.dma_start(o_mid[:, :, bass.ds(b * LEN, LEN)].rearrange("c p n -> p c n"), o_T).then_inc(o_stored.sem, 16)

            def pair_io(i, first, last):
                for p in range(2):
                    if not last:
                        sp.wait_ge(h_lo_set.sem, h_lo_set.at(i, p + 2))
                        load_h(i * 2 + p + 2)
                    if p == 1 or not first:
                        store_o(i * 2 + p - 1, i, p)
                    if not last:
                        sp.wait_ge(s_full.sem, s_full.at(i, (p + 1) * AH))
                        load_q(i * 2 + p + 2, p)

            pair_io(0, True, False)
            with sp.Fori(1, PAIRS - 1) as i:
                pair_io(i, False, False)
            pair_io(PAIRS - 1, False, True)
            store_o(SEQS - 1, PAIRS, 0)

            sp.wait_ge(o_stored.sem, 16 * SEQS)
            sp.dma_start(attn, group_cols(o_mid, 0)).then_inc(attn_in.sem, 16)
            sp.dma_start(res_in, group_cols(x_mid, 0)).then_inc(attn_in.sem, 16)
            for c in range(W_CHUNKS):
                sp.dma_start(w_1[c][2], rows(w_mlp1)[:, :, c * C:(c + 1) * C]).then_inc(weights_in[2 * c].sem, 16)
                sp.dma_start(w_2[c][2], rows(w_mlp2)[:, c * CT:(c + 1) * CT, :]).then_inc(weights_in[2 * c + 1].sem, 16)

            def group_io(g, last):
                sp.wait_ge(c_out.sem, 16 * g)
                sp.dma_start(res_out, group_cols(x_mid, g)).then_inc(out_in.sem, 16)
                if not last:
                    sp.wait_ge(cstd_ready.sem, cstd_ready.at(g))
                    sp.wait_ge(resid_ready.sem, resid_ready.at(g))
                    sp.dma_start(attn, group_cols(o_mid, g + 1)).then_inc(attn_in.sem, 16)
                    sp.dma_start(res_in, group_cols(x_mid, g + 1)).then_inc(attn_in.sem, 16)
                sp.wait_ge(out_ready.sem, out_ready.at(g))
                sp.dma_start(group_cols(out, g), res_out).then_inc(c_out.sem, 16)

            with sp.Fori(0, GROUPS - 1) as g:
                group_io(g, False)
            group_io(GROUPS - 1, True)
            sp.wait_ge(c_out.sem, 16 * GROUPS)

        @block.tensor
        def _(pe):
            mm = nc.tensor.matmul
            pe.wait_ge(loaded.sem, ALL_LOADED)
            pe.wait_ge(consts_set.sem, consts_set.per)

            def exact(ps, weights, moving, first, last):
                mm(ps, weights[0], moving[0], start=first, stop=False)
                mm(ps, weights[1], moving[0], start=False, stop=False)
                return mm(ps, weights[0], moving[1], start=False, stop=last)

            def project(res, g, key, w, ct, src):
                ps = res.claim(pe, g, key)
                cols = slice(ct * P, (ct + 1) * P)
                for kt in range(CT):
                    last = exact(ps[:, 0:GT], (w[0][:, kt, cols], w[1][:, kt, cols]), (src[0][:, kt, :], src[1][:, kt, :]), kt == 0, kt == CT - 1)
                res.filled(last, key)

            def mean_1(g):
                pe.wait_ge(x_in.sem, 32 * g + 32)
                for kt in range(CT):
                    last = mm(bank[7][:, 0:GT], mean_ones, xa[:, kt, :], start=kt == 0, stop=kt == CT - 1)
                last.then_inc(mean_full.sem, 1)

            def var_1(g):
                pe.wait_ge(square_ready.sem, square_ready.at(g))
                for kt in range(CT):
                    last = mm(bank[6][:, 0:GT], mean_ones, scratch[:, kt, :], start=kt == 0, stop=kt == CT - 1)
                last.then_inc(var_full.sem, 1)

            def projections(g, last_group):
                pe.wait_ge(mixx_ready.sem, mixx_ready.at(g))
                for key, lo, hi in (("rank4", 0, P), ("rank1", P, MIX * MIXR)):
                    ps = ra.claim(pe, g, key)
                    for kt in range(CT):
                        last = mm(ps[0:hi - lo, 0:GT], mix1[:, kt, lo:hi], scratch[:, kt, :], start=kt == 0, stop=kt == CT - 1)
                    ra.filled(last, key)
                pe.wait_ge(mix_rank.sem, mix_rank.at(g))
                for j in MIX_ORDER:
                    lo = MIXR * (j % 4)
                    w, t = (mix2a, mix_t4) if j < 4 else (mix2b, mix_t1)
                    for ct in range(CT):
                        ps = ra.claim(pe, g, ("mix", j, ct))
                        ra.filled(mm(ps[:, 0:GT], w[lo:lo + MIXR, ct * P:(ct + 1) * P], t[lo:lo + MIXR, :], start=True, stop=True),
                                  ("mix", j, ct))
                for n, (name, m) in enumerate((("k", 1), ("v", 2), ("r", 0), ("g", 3))):
                    pe.wait_ge(mixed_lo.sem, mixed_lo.at(g, n + 1))
                    if n == 2:
                        pe.wait_ge(mixed_ready.sem, mixed_ready.at(g))
                        ps = ra.claim(pe, g, "dec1")
                        for kt in range(CT):
                            last = mm(ps[0:DECR, 0:GT], dec1[:, kt, :], mixed_w[:, kt, :], start=kt == 0, stop=kt == CT - 1)
                        ra.filled(last, "dec1")
                        if not last_group:
                            var_1(g + 1)
                    if n == 3:
                        pe.wait_ge(dec_rank.sem, dec_rank.at(g))
                        for ct in range(CT):
                            ps = ra.claim(pe, g, ("dec2", ct))
                            ra.filled(mm(ps[:, 0:GT], dec2[:, ct * P:(ct + 1) * P], dec_t, start=True, stop=True), ("dec2", ct))
                    for ct in range(CT):
                        project(ra, g, (name, ct), w_rkvg_s[m], ct, mixed_s[n])
                    if n == 0 and not last_group:
                        mean_1(g + 1)

            mean_1(0)
            var_1(0)
            pe.wait_ge(rkvg_lo.sem, rkvg_lo.per)
            with pe.Fori(0, GROUPS - 1) as g:
                projections(g, False)
            projections(GROUPS - 1, True)

            pe.wait_ge(w_ready.sem, w_ready.at(GROUPS - 1))
            pe.wait_ge(g_ready.sem, g_ready.at(GROUPS - 1))
            pe.wait_ge(pick_set.sem, 1)

            def recurrence(g, u, first):
                if u < UNITS:
                    ct, q = divmod(u, QUADS)
                    if q == 0:
                        pe.wait_ge(v_lo_set.sem, v_lo_set.at(g, ct + 1))
                    if u > 0 or not first:
                        pe.wait_ge(outer_ready.sem, outer_ready.at(g, u))
                    for i in range(4):
                        rows_i = slice(32 * i, 32 * i + 32)
                        mm(ps_v[:, i, :], pick_r[rows_i, q, :], v_hi2[ct % 2][rows_i, :], start=True, stop=False)
                        last = mm(ps_v[:, i, :], pick_r[rows_i, q, :], v_lo2[ct % 2][rows_i, :], start=False, stop=True)
                    last.then_inc(vals_full.sem, 1)
                    if q == 1:
                        pe.wait_ge(rk_ready.sem, rk_ready.at(g, ct + 1))
                        if ct >= 2 or not first:
                            pe.wait_ge(bonus_ready.sem, bonus_ready.at(g, ct - 1))
                        mm(bank[6 + ct % 2][:, 0:GT], block_ones, rk2[:, ct % 2, :], start=True, stop=True).then_inc(bonus_full.sem, 1)
                x = u - SUM_LAG
                if x < UNITS and (x >= 0 or not first):
                    ct, q = divmod(x, QUADS)
                    pe.wait_ge(weighed.sem, weighed.at(g, x + 1))
                    if q == 0 and (ct >= 2 or not first):
                        pe.wait_ge(y_ready.sem, y_ready.at(g, ct - 1))
                    for i in range(4):
                        row = P - HPT - HPT * (4 * i + q)
                        last = mm(bank[4 + ct % 2][:, 0:GT], window[:, row:row + P], ring[x % RING][:, i, :], start=q == 0 and i == 0, stop=q == 3 and i == 3)
                    last.then_inc(summed.sem, 1)

            for u in range(UNITS):
                recurrence(0, u, True)
            with pe.Fori(1, GROUPS - 1) as g:
                for u in range(UNITS):
                    recurrence(g, u, False)
            for u in range(UNITS + REC_DRAIN):
                recurrence(GROUPS - 1, u, False)

            pe.wait_ge(y_ready.sem, CT * GROUPS)
            pe.wait_ge(off_lo.sem, off_lo.per)

            def y_mean(g):
                pe.wait_ge(yg_in.sem, 32 * g + 32)
                for ct in range(CT):
                    ps = r1.claim(pe, g, ("ymean", ct))
                    r1.filled(mm(ps[:, 0:GT], block_ones, y_s[2][:, ct, :], start=True, stop=True), ("ymean", ct))

            def y_var(g):
                ps = r1.claim(pe, g, "yvar")
                for ct in range(CT):
                    pe.wait_ge(y_square.sem, y_square.at(g, ct + 1))
                    last = mm(ps[0:RH, 0:GT], heads_sum_sb[:, ct, :], squares[:, ct, :], start=ct == 0, stop=ct == CT - 1)
                r1.filled(last, "yvar")

            def y_back(g):
                pe.wait_ge(y_rstd.sem, y_rstd.at(g))
                for ct in range(CT):
                    ps = r1.claim(pe, g, ("yback", ct))
                    r1.filled(mm(ps[:, 0:GT], heads_back_sb[:, ct, :], rstd[0:RH, :], start=True, stop=True), ("yback", ct))

            def y_project(g):
                pe.wait_ge(y_lo_set.sem, y_lo_set.at(g))
                for ct in range(CT):
                    project(r1, g, ("o", ct), w_off_s[0], ct, y_s)

            def mean_2(g):
                pe.wait_ge(x2_ready.sem, x2_ready.at(g))
                ps = r1.claim(pe, g, "mean2")
                for kt in range(CT):
                    last = mm(ps[:, 0:GT], mean_ones, x2[:, kt, :], start=kt == 0, stop=kt == CT - 1)
                r1.filled(last, "mean2")

            def var_2(g):
                pe.wait_ge(square3.sem, square3.at(g))
                ps = r1.claim(pe, g, "var2")
                for kt in range(CT):
                    last = mm(ps[:, 0:GT], mean_ones, squares[:, kt, :], start=kt == 0, stop=kt == CT - 1)
                r1.filled(last, "var2")

            def channel_mixing(g, n):
                if n is not None:
                    y_mean(n)
                if g is not None:
                    pe.wait_ge(xrk_lo.sem, xrk_lo.at(g, 1))
                    for ct in range(CT):
                        project(r2, g, ("fr", ct), w_off_s[1], ct, xr_s)
                if n is not None:
                    y_var(n)
                if g is not None:
                    pe.wait_ge(xrk_lo.sem, xrk_lo.at(g, 2))
                    for ct in range(CT):
                        project(r2, g, ("fk", ct), w_off_s[2], ct, xk_s)
                if n is not None:
                    y_back(n)
                if g is not None:
                    pe.wait_ge(kk_lo_set.sem, kk_lo_set.at(g))
                    for ct in range(CT):
                        project(r2, g, ("fv", ct), w_off_s[3], ct, kk_s)
                if n is not None:
                    y_project(n)
                    mean_2(n)
                if g is not None:
                    pe.wait_ge(x3_lo_set.sem, x3_lo_set.at(g))
                    for ct in (0, 1):
                        project(r2, g, ("q", ct), w_off_s[4], ct, kk_s)
                if n is not None:
                    var_2(n)
                if g is not None:
                    for ct in (2, 3):
                        project(r2, g, ("q", ct), w_off_s[4], ct, kk_s)

            channel_mixing(None, 0)
            with pe.Fori(0, GROUPS - 1) as g:
                channel_mixing(g, g + 1)
            channel_mixing(GROUPS - 1, None)

            pe.wait_ge(q_ready.sem, CT * GROUPS)
            pe.wait_ge(kv_w_lo.sem, kv_w_lo.per)
            pe.wait_ge(pads_set.sem, pads_set.per)

            def make_kv(i, p, n, kts):
                if kts[0] == 0:
                    pe.wait_ge(kv_done.sem, kv_done.at(i, max(p * 8 + n - 1, 0)))
                    if n == 0:
                        pe.wait_ge(h_lo_set.sem, h_lo_set.at(i, p + 1))
                ps = bank[6 + n % 2]
                for kt in kts:
                    h = (h_hi[p][:, kt, :], h_lo[p][:, kt, :])
                    if n < CT:
                        cols = slice(n * P, (n + 1) * P)
                        last = exact(ps[:, 0:KPAD], (w_k[0][:, kt, cols], w_k[1][:, kt, cols]), h, kt == 0, kt == CT - 1)
                    else:
                        cols = slice((n - CT) * KT_W, (n - CT + 1) * KT_W)
                        last = exact(ps[0:KT_W, :], (h[0][:, cols], h[1][:, cols]), (w_v[0][:, kt, :], w_v[1][:, kt, :]), kt == 0, kt == CT - 1)
                if kts[-1] == CT - 1:
                    last.then_inc(kv_full.sem, 1)

            for n in range(8):
                make_kv(0, 0, n, (0, 1, 2, 3))

            def attend(i, t, first, last):
                p, h = divmod(t, AH)
                if t < PAIR:
                    if h == 0:
                        pe.wait_ge(kv_done.sem, kv_done.at(i, p * 8 + CT))
                        pe.wait_ge(q_lo_set.sem, q_lo_set.at(i, p + 1))
                    ct, rows_h = h // 4, slice(AD * (h % 4), AD * (h % 4) + AD)
                    if t >= 2 or not first:
                        pe.wait_ge(s_masked.sem, s_masked.at(i, t - 1))
                    exact(bank[t % 2][0:LEN, 0:KPAD], (q_hi[p][rows_h, ct, :], q_lo[p][rows_h, ct, :]),
                          (kT_hi[p][rows_h, ct, :], kT_lo[p][rows_h, ct, :]), True, True).then_inc(s_full.sem, 1)
                    if p == 0 or not last:
                        make_kv(i + p, 1 - p, h // 2, (0, 1) if h % 2 == 0 else (2, 3))
                x = t - T_LAG
                if runs(x, first):
                    pe.wait_ge(p_ready.sem, p_ready.at(i, x + 1))
                    if x >= 2 or not first:
                        pe.wait_ge(pT_ready.sem, pT_ready.at(i, x - 1))
                    for k in range(KT_N):
                        done = nc.tensor.transpose(bank[2 + x % 2][0:KT_W, k * LEN:(k + 1) * LEN], probs[x % 4][0:LEN, k * KT_W:(k + 1) * KT_W], ident[0:LEN, 0:LEN])
                    done.then_inc(t_full.sem, 1)
                x = t - PV_LAG
                if runs(x, first):
                    b, h_x = divmod(x, AH)
                    pe.wait_ge(pT_ready.sem, pT_ready.at(i, x + 1))
                    if h_x == 0:
                        pe.wait_ge(kv_done.sem, kv_done.at(i, (b + 1) * 8))
                        if b > 0 or not first:
                            pe.wait_ge(o_summed.sem, o_summed.at(i, 2 * b - 1))
                    if h_x == AH // 2 and (b > 0 or not first):
                        pe.wait_ge(oT_ready.sem, oT_ready.at(i, b))
                    ps = bank[5 - h_x // (AH // 2)][0:LEN, h_x % (AH // 2) * 2 * AD:(h_x % (AH // 2) + 1) * 2 * AD]
                    for k in range(KT_N):
                        mm(ps, pT_hi[x % 4][0:KT_W, k, :], v_all[b % 2][0:KT_W, k, h_x].rearrange("p s d -> p (s d)"), start=k == 0, stop=False)
                        done = mm(ps[:, 0:AD], pT_lo[x % 4][0:KT_W, k, :], v_all[b % 2][0:KT_W, k, h_x, 0, :], start=False, stop=k == KT_N - 1)
                    done.then_inc(pv_done.sem, 1)
                if h == 5 and runs((p - 1) * AH, first):
                    pe.wait_ge(o_ready.sem, o_ready.at(i, p))
                    for ct in range(CT):
                        done = nc.tensor.transpose(bank[4][:, ct * LEN:(ct + 1) * LEN], o_tok[0:LEN, ct * P:(ct + 1) * P], ident[0:LEN, 0:LEN])
                    done.then_inc(oT_full.sem, 1)

            for t in range(PAIR):
                attend(0, t, True, False)
            with pe.Fori(1, PAIRS - 1) as i:
                for t in range(PAIR):
                    attend(i, t, False, False)
            for t in range(PAIR + DRAIN):
                attend(PAIRS - 1, t, False, True)

            pe.wait_ge(o_w_in.sem, 16)
            pe.wait_ge(oT_ready.sem, SEQS)

            def project_out(g):
                pe.wait_ge(attn_in.sem, 32 * g + 32)
                for ct in range(CT):
                    ps = rf.claim(pe, g, ("o", ct))
                    for kt in range(CT):
                        last = mm(ps[:, 0:GT], w_o[:, kt, ct * P:(ct + 1) * P], attn[:, kt, :], start=kt == 0, stop=kt == CT - 1)
                    rf.filled(last, ("o", ct))

            def mean_square(g):
                pe.wait_ge(sq_ready.sem, sq_ready.at(g))
                ps = rf.claim(pe, g, "ms")
                for kt in range(CT):
                    last = mm(ps[:, 0:GT], mean_ones, square_c[:, kt, :], start=kt == 0, stop=kt == CT - 1)
                rf.filled(last, "ms")

            def mlp(g, first, last_group):
                pe.wait_ge(mid_lo_set.sem, mid_lo_set.at(g))
                for f in range(FT + 2):
                    if f < FT:
                        c, cols = f // CT, slice(f % CT * P, (f % CT + 1) * P)
                        if first and f % CT == 0:
                            pe.wait_ge(mlp_w_lo.sem, 2 * c + 1)
                        pe.wait_ge(hid_ready.sem, hid_ready.at(g, max(f - 1, 0)))
                        for kt in range(CT):
                            last = exact(bank[4 + f % 2][:, 0:GT], (w_1[c][0][:, kt, cols], w_1[c][1][:, kt, cols]),
                                         (mid_hi[:, kt, :], mid_lo[:, kt, :]), kt == 0, kt == CT - 1)
                        last.then_inc(hid_full.sem, 1)
                    if f >= 2:
                        e = f - 2
                        if first and e % CT == 0:
                            pe.wait_ge(mlp_w_lo.sem, 2 * (e // CT) + 2)
                        pe.wait_ge(hid_lo_set.sem, hid_lo_set.at(g, e + 1))
                        for ct in range(CT):
                            if e == 0:
                                pe.wait_ge(out_ready.sem, out_ready.at(g, 0))
                            cols = slice(ct * P, (ct + 1) * P)
                            last = exact(bank[ct][:, 0:GT], (w_2[e // CT][0][:, e % CT, cols], w_2[e // CT][1][:, e % CT, cols]),
                                         (hid_hi[e % 4], hid_lo[e % 4]), e == 0, e == FT - 1)
                        last.then_inc(hid_used.sem, 1)
                    if not last_group and f == 3:
                        project_out(g + 1)
                    if not last_group and f == 7:
                        mean_square(g + 1)

            project_out(0)
            mean_square(0)
            mlp(0, True, False)
            with pe.Fori(1, GROUPS - 1) as g:
                mlp(g, False, False)
            mlp(GROUPS - 1, False, True)

        @block.scalar
        def _(act):
            af = nc.scalar.activation
            for dst, src in loads:
                act.dma_start(dst, src).then_inc(loaded.sem, 16)
            act.wait_ge(loaded.sem, ALL_LOADED)
            act.wait_ge(consts_set.sem, consts_set.per)

            def square_1(g):
                act.wait_ge(centred_ready.sem, centred_ready.at(g))
                af(scratch, xa, ACT.Square).then_inc(square_ready.sem, 1)

            def std_1(g):
                act.wait_ge(var_full.sem, var_full.at(g))
                af(std, bank[6][:, 0:GT], ACT.Sqrt, bias=eps[:, 0:1]).then_inc(std_ready.sem, 1)

            def affine_1(g):
                act.wait_ge(mixed_ready.sem, mixed_ready.at(g, 0))
                af(ext[:, :, :, 0], edge_sb, ACT.Copy).then_inc(ext_ready.sem, 1)
                act.wait_ge(normed.sem, normed.at(g))
                for ct in range(CT):
                    af(ext[:, ct, :, 1:LEN + 1], by_seq(xa[:, ct, :]), ACT.Identity,
                       bias=vcol("ln1_b", ct), scale=vcol("ln1_w", ct)).then_inc(ext_ready.sem, 1)

            def evict(g, name, dst, fn, ready):
                for ct in range(CT):
                    ps = ra.take(act, g, (name, ct))
                    af(dst[:, ct, :], ps[:, 0:GT], fn).then_inc(ready.sem, 1)

            def projections(g, last_group):
                ps = ra.take(act, g, "rank4")
                af(mix_t4, ps[:, 0:GT], ACT.Tanh).then_inc(mix_rank.sem, 1)
                ps = ra.take(act, g, "rank1")
                af(mix_t1, ps[0:MIXR, 0:GT], ACT.Tanh).then_inc(mix_rank.sem, 1)
                for n in range(MIX - 1):
                    act.wait_ge(mixed_ready.sem, mixed_ready.at(g, n + 1))
                    af(mixed_s[n][0], mixed_s[n][2], ACT.Copy).then_inc(mixed_hi.sem, 1)
                act.wait_ge(rec_stored.sem, 80 * g)
                evict(g, "k", k_sb, ACT.Copy, k_ready)
                if not last_group:
                    square_1(g + 1)
                evict(g, "v", v_sb, ACT.Copy, v_ready)
                ps = ra.take(act, g, "dec1")
                af(dec_t, ps[0:DECR, 0:GT], ACT.Tanh).then_inc(dec_rank.sem, 1)
                if not last_group:
                    std_1(g + 1)
                evict(g, "r", r_sb, ACT.Copy, r_ready)
                if not last_group:
                    affine_1(g + 1)
                for ct in range(CT):
                    ps = ra.take(act, g, ("dec2", ct))
                    af(mixed_w[:, ct, :], ps[:, 0:GT], ACT.Exp, bias=vcol("time_decay", ct)).then_inc(dec_exp.sem, 1)
                for ct in range(CT):
                    act.wait_ge(dec_exp.sem, dec_exp.at(g, ct + 1))
                    af(by_seq(w_sb[:, ct, :])[:, :, 1:LEN], by_seq(mixed_w[:, ct, :])[:, :, 0:LEN - 1],
                       ACT.Exp, scale=-1.0).then_inc(w_ready.sem, 1)
                evict(g, "g", g_sb, ACT.Silu, g_ready)

            square_1(0)
            std_1(0)
            affine_1(0)
            for n, m in enumerate((1, 2, 0, 3)):
                await_weights(act, "rkvg", m)
                af(w_rkvg_s[m][0], w_rkvg_s[m][2], ACT.Copy).then_inc(rkvg_hi.sem, 1)
            with act.Fori(0, GROUPS - 1) as g:
                projections(g, False)
            projections(GROUPS - 1, True)

            act.wait_ge(rec_stored.sem, 80 * GROUPS)
            af(pick_r, pick, ACT.Copy).then_inc(pick_set.sem, 1)

            def high_v(g, ct, used):
                act.wait_ge(tile_in[ct].sem, 32 * g + 32)
                act.wait_ge(vals_full.sem, used)
                af(v_hi2[ct % 2], rec_in[ct][:, 1, :], ACT.Copy).then_inc(v_hi_set.sem, 1)

            def recurrence(g, u, first, last):
                ct, q = divmod(u, QUADS)
                act.wait_ge(tile_in[ct].sem, 32 * g + 32)
                if u >= RING or not first:
                    act.wait_ge(summed.sem, summed.at(g, u - RING + 1))
                af(ring[u % RING].rearrange("p j (b l) -> p j b l", b=GB)[:, :, :, 0], s0_in[ct][:, q], ACT.Copy).then_inc(start_state.sem, 1)
                if q == 0 and ct < CT - 1:
                    high_v(g, ct + 1, vals_full.at(g, u))
                elif q == 0 and not last:
                    high_v(g + 1, 0, vals_full.at(g, u))

            high_v(0, 0, 0)
            for u in range(UNITS):
                recurrence(0, u, True, False)
            with act.Fori(1, GROUPS - 1) as g:
                for u in range(UNITS):
                    recurrence(g, u, False, False)
            for n in range(5):
                await_weights(act, "off", n)
                af(w_off_s[n][0], w_off_s[n][2], ACT.Copy).then_inc(off_hi.sem, 1)
            for u in range(UNITS):
                recurrence(GROUPS - 1, u, False, True)

            for p in range(2):
                act.wait_ge(y_stored[p].sem, 16 * CT // 2 * GROUPS)

            def channel_mixing(g, n):
                if n is not None:
                    for ct in range(CT):
                        act.wait_ge(y_centred.sem, y_centred.at(n, ct + 1))
                        af(squares[:, ct, :], y_s[2][:, ct, :], ACT.Square).then_inc(y_square.sem, 1)
                if g is not None:
                    for ct in range(CT):
                        ps = r2.take(act, g, ("fr", ct))
                        af(rr[:, ct, :], ps[:, 0:GT], ACT.Sigmoid).then_inc(rr_ready.sem, 1)
                if n is not None:
                    ps = r1.take(act, n, "yvar")
                    af(std[0:RH, :], ps[0:RH, 0:GT], ACT.Sqrt, bias=eps[0:RH, 0:1], scale=1.0 / RS).then_inc(y_std.sem, 1)
                if g is not None:
                    for ct in range(CT + 1):
                        if ct < CT:
                            ps = r2.take(act, g, ("fk", ct))
                            af(kk_s[2][:, ct, :], ps[:, 0:GT], ACT.Relu).then_inc(relu_ready.sem, 1)
                        if ct > 0:
                            act.wait_ge(kk_ready.sem, kk_ready.at(g, ct))
                            af(kk_s[0][:, ct - 1, :], kk_s[2][:, ct - 1, :], ACT.Copy).then_inc(kk_hi_set.sem, 1)
                if n is not None:
                    for ct in range(CT):
                        act.wait_ge(y_gated.sem, y_gated.at(n, ct + 1))
                        af(y_s[0][:, ct, :], y_s[2][:, ct, :], ACT.Copy).then_inc(y_hi_set.sem, 1)
                if g is not None:
                    act.wait_ge(x3_ready.sem, x3_ready.at(g))
                    af(kk_s[0], x3_raw, ACT.Copy).then_inc(x3_hi_set.sem, 1)
                if n is not None:
                    act.wait_ge(centred3.sem, centred3.at(n))
                    af(squares, x_in3, ACT.Square).then_inc(square3.sem, 1)
                if g is not None:
                    act.wait_ge(q_stored.sem, 16 * g)
                    for ct in (0, 1):
                        ps = r2.take(act, g, ("q", ct))
                        af(q_out[:, ct, :], ps[:, 0:GT], ACT.Identity, bias=vcol("q_b", ct)).then_inc(q_ready.sem, 1)
                if n is not None:
                    ps = r1.take(act, n, "var2")
                    af(std, ps[:, 0:GT], ACT.Sqrt, bias=eps[:, 0:1]).then_inc(std3.sem, 1)
                if g is not None:
                    for ct in (2, 3):
                        ps = r2.take(act, g, ("q", ct))
                        af(q_out[:, ct, :], ps[:, 0:GT], ACT.Identity, bias=vcol("q_b", ct)).then_inc(q_ready.sem, 1)
                if n is not None:
                    act.wait_ge(xk_ready.sem, xk_ready.at(n, 0))
                    af(ext3[:, :, :, 0], edge3, ACT.Copy).then_inc(ext3_ready.sem, 1)
                    act.wait_ge(normed3.sem, normed3.at(n))
                    for ct in range(CT):
                        af(ext3[:, ct, :, 1:LEN + 1], by_seq(x_in3[:, ct, :]), ACT.Identity,
                           bias=vcol("ln2_b", ct), scale=vcol("ln2_w", ct)).then_inc(ext3_ready.sem, 1)
                    for m, (x_s, ready) in enumerate(((xr_s, xr_ready), (xk_s, xk_ready))):
                        act.wait_ge(ready.sem, ready.at(n))
                        af(x_s[0], x_s[2], ACT.Copy).then_inc(xrk_hi.sem, 1)

            channel_mixing(None, 0)
            with act.Fori(0, GROUPS - 1) as g:
                channel_mixing(g, g + 1)
            channel_mixing(GROUPS - 1, None)

            for n, w in enumerate((w_k, w_v)):
                await_weights(act, "kv", n)
                af(w[0], w[2], ACT.Copy).then_inc(kv_w_hi.sem, 1)

            def split_h(i, p, used):
                act.wait_ge(h_in.sem, 64 * i + 32 * p + 32)
                act.wait_ge(kv_full.sem, used)
                af(h_hi[p], h_raw, ACT.Copy).then_inc(h_hi_set.sem, 1)

            def split_q(i, p, used):
                act.wait_ge(q_in[p].sem, 32 * i + 32)
                act.wait_ge(s_full.sem, used)
                af(q_hi[p], q_raw[p], ACT.Copy).then_inc(q_hi_set.sem, 1)

            def high_kv(i, p, n):
                act.wait_ge(kv_full.sem, kv_full.at(i, p * 8 + n + 1))
                ps = bank[6 + n % 2]
                if n < CT:
                    af(kT_hi[p][:, n, :], ps[:, 0:KPAD], ACT.Identity, bias=vcol("k_b", n)).then_inc(kv_hi_set.sem, 1)
                else:
                    af(v_all[p][0:KT_W, n - CT, :, 0, :], ps[0:KT_W, :].rearrange("p (h d) -> p h d", h=AH), ACT.Copy).then_inc(kv_hi_set.sem, 1)

            def attend(i, t, first, last):
                p, h = divmod(t, AH)
                x = t - HI_LAG
                if runs(x, first):
                    act.wait_ge(t_full.sem, t_full.at(i, x + 1))
                    if x >= 4 or not first:
                        act.wait_ge(pv_done.sem, pv_done.at(i, x - 3))
                    af(pT_hi[x % 4][0:KT_W, :, :], bank[2 + x % 2][0:KT_W, 0:KT_N * LEN].rearrange("p (k n) -> p k n", k=KT_N), ACT.Copy).then_inc(pT_hi_set.sem, 1)
                x = t - 1
                if runs(x, first):
                    b, h_x = divmod(x, AH)
                    act.wait_ge(s_masked.sem, s_masked.at(i, x + 1))
                    af(probs[x % 4][0:LEN, 0:KEYS], probs[x % 4][0:LEN, 0:KEYS], ACT.Exp, bias=row_max[0:LEN, h_x:h_x + 1], scale=-1.0,
                       accum_out=row_sum[b % 2][0:LEN, h_x:h_x + 1]).then_inc(p_ready.sem, 1)
                if h == 0 and t < PAIR and runs(t - AH, first):
                    high_kv(i, p, 7)
                elif h % 2 == 0 and h > 0 and t < PAIR and (p == 0 or not last):
                    high_kv(i + p, 1 - p, h // 2 - 1)
                if h == 9 and not last:
                    split_h(i + 1, p, kv_full.at(i, p * 8 + 8))
                if h == 7 and t < PAIR and (p == 0 or not last):
                    split_q(i + p, 1 - p, s_full.at(i, p * AH))
                if h == 6 and runs((p - 1) * AH, first):
                    act.wait_ge(oT_full.sem, oT_full.at(i, p))
                    if p > 1 or not first:
                        act.wait_ge(o_stored.sem, 32 * i + 16 * (p - 1))
                    for ct in range(CT):
                        done = af(o_T[:, ct, :], bank[4][:, ct * LEN:(ct + 1) * LEN], ACT.Identity, bias=vcol("v_b", ct))
                    done.then_inc(oT_ready.sem, 1)

            act.wait_ge(pads_set.sem, pads_set.per)
            split_h(0, 0, 0)
            split_q(0, 0, 0)
            for n in range(8):
                high_kv(0, 0, n)
            split_h(0, 1, 0)
            for t in range(PAIR):
                attend(0, t, True, False)
            with act.Fori(1, PAIRS - 1) as i:
                for t in range(PAIR):
                    attend(i, t, False, False)
            for t in range(PAIR + DRAIN):
                attend(PAIRS - 1, t, False, True)

            act.wait_ge(o_stored.sem, 16 * SEQS)

            def norm_c(g):
                act.wait_ge(resid_ready.sem, resid_ready.at(g))
                af(square_c, mid, ACT.Square).then_inc(sq_ready.sem, 1)

            def root_c(g):
                ps = rf.take(act, g, "ms")
                af(std, ps[:, 0:GT], ACT.Sqrt, bias=eps[:, 1:2]).then_inc(cstd_ready.sem, 1)

            def high_w(n):
                c = n // 2
                w = w_1[c] if n % 2 == 0 else w_2[c]
                await_weights(act, "mlp", n)
                af(w[0], w[2], ACT.Copy).then_inc(mlp_w_hi.sem, 1)

            def high_mid(g):
                act.wait_ge(mid_ready.sem, mid_ready.at(g))
                act.wait_ge(hid_full.sem, hid_full.at(g, 0))
                af(mid_hi, mid, ACT.Copy).then_inc(mid_hi_set.sem, 1)

            def mlp(g, first, last_group):
                for f in range(FT):
                    if first and f % CT == 0:
                        high_w(f // CT * 2)
                        high_w(f // CT * 2 + 1)
                    act.wait_ge(hid_full.sem, hid_full.at(g, f + 1))
                    act.wait_ge(hid_lo_set.sem, hid_lo_set.at(g, max(f - 3, 0)))
                    af(hid[f % 4], bank[4 + f % 2][:, 0:GT], ACT.Gelu_apprx_tanh, bias=bias1(f)).then_inc(hid_ready.sem, 1)
                    if not last_group and f == 4:
                        norm_c(g + 1)
                    if not last_group and f == 8:
                        root_c(g + 1)
                if not last_group:
                    high_mid(g + 1)

            norm_c(0)
            root_c(0)
            high_mid(0)
            mlp(0, True, False)
            with act.Fori(1, GROUPS - 1) as g:
                mlp(g, False, False)
            mlp(GROUPS - 1, False, True)

        @block.gpsimd
        def _(pool):
            tt = nc.gpsimd.tensor_tensor
            with pool.Fori(0, GROUPS) as g:
                for n in range(MIX):
                    pool.wait_ge(mix_scaled.sem, mix_scaled.at(g, (n + 1) * CT))
                    m = (mixed_s[n][2] if n < MIX - 1 else mixed_w).rearrange("p c (b l) -> p c b l", b=GB)
                    tt(m, m, ext[:, :, :, 1:LEN + 1], ALU.add).then_inc(mixed_ready.sem, 1)

            def low_v(g, ct):
                pool.wait_ge(v_hi_set.sem, v_hi_set.at(g, ct + 1))
                tt(v_lo2[ct % 2], rec_in[ct][:, 1, :], v_hi2[ct % 2].bitcast(F32), ALU.subtract).then_inc(v_lo_set.sem, 1)

            def recurrence(g, last):
                for u in range(UNITS):
                    ct, q = divmod(u, QUADS)
                    if q == 0 and ct < CT - 1:
                        low_v(g, ct + 1)
                    elif q == 0 and not last:
                        low_v(g + 1, 0)
                    pool.wait_ge(scanned.sem, scanned.at(g, u + 1))
                    tt(ring[u % RING], ring[u % RING], spread(rec_in[ct][:, 2, :], 1, 4), ALU.mult).then_inc(weighed.sem, 1)

            low_v(0, 0)
            with pool.Fori(0, GROUPS - 1) as g:
                recurrence(g, False)
            recurrence(GROUPS - 1, True)

            with pool.Fori(0, GROUPS) as g:
                for ct in range(CT):
                    pool.wait_ge(relu_ready.sem, relu_ready.at(g, ct + 1))
                    tt(kk_s[2][:, ct, :], kk_s[2][:, ct, :], kk_s[2][:, ct, :], ALU.mult).then_inc(kk_ready.sem, 1)

            def split_h(i, p):
                pool.wait_ge(h_hi_set.sem, h_hi_set.at(i, p + 1))
                tt(h_lo[p], h_raw, h_hi[p].bitcast(F32), ALU.subtract).then_inc(h_lo_set.sem, 1)

            def split_q(i, p):
                pool.wait_ge(q_hi_set.sem, q_hi_set.at(i, p + 1))
                tt(q_lo[p], q_raw[p], q_hi[p].bitcast(F32), ALU.subtract).then_inc(q_lo_set.sem, 1)

            def attend(i, p, last_seq, last_pair):
                if not last_pair:
                    split_h(i + 1, p)
                if not last_seq:
                    split_q(i + p, 1 - p)

            split_h(0, 0)
            split_q(0, 0)
            split_h(0, 1)
            with pool.Fori(0, PAIRS - 1) as i:
                attend(i, 0, False, False)
                attend(i, 1, False, False)
            attend(PAIRS - 1, 0, False, True)

            with pool.Fori(0, GROUPS) as g:
                for f in range(FT):
                    pool.wait_ge(hid_ready.sem, hid_ready.at(g, f + 1))
                    pool.wait_ge(hid_used.sem, hid_used.at(g, max(f - 3, 0)))
                    tt(hid_hi[f % 4], hid[f % 4], one.broadcast_to([P, GT]), ALU.mult).then_inc(hid_hi_set.sem, 1)

        @block.vector
        def _(dve):
            v = nc.vector
            v.memset(mean_ones[:, :], 1.0 / C).then_inc(consts_set.sem, 1)
            v.memset(eps[:, 0:1], LN_EPS).then_inc(consts_set.sem, 1)
            v.memset(eps[:, 1:2], RMS_EPS).then_inc(consts_set.sem, 1)
            v.memset(one, 1.0).then_inc(consts_set.sem, 1)
            v.memset(rec_out[:, 3], 0.0).then_inc(consts_set.sem, 1)
            dve.wait_ge(loaded.sem, ALL_LOADED)

            def token_shift(dst, src, done):
                v.tensor_tensor(dst.rearrange("p c (b l) -> p c b l", b=GB), src[:, :, :, 0:LEN], src[:, :, :, 1:LEN + 1], ALU.subtract).then_inc(done.sem, 1)

            def mix_in(dst, moved, src, w, done):
                for ct in range(CT):
                    v.scalar_tensor_tensor(by_seq(dst[:, ct, :]), by_seq(moved[:, ct, :]), vcol(w, ct), src[:, ct, :, 1:LEN + 1],
                                           ALU.mult, ALU.add).then_inc(done.sem, 1)

            def centre_1(g):
                dve.wait_ge(mean_full.sem, mean_full.at(g))
                v.tensor_tensor(xa, xa, spread(bank[7][:, 0:GT], 1, CT), ALU.subtract).then_inc(centred_ready.sem, 1)

            def norm_1(g):
                dve.wait_ge(std_ready.sem, std_ready.at(g))
                v.reciprocal(rstd, std).then_inc(rstd_ready.sem, 1)
                dve.wait_ge(rstd_ready.sem, rstd_ready.at(g))
                v.tensor_tensor(xa, xa, spread(rstd, 1, CT), ALU.mult).then_inc(normed.sem, 1)
                dve.wait_ge(ext_ready.sem, ext_ready.at(g))
                token_shift(shift, ext, shift_ready)
                dve.wait_ge(shift_ready.sem, shift_ready.at(g))
                mix_in(scratch, shift, ext, "maa_x", mixx_ready)

            def low_mixed(g, n):
                dve.wait_ge(mixed_hi.sem, mixed_hi.at(g, n + 1))
                v.tensor_tensor(mixed_s[n][1], mixed_s[n][2], mixed_s[n][0].bitcast(F32), ALU.subtract).then_inc(mixed_lo.sem, 1)

            def projections(g, last_group):
                for n, j in enumerate(MIX_ORDER):
                    dst = mixed_s[n][2] if n < MIX - 1 else mixed_w
                    if n == MIX - 1:
                        dve.wait_ge(w_ready.sem, w_ready.at(g, 0))
                    for ct in range(CT):
                        ps = ra.take(dve, g, ("mix", j, ct))
                        v.scalar_tensor_tensor(dst[:, ct, :], ps[:, 0:GT], vcol(VECS[5 + j], ct), shift[:, ct, :],
                                               ALU.add, ALU.mult).then_inc(mix_scaled.sem, 1)
                    if n >= 2:
                        low_mixed(g, n - 2)
                low_mixed(g, 3)
                if not last_group:
                    centre_1(g + 1)
                    norm_1(g + 1)

            centre_1(0)
            norm_1(0)
            for n, m in enumerate((1, 2, 0, 3)):
                w = w_rkvg_s[m]
                dve.wait_ge(rkvg_hi.sem, n + 1)
                v.tensor_tensor(w[1], w[2], w[0].bitcast(F32), ALU.subtract).then_inc(rkvg_lo.sem, 1)
            with dve.Fori(0, GROUPS - 1) as g:
                projections(g, False)
            projections(GROUPS - 1, True)

            dve.wait_ge(rec_stored.sem, 80 * GROUPS)

            def recurrence(g, u, first):
                ct, q = divmod(u, QUADS)
                if u < UNITS:
                    k, vals, r, w = (rec_in[ct][:, n, :] for n in range(4))
                    if q == 0:
                        dve.wait_ge(tile_in[ct].sem, 32 * g + 32)
                        if ct >= 2 or not first:
                            dve.wait_ge(bonus_full.sem, bonus_full.at(g, ct - 1))
                        v.scalar_tensor_tensor(rk2[:, ct % 2, :], r, vcol("faaaa", ct), k, ALU.mult, ALU.mult).then_inc(rk_ready.sem, 1)
                    states = ring[u % RING].rearrange("p j (b l) -> p j b l", b=GB)
                    dve.wait_ge(vals_full.sem, vals_full.at(g, u + 1))
                    if u >= RING or not first:
                        dve.wait_ge(summed.sem, summed.at(g, u - RING + 1))
                    v.tensor_tensor(states[:, :, :, 1:LEN], spread(by_seq(k)[:, :, 0:LEN - 1], 1, 4),
                                    ps_v.rearrange("p j (b l) -> p j b l", b=GB)[:, :, :, 0:LEN - 1], ALU.mult).then_inc(outer_ready.sem, 1)
                    dve.wait_ge(outer_ready.sem, outer_ready.at(g, u + 1))
                    dve.wait_ge(start_state.sem, start_state.at(g, u + 1))
                    for i in range(4):
                        row = ring[u % RING][:, i, :]
                        last = v.tensor_tensor_scan(row, w, row, 0.0, ALU.mult, ALU.add)
                    last.then_inc(scanned.sem, 1)
                    if q == 2:
                        dve.wait_ge(bonus_full.sem, bonus_full.at(g, ct + 1))
                        v.tensor_tensor(bonus2[:, ct % 2, :], bank[6 + ct % 2][:, 0:GT], vals, ALU.mult).then_inc(bonus_ready.sem, 1)
                c = ct - 1
                if q == 3 and (c >= 0 or not first):
                    dve.wait_ge(summed.sem, summed.at(g, ct * QUADS))
                    dve.wait_ge(bonus_ready.sem, bonus_ready.at(g, ct))
                    if c >= 2 or not first:
                        dve.wait_ge(y_stored[c % 2].sem, 32 * g + 16 * (c // 2))
                    v.tensor_tensor(y_out[:, c % 2, :], bank[4 + c % 2][:, 0:GT], bonus2[:, c % 2, :], ALU.add).then_inc(y_ready.sem, 1)

            for u in range(UNITS):
                recurrence(0, u, True)
            with dve.Fori(1, GROUPS - 1) as g:
                for u in range(UNITS):
                    recurrence(g, u, False)
            for n in range(5):
                w = w_off_s[n]
                dve.wait_ge(off_hi.sem, n + 1)
                v.tensor_tensor(w[1], w[2], w[0].bitcast(F32), ALU.subtract).then_inc(off_lo.sem, 1)
            for u in range(UNITS + REC_DRAIN):
                recurrence(GROUPS - 1, u, False)

            for p in range(2):
                dve.wait_ge(y_stored[p].sem, 16 * CT // 2 * GROUPS)

            def channel_mixing(g, n):
                if n is not None:
                    for ct in range(CT):
                        ps = r1.take(dve, n, ("ymean", ct))
                        v.scalar_tensor_tensor(y_s[2][:, ct, :], ps[:, 0:GT], -1.0 / RS, y_s[2][:, ct, :], ALU.mult, ALU.add).then_inc(y_centred.sem, 1)
                    dve.wait_ge(y_std.sem, y_std.at(n))
                    v.reciprocal(rstd[0:RH, :], std[0:RH, :]).then_inc(y_rstd.sem, 1)
                if g is not None:
                    for ct in range(CT):
                        dve.wait_ge(kk_hi_set.sem, kk_hi_set.at(g, ct + 1))
                        v.tensor_tensor(kk_s[1][:, ct, :], kk_s[2][:, ct, :], kk_s[0][:, ct, :].bitcast(F32), ALU.subtract).then_inc(kk_lo_set.sem, 1)
                if n is not None:
                    for ct in range(CT):
                        ps = r1.take(dve, n, ("yback", ct))
                        v.scalar_tensor_tensor(y_s[2][:, ct, :], ps[:, 0:GT], vcol("gn_w", ct), y_s[2][:, ct, :], ALU.mult, ALU.mult).then_inc(y_scaled.sem, 1)
                    for ct in range(CT):
                        dve.wait_ge(y_scaled.sem, y_scaled.at(n, ct + 1))
                        v.scalar_tensor_tensor(y_s[2][:, ct, :], y_s[2][:, ct, :], vcol("gn_b", ct), gate[:, ct, :], ALU.add, ALU.mult).then_inc(y_gated.sem, 1)
                    for ct in range(CT):
                        dve.wait_ge(y_hi_set.sem, y_hi_set.at(n, ct + 1))
                        v.tensor_tensor(y_s[1][:, ct, :], y_s[2][:, ct, :], y_s[0][:, ct, :].bitcast(F32), ALU.subtract).then_inc(y_lo_set.sem, 1)
                if g is not None:
                    for ct in range(CT):
                        ps = r2.take(dve, g, ("fv", ct))
                        dve.wait_ge(rr_ready.sem, rr_ready.at(g, ct + 1))
                        v.tensor_tensor(rr[:, ct, :], ps[:, 0:GT], rr[:, ct, :], ALU.mult).then_inc(ff_ready.sem, 1)
                    dve.wait_ge(x3_stored.sem, 16 * g)
                    for ct in range(CT):
                        dve.wait_ge(ff_ready.sem, ff_ready.at(g, ct + 1))
                        v.tensor_tensor(x3_raw[:, ct, :], x2[:, ct, :], rr[:, ct, :], ALU.add).then_inc(x3_ready.sem, 1)
                    dve.wait_ge(x3_hi_set.sem, x3_hi_set.at(g))
                    v.tensor_tensor(kk_s[1], x3_raw, kk_s[0].bitcast(F32), ALU.subtract).then_inc(x3_lo_set.sem, 1)
                if n is not None:
                    dve.wait_ge(x3_in.sem, 32 * n + 32)
                    for ct in range(CT):
                        ps = r1.take(dve, n, ("o", ct))
                        v.tensor_tensor(x2[:, ct, :], ps[:, 0:GT], x_in3[:, ct, :], ALU.add).then_inc(x2_ready.sem, 1)
                    dve.wait_ge(x2_ready.sem, x2_ready.at(n))
                    ps = r1.take(dve, n, "mean2")
                    v.tensor_tensor(x_in3, x2, spread(ps[:, 0:GT], 1, CT), ALU.subtract).then_inc(centred3.sem, 1)
                    dve.wait_ge(std3.sem, std3.at(n))
                    v.reciprocal(rstd, std).then_inc(rstd3.sem, 1)
                    dve.wait_ge(rstd3.sem, rstd3.at(n))
                    v.tensor_tensor(x_in3, x_in3, spread(rstd, 1, CT), ALU.mult).then_inc(normed3.sem, 1)
                    dve.wait_ge(ext3_ready.sem, ext3_ready.at(n))
                    token_shift(shift3, ext3, shift3_ready)
                    dve.wait_ge(shift3_ready.sem, shift3_ready.at(n))
                    mix_in(xr_s[2], shift3, ext3, "fmaa_r", xr_ready)
                    mix_in(xk_s[2], shift3, ext3, "fmaa_k", xk_ready)
                    for m, x_s in enumerate((xr_s, xk_s)):
                        dve.wait_ge(xrk_hi.sem, xrk_hi.at(n, m + 1))
                        v.tensor_tensor(x_s[1], x_s[2], x_s[0].bitcast(F32), ALU.subtract).then_inc(xrk_lo.sem, 1)

            channel_mixing(None, 0)
            with dve.Fori(0, GROUPS - 1) as g:
                channel_mixing(g, g + 1)
            channel_mixing(GROUPS - 1, None)

            dve.wait_ge(x3_stored.sem, 16 * GROUPS)
            dve.wait_ge(q_stored.sem, 16 * GROUPS)
            v.memset(h_raw[:, :, KEYS:KPAD], 0.0).then_inc(pads_set.sem, 1)
            for p in range(2):
                v.memset(mask_f[p][:, CTX:KPAD], 0.0).then_inc(pads_set.sem, 1)
            for t in range(4):
                v.memset(probs[t][:, KEYS:KPAD], 0.0).then_inc(pads_set.sem, 1)
            for n, w in enumerate((w_k, w_v)):
                dve.wait_ge(kv_w_hi.sem, n + 1)
                v.tensor_tensor(w[1], w[2], w[0].bitcast(F32), ALU.subtract).then_inc(kv_w_lo.sem, 1)
            dve.wait_ge(pads_set.sem, pads_set.per)

            def low_kv(i, p, n):
                dve.wait_ge(kv_hi_set.sem, kv_hi_set.at(i, p * 8 + n + 1))
                ps = bank[6 + n % 2]
                if n < CT:
                    v.scalar_tensor_tensor(kT_lo[p][:, n, :], ps[:, 0:KPAD], vcol("k_b", n), kT_hi[p][:, n, :].bitcast(F32),
                                           ALU.add, ALU.subtract).then_inc(kv_done.sem, 1)
                else:
                    v.tensor_tensor(v_all[p][0:KT_W, n - CT, :, 1, :], ps[0:KT_W, :].rearrange("p (h d) -> p h d", h=AH),
                                    v_all[p][0:KT_W, n - CT, :, 0, :].bitcast(F32), ALU.subtract).then_inc(kv_done.sem, 1)

            for n in range(8):
                low_kv(0, 0, n)

            def mask_scores(i, p):
                dve.wait_ge(q_in[p].sem, 32 * i + 32)
                v.tensor_scalar(mask_f[p][0:LEN, 0:CTX], mask_i[p][0:LEN, :], 0.0, MASKED, ALU.is_equal, ALU.mult).then_inc(mask_ready.sem, 1)

            def attend(i, t, first, last):
                p, h = divmod(t, AH)
                if t < PAIR:
                    dve.wait_ge(s_full.sem, s_full.at(i, t + 1))
                    if t >= 4 or not first:
                        dve.wait_ge(t_full.sem, t_full.at(i, t - 3))
                    if h == 0:
                        dve.wait_ge(mask_ready.sem, mask_ready.at(i, p + 1))
                    v.tensor_copy(tick[:, t:t + 1], eps[0:1, 0:1])
                    v.tensor_tensor_reduce(out=probs[t % 4][0:LEN, 0:KEYS], in0=bank[t % 2][0:LEN, 0:KEYS], in1=mask_f[p][0:LEN, 0:KEYS],
                                           scale=-1.0 / AD, scalar=3.0e38, op0=ALU.add, op1=ALU.min,
                                           accum_out=row_max[0:LEN, h:h + 1]).then_inc(s_masked.sem, 1)
                if h == 12 and t < PAIR:
                    if p > 0 or not first:
                        dve.wait_ge(oT_full.sem, oT_full.at(i, p))
                    dve.wait_ge(pv_done.sem, pv_done.at(i, t - PV_LAG))
                    sum_heads(0, i, p * 2 + 1)
                if h == 4 and runs((p - 1) * AH, first):
                    dve.wait_ge(pv_done.sem, pv_done.at(i, p * AH))
                    sum_heads(1, i, p * 2)
                    dve.wait_ge(o_summed.sem, o_summed.at(i, p * 2))
                    dve.wait_ge(inv_ready.sem, inv_ready.at(i, p))
                    heads_o = o_tok[0:LEN, :].rearrange("p (h d) -> p h d", h=AH)
                    v.tensor_tensor(heads_o, heads_o, spread(row_inv[0:LEN, :], 2, AD), ALU.mult).then_inc(o_ready.sem, 1)
                x = t - LO_LAG
                if runs(x, first):
                    dve.wait_ge(pT_hi_set.sem, pT_hi_set.at(i, x + 1))
                    v.tensor_tensor(pT_lo[x % 4][0:KT_W, :, :], bank[2 + x % 2][0:KT_W, 0:KT_N * LEN].rearrange("p (k n) -> p k n", k=KT_N),
                                    pT_hi[x % 4][0:KT_W, :, :].bitcast(F32), ALU.subtract).then_inc(pT_ready.sem, 1)
                if h == 0 and t < PAIR and runs(t - AH, first):
                    low_kv(i, p, 7)
                elif h % 2 == 0 and h > 0 and t < PAIR and (p == 0 or not last):
                    low_kv(i + p, 1 - p, h // 2 - 1)
                if h == 12 and t < PAIR and (p == 0 or not last):
                    mask_scores(i + p, 1 - p)
                if h == 2 and runs((p - 1) * AH, first):
                    dve.wait_ge(p_ready.sem, p_ready.at(i, p * AH))
                    v.reciprocal(row_inv[0:LEN, :], row_sum[(p - 1) % 2][0:LEN, :]).then_inc(inv_ready.sem, 1)

            def sum_heads(half, i, k):
                parts = bank[5 - half][0:LEN, :].rearrange("p (h s d) -> p h s d", h=AH // 2, s=2)
                dst = o_tok[0:LEN, half * C // 2:(half + 1) * C // 2].rearrange("p (h d) -> p h d", h=AH // 2)
                v.tensor_copy(dst, parts[:, :, 0, :]).then_inc(o_copied.sem, 1)
                dve.wait_ge(o_copied.sem, o_copied.at(i, k))
                v.tensor_tensor(dst, dst, parts[:, :, 1, :], ALU.add).then_inc(o_summed.sem, 1)

            mask_scores(0, 0)
            for t in range(PAIR):
                attend(0, t, True, False)
            with dve.Fori(1, PAIRS - 1) as i:
                for t in range(PAIR):
                    attend(i, t, False, False)
            for t in range(PAIR + DRAIN):
                attend(PAIRS - 1, t, False, True)

            dve.wait_ge(o_stored.sem, 16 * SEQS)

            def residual(g):
                dve.wait_ge(attn_in.sem, 32 * g + 32)
                for ct in range(CT):
                    ps = rf.take(dve, g, ("o", ct))
                    v.scalar_tensor_tensor(mid[:, ct, :], ps[:, 0:GT], vcol("out_b", ct), res_in[:, ct, :], ALU.add, ALU.add).then_inc(resid_ready.sem, 1)

            def norm_c(g):
                dve.wait_ge(cstd_ready.sem, cstd_ready.at(g))
                v.reciprocal(rstd, std).then_inc(crstd_ready.sem, 1)
                dve.wait_ge(crstd_ready.sem, crstd_ready.at(g))
                for ct in range(CT):
                    v.scalar_tensor_tensor(mid[:, ct, :], mid[:, ct, :], vcol("postnorm_w", ct), rstd, ALU.mult, ALU.mult).then_inc(mid_ready.sem, 1)

            def low_mid(g):
                dve.wait_ge(mid_hi_set.sem, mid_hi_set.at(g))
                v.tensor_tensor(mid_lo, mid, mid_hi.bitcast(F32), ALU.subtract).then_inc(mid_lo_set.sem, 1)

            def mlp(g, first, last_group):
                for f in range(FT):
                    if first and f % CT == 0:
                        for n in (f // CT * 2, f // CT * 2 + 1):
                            w = w_1[n // 2] if n % 2 == 0 else w_2[n // 2]
                            dve.wait_ge(mlp_w_hi.sem, n + 1)
                            v.tensor_tensor(w[1], w[2], w[0].bitcast(F32), ALU.subtract).then_inc(mlp_w_lo.sem, 1)
                    dve.wait_ge(hid_hi_set.sem, hid_hi_set.at(g, f + 1))
                    v.tensor_tensor(hid_lo[f % 4], hid[f % 4], hid_hi[f % 4].bitcast(F32), ALU.subtract).then_inc(hid_lo_set.sem, 1)
                    if not last_group and f == 3:
                        residual(g + 1)
                    if not last_group and f == 8:
                        norm_c(g + 1)
                if not last_group:
                    low_mid(g + 1)
                dve.wait_ge(hid_used.sem, hid_used.at(g))
                dve.wait_ge(out_in.sem, 16 * g + 16)
                for ct in range(CT):
                    v.scalar_tensor_tensor(res_out[:, ct, :], bank[ct][:, 0:GT], vcol("mlp_b2", ct), res_out[:, ct, :], ALU.add, ALU.add).then_inc(out_ready.sem, 1)

            residual(0)
            norm_c(0)
            low_mid(0)
            mlp(0, True, False)
            with dve.Fori(1, GROUPS - 1) as g:
                mlp(g, False, False)
            mlp(GROUPS - 1, False, True)


def head_constants():
    row = np.arange(P)
    head, chan = row % HPT, row // HPT
    same = (head[:, None] == head[None, :]).astype(np.float32)
    pick = (same[:, None, :] * (chan[:, None, None] % 4 == np.arange(4)[None, :, None])).astype(np.float32)
    window = np.zeros((P, 2 * P - HPT), np.float32)
    window[row, P - HPT + head] = 1
    heads = np.concatenate([np.eye(P, dtype=np.float32), same, pick.reshape(P, -1), window], 1)
    heads_sum = np.zeros((P, CT, RH), np.float32)
    for ct in range(CT):
        heads_sum[row, ct, ct * HPT + head] = 1
    heads_back = np.ascontiguousarray(heads_sum.transpose(2, 1, 0))
    return heads, heads_sum, heads_back


def kernel(**inputs):
    import concourse.bacc as bacc
    from concourse.bass_utils import run_bass_kernel_spmd

    a = {k: np.asarray(v) for k, v in inputs.items()}
    l0 = {k[len("L0_xattn_"):]: v for k, v in a.items() if k.startswith("L0_")}
    l1 = {k[len("L1_xattn_"):]: v for k, v in a.items() if k.startswith("L1_")}

    def channels(x):
        return x.transpose(2, 0, 1).reshape(CT, P, -1)

    def tiles(x):
        return x.reshape(-1, P).T

    ctx = a["ctx_2048"]
    kv_w = l1["kv_w"].reshape(C, C, 2)
    kv_b = l1["kv_b"].reshape(C, 2)

    def by_row(x, axis):
        x = np.moveaxis(x, axis, 0)
        x = x.reshape(CT, HPT, RS, -1).transpose(0, 2, 1, 3).reshape(x.shape)
        return np.moveaxis(x, 0, axis)

    named = {**l0, **l1, "k_b": kv_b[:, 0], "v_b": kv_b[:, 1], "faaaa": l0["faaaa"].reshape(C)}
    for n in ("time_decay", "faaaa", "gn_w", "gn_b"):
        named[n] = by_row(named[n], 0)
    heads, heads_sum, heads_back = head_constants()
    s0 = ctx[:, 2:2 + RS].reshape(GROUPS, GB, CT, HPT, RS, 4, 4).transpose(0, 4, 3, 2, 6, 5, 1).reshape(GROUPS, P, CT, QUADS, 4, GB)
    edge = ctx[:, 0:2].reshape(GROUPS, GB, 2, CT, P).transpose(0, 4, 2, 3, 1)
    arrays = {
        "xT": channels(a["x"]), "ctxT": ctx.transpose(0, 2, 1).reshape(SEQS, CT, P, CTX), "mask": a["mask_BxS2_ik0"],
        "edgeT": edge, "s0T": s0,
        "vecs": np.concatenate([tiles(named[n]) for n in VECS] + [tiles(l1["mlp_b1"])], 1),
        "w_mix1": l0["maa_w1"], "w_mix2": l0["maa_w2"].reshape(MIX * MIXR, C),
        "w_dec1": l0["decay_w1"], "w_dec2": by_row(l0["decay_w2"], 1),
        "w_rkvg": np.stack([by_row(l0[n].T, 1) for n in ("Wr", "Wk", "Wv", "Wg")]),
        "w_off": np.stack([by_row(l0["Wo"].T, 0)] + [l0[n].T for n in ("fWr", "fWk", "fWv")]),
        "w_q": l1["q_w"], "w_kv": kv_w.transpose(2, 0, 1), "w_out": l1["out_w"],
        "w_mlp1": l1["mlp_w1"], "w_mlp2": l1["mlp_w2"],
        "heads": heads, "heads_sum": heads_sum, "heads_back": heads_back,
    }
    arrays = {k: np.ascontiguousarray(v) for k, v in arrays.items()}
    nc = bacc.Bacc("TRN2", target_bir_lowering=False, num_devices=1)
    args = {k: nc.dram_tensor(k, v.shape, mybir.dt.from_np(v.dtype), kind="ExternalInput").ap() for k, v in arrays.items()}
    out = nc.dram_tensor("out", [CT, P, TOK], F32, kind="ExternalOutput").ap()
    rwkv_perceiver(nc, **args, out=out)
    r = run_bass_kernel_spmd(nc, [arrays], core_ids=[0])
    got = r.results[0]["out"]
    return np.ascontiguousarray(got.reshape(C, SEQS, LEN).transpose(1, 2, 0))
```

```python
from contextlib import ExitStack

import numpy as np

import concourse.bass as bass
from concourse import mybir

F32 = mybir.dt.float32
F32R = mybir.dt.float32r
I32 = mybir.dt.int32
ALU = mybir.AluOpType
ACT = mybir.ActivationFunctionType

P = 128
SEQS, LEN, C = 16, 100, 512
CTX = 361
CT = C // P
GROUPS = 4
GB = SEQS // GROUPS
GT = GB * LEN
TOK = SEQS * LEN
RH, RS = 32, 16
HPT = P // RS
MIX, MIXR = 5, 32
DECR = 64
AH, AD = 16, 32
KEYS = CTX + LEN
KT_N = 4
KT_W = 116
KPAD = KT_N * KT_W
FF = 4 * C
FT = FF // P
QUADS = RS // 4
UNITS = CT * QUADS
RING = 4
SUM_LAG = 3
REC_DRAIN = 4
MIX_ORDER = [1, 2, 3, 4, 0]
LN_EPS, RMS_EPS = 1e-5, 1e-6
MASKED = -3.0e38
MEM_AT = 16512
MEM_WORDS = 53200
PAIR = 2 * AH
T_LAG, HI_LAG, LO_LAG, PV_LAG = 2, 3, 3, 4
DRAIN = 7
W_CHUNKS = 4
EARLY_W = 3

VECS = ["ln1_w", "ln1_b", "ln2_w", "ln2_b", "maa_x", "maa_w", "maa_k", "maa_v", "maa_r", "maa_g",
        "time_decay", "faaaa", "gn_w", "gn_b", "fmaa_k", "fmaa_r", "q_b", "k_b", "v_b", "out_b",
        "postnorm_w", "mlp_b2"]
NVEC = len(VECS) * CT + FT + AH


def spread(ap, axis, n):
    a = ap.unsqueeze(axis)
    return a.broadcast_to(list(a.shape[:axis]) + [n] + list(a.shape[axis + 1:]))


class Signal:

    def __init__(self, nc, ctx, name, per=1):
        self.sem, self.per = ctx.enter_context(nc.semaphore(name)), per

    def at(self, turn, k=None):
        k = self.per if k is None else k
        return turn * self.per + k


class Memory:

    def __init__(self, nc):
        self.nc, self.word = nc, 0

    def at(self, word):
        self.word = word

    def lay(self, name, shape, dt=F32):
        words = int(np.prod(shape[1:]))
        t = self.nc.alloc_sbuf_tensor_at(name, shape, dt, offset=MEM_AT + 4 * self.word)
        self.word += (words + 7) // 8 * 8
        assert self.word <= MEM_WORDS, (name, self.word)
        return t[tuple(slice(None) for _ in shape)]

    def split(self, name, shape):
        here = self.word
        lo = self.lay(name + "_lo", shape, F32R)
        self.at(here)
        raw = self.lay(name + "_raw", shape)
        return self.lay(name + "_hi", shape, F32R), lo, raw


class Results:

    def __init__(self, nc, ctx, name, banks, readers):
        self.banks, self.readers = banks, list(readers.values())
        self.order = {key: i for i, key in enumerate(readers)}
        n = len(banks)
        self.full = [Signal(nc, ctx, f"{name}{b}_full", len(self.readers[b::n])) for b in range(n)]

    def bank(self, key):
        return self.banks[self.order[key] % len(self.banks)]

    def claim(self, eng, turn, key):
        i, n = self.order[key], len(self.banks)
        if i >= n:
            signal, k = self.readers[i - n]
            eng.wait_ge(signal.sem, signal.at(turn, k))
        else:
            signal, _ = self.readers[i::n][-1]
            eng.wait_ge(signal.sem, signal.at(turn, 0))
        return self.banks[i % n]

    def filled(self, ins, key):
        ins.then_inc(self.full[self.order[key] % len(self.banks)].sem, 1)

    def take(self, eng, turn, key):
        i, n = self.order[key], len(self.banks)
        full = self.full[i % n]
        eng.wait_ge(full.sem, full.at(turn, i // n + 1))
        return self.banks[i % n]


def rwkv_perceiver(nc, xT, ctxT, mask, edgeT, s0T, vecs, w_mix1, w_mix2, w_dec1, w_dec2, w_kvrg,
                   w_off, w_q, w_kv, w_out, w_mlp1, w_mlp2, heads, heads_sum, heads_back, out):
    with ExitStack() as ctx:
        mem = Memory(nc)
        sb = mem.lay

        vec = sb("vec", [P, NVEC])
        heads_sb = sb("heads_sb", [P, 6 * P + 2 * P - HPT])
        ident = heads_sb[:, 0:P]
        block_ones = heads_sb[:, P:2 * P]
        pick = heads_sb[:, 2 * P:6 * P].rearrange("p (i n) -> p i n", i=4)
        window = heads_sb[:, 6 * P:]
        heads_sum_sb = sb("heads_sum_sb", [P, CT, RH])
        heads_back_sb = sb("heads_back_sb", [RH, CT, P])
        mean_ones = sb("mean_ones", [P, P])
        eps = sb("eps", [P, 2])
        one = sb("one", [P, 1])
        std = sb("std", [P, GT])
        rstd = sb("rstd", [P, GT])
        tick = sb("tick", [1, PAIR])
        phase_at = mem.word


        def tile_ct(name, words=GT, dt=F32):
            return sb(name, [P, CT, words], dt)

        w_kvrg_s = [mem.split(f"w_{n}", [P, CT, C]) for n in "kvrg"]
        mix1 = sb("mix1", [P, CT, MIX * MIXR])
        mix2a_s = mem.split("mix2a", [P, C])
        mix2b_s = mem.split("mix2b", [MIXR, C])
        dec1 = sb("dec1", [P, CT, DECR])
        dec2 = sb("dec2", [DECR, C])
        xa = tile_ct("xa")
        scratch = tile_ct("scratch")
        shift = tile_ct("shift")
        ext = sb("ext", [P, CT, GB, LEN + 1])
        edge_sb = sb("edge_sb", [P, CT, GB])
        mixed_s = [mem.split(f"mixed{j}", [P, CT, GT]) for j in range(1, MIX)]
        mixed_w = tile_ct("mixed_w")
        rec_out = sb("rec_out", [P, MIX, CT, GT])
        k_sb, v_sb, r_sb, w_sb, g_sb = (rec_out[:, n] for n in range(MIX))
        mix_t1_s = mem.split("mix_t1", [MIXR, GT])
        mix_t4_s = mem.split("mix_t4", [P, GT])
        mem.at(mem.word - GT)
        dec_t = sb("dec_t", [DECR, GT])

        mem.at(phase_at)
        x3_raw = tile_ct("x3_raw")
        x2 = tile_ct("x2")
        half_1_at = mem.word
        y_s = mem.split("y", [P, CT, GT])
        squares = tile_ct("squares")
        gate = tile_ct("gate")
        x_in3 = tile_ct("x_in3")
        ext3 = sb("ext3", [P, CT, GB, LEN + 1])
        edge3 = sb("edge3", [P, CT, GB])
        shift3 = tile_ct("shift3")
        half_2_at = mem.word
        xr_s, xk_s, kk_s = (mem.split(n, [P, CT, GT]) for n in ("xr", "xk", "kk"))
        rr = tile_ct("rr")
        q_out = tile_ct("q_out")
        w_off_s = [mem.split(f"w_{n}", [P, CT, C]) for n in ("o", "fr", "fk", "fv")] + [mem.split("w_q", [P, CT, C])]

        mem.at(phase_at)
        rec_in = [sb(f"rec_in{ct}", [P, 4, GT]) for ct in range(CT)]
        assert phase_at + 2 * 4 * GT == half_1_at
        s0_in = [sb(f"s0_in{ct}", [P, QUADS, 4, GB]) for ct in range(CT)]
        mem_rec_in, mem_w_v = mem.word, phase_at + 4 * CT * C
        v_hi2, v_lo2 = ([sb(f"{n}{p}", [P, GT], F32R) for p in range(2)] for n in ("v_hi2_", "v_lo2_"))
        ring = [sb(f"ring{n}", [P, 4, GT]) for n in range(RING)]
        rk2, bonus2, y_out = (sb(n, [P, 2, GT]) for n in ("rk2", "bonus2", "y_out"))
        pick_r = sb("pick_r", [P, 4, P], F32R)

        mem.at(phase_at)
        w_o = sb("w_o", [P, CT, C])
        b_at = mem.word
        mask_i = [sb(f"mask_i{p}", [P, CTX], I32) for p in range(2)]
        row_max, row_inv = (sb(n, [P, AH]) for n in ("row_max", "row_inv"))
        row_sum = [sb(f"row_sum{p}", [P, AH]) for p in range(2)]
        assert mem.word <= half_1_at
        mem.at(half_1_at)
        w_k, w_v = (mem.split(n, [P, CT, C]) for n in ("w_kk", "w_vv"))
        h_raw = tile_ct("h_raw", KPAD)
        assert mem.word <= half_2_at
        mem.at(half_2_at)
        h_hi, h_lo = ([tile_ct(f"{n}{p}", KPAD, F32R) for p in range(2)] for n in ("h_hi", "h_lo"))
        h_end = mem.word
        k_stack = sb("k_stack", [3 * AD, AH, KPAD], F32R)
        v_all = [sb(f"v_all{p}", [P, KT_N, AH, 2, AD], F32R) for p in range(2)]
        q_raw = sb("q_raw", [3 * AD, AH, LEN])
        q_stack = [sb(f"q_stack{p}", [3 * AD, AH, LEN], F32R) for p in range(2)]
        mask_f = [sb(f"mask_f{p}", [P, KPAD]) for p in range(2)]
        probs = [sb(f"probs{t}", [P, KPAD]) for t in range(4)]
        pT_hi, pT_lo = ([sb(f"{n}{t}", [P, KT_N, LEN], F32R) for t in range(4)] for n in ("pT_hi", "pT_lo"))
        o_tok = sb("o_tok", [P, C])
        o_T = tile_ct("o_T", LEN)

        mem.at(half_1_at)
        attn, res_in, mid = (tile_ct(n) for n in ("attn", "res_in", "mid"))
        square_c = attn
        w_1, w_2 = [None] * W_CHUNKS, [None] * W_CHUNKS
        mlp_w = []
        for c in range(W_CHUNKS):
            for n, (w, shape) in enumerate(((w_1, [P, CT, C]), (w_2, [P, FT // W_CHUNKS, C]))):
                w[c] = mem.split(f"w_{n + 1}{c}", shape)
                mlp_w.append(w[c])
                if len(mlp_w) == EARLY_W:
                    assert mem.word <= h_end
        res_out = tile_ct("res_out")
        mid_hi, mid_lo = (tile_ct(n, GT, F32R) for n in ("mid_hi", "mid_lo"))
        hid = [sb(f"hid{t}", [P, GT]) for t in range(2)]
        rest_at = mem.word
        mem.at(b_at)
        hid += [sb(f"hid{t}", [P, GT]) for t in (2, 3)]
        assert mem.word <= half_1_at
        mem.at(rest_at)
        hid_hi, hid_lo = ([sb(f"{n}{t}", [P, GT], F32R) for t in range(4)] for n in ("hid_hi", "hid_lo"))

        rec_mid = nc.dram_tensor("rec_mid", [4, CT, P, TOK], F32, kind="Internal").ap()
        g_mid = nc.dram_tensor("g_mid", [CT, P, TOK], F32, kind="Internal").ap()
        y_mid = nc.dram_tensor("y_mid", [CT, P, TOK], F32, kind="Internal").ap()
        x_mid = nc.dram_tensor("x_mid", [CT, P, TOK], F32, kind="Internal").ap()
        q_mid = nc.dram_tensor("q_mid", [CT, P, TOK], F32, kind="Internal").ap()
        o_mid = nc.dram_tensor("o_mid", [CT, P, TOK], F32, kind="Internal").ap()

        ps_all = ctx.enter_context(nc.psum_tensor("ps_all", [P, 8, 512], F32))
        bank = [ps_all[:, i, :] for i in range(8)]
        ps_v = ps_all[:, 0:4, 0:GT]

        def vcol(name, ct):
            i = VECS.index(name) * CT + ct
            return vec[:, i:i + 1]

        def bias1(m):
            return vec[:, len(VECS) * CT + m:len(VECS) * CT + m + 1]

        def k_bias(h):
            return vec[0:AD, NVEC - AH + h:NVEC - AH + h + 1]

        def by_seq(ap):
            return ap.rearrange("p (b l) -> p b l", b=GB)

        def group_cols(dram, g):
            return dram[:, :, bass.ds(g * GT, GT)].rearrange("c p n -> p c n")

        def sig(name, per=1):
            return Signal(nc, ctx, name, per)

        loaded = sig("loaded")
        weights_in = [sig(f"weights_in{n}") for n in range(2 * W_CHUNKS)]
        weights_due = {}
        for phase, number in (("kvrg", 4), ("off", 5), ("kv", 3), ("mlp", 2 * W_CHUNKS)):
            for n in range(number):
                weights_due[phase, n] = 16 + sum(16 for other, m in weights_due if m == n)

        def await_weights(eng, phase, n):
            eng.wait_ge(weights_in[n].sem, weights_due[phase, n])

        kvrg_hi, kvrg_lo = sig("kvrg_hi", 4), sig("kvrg_lo", 4)
        consts_set = sig("consts_set", 5)
        x_in = sig("x_in")
        mean_full, var_full = sig("mean_full"), sig("var_full")
        centred_ready = sig("centred_ready")
        square_ready = sig("square_ready")
        std_ready = sig("std_ready")
        rstd_ready = sig("rstd_ready")
        normed = sig("normed")
        ext_ready = sig("ext_ready", CT + 1)
        shift_ready = sig("shift_ready")
        mixx_ready = sig("mixx_ready", CT)
        mix_rank, mix_t_hi, mix_t_lo = (sig(n, 2) for n in ("mix_rank", "mix_t_hi", "mix_t_lo"))
        mix2_hi, mix2_lo = sig("mix2_hi", 2), sig("mix2_lo", 2)
        mix_scaled = sig("mix_scaled", MIX * CT)
        mixed_ready = sig("mixed_ready", MIX)
        mixed_hi = sig("mixed_hi", MIX - 1)
        mixed_lo = sig("mixed_lo", MIX - 1)
        dec_rank = sig("dec_rank")
        dec_exp = sig("dec_exp", CT)
        k_ready, v_ready, r_ready, w_ready, g_ready = (sig(f"{n}_ready", CT) for n in "kvrwg")
        rec_stored = sig("rec_stored")

        readers = {"rank4": (mix_rank, 1), "rank1": (mix_rank, 2)}
        readers |= {("mix", j, ct): (mix_scaled, n * CT + ct + 1) for n, j in enumerate(MIX_ORDER) for ct in range(CT)}
        readers |= {("k", ct): (k_ready, ct + 1) for ct in range(CT)} | {("v", ct): (v_ready, ct + 1) for ct in range(CT)}
        readers |= {"dec1": (dec_rank, 1)} | {("r", ct): (r_ready, ct + 1) for ct in range(CT)}
        readers |= {("dec2", ct): (dec_exp, ct + 1) for ct in range(CT)} | {("g", ct): (g_ready, ct + 1) for ct in range(CT)}
        ra = Results(nc, ctx, "ra", bank[0:5], readers)

        tile_in = [sig(f"tile_in{ct}") for ct in range(CT)]
        v_hi_set, v_lo_set = sig("v_hi_set", CT), sig("v_lo_set", CT)
        vals_full = sig("vals_full", UNITS)
        start_state = sig("start_state", UNITS)
        outer_ready = sig("outer_ready", UNITS)
        scanned = sig("scanned", UNITS)
        weighed = sig("weighed", UNITS)
        summed = sig("summed", UNITS)
        rk_ready = sig("rk_ready", CT)
        bonus_full = sig("bonus_full", CT)
        bonus_ready = sig("bonus_ready", CT)
        y_ready = sig("y_ready", CT)
        y_stored = [sig(f"y_stored{p}") for p in range(2)]

        off_hi, off_lo = sig("off_hi", 5), sig("off_lo", 5)
        yg_in = sig("yg_in")
        x3_in = sig("x3_in")
        y_centred = sig("y_centred", CT)
        y_square = sig("y_square", CT)
        y_std = sig("y_std")
        y_rstd = sig("y_rstd")
        y_scaled = sig("y_scaled", CT)
        y_gated = sig("y_gated", CT)
        y_hi_set, y_lo_set = sig("y_hi_set", CT), sig("y_lo_set", CT)
        x2_ready = sig("x2_ready", CT)
        centred3 = sig("centred3")
        square3 = sig("square3")
        std3 = sig("std3")
        rstd3 = sig("rstd3")
        normed3 = sig("normed3", CT)
        ext3_ready = sig("ext3_ready", CT + 1)
        shift3_ready = sig("shift3_ready", CT)
        xr_ready, xk_ready = sig("xr_ready", CT), sig("xk_ready", CT)
        xrk_hi, xrk_lo = sig("xrk_hi", 2 * CT), sig("xrk_lo", 2 * CT)
        rr_ready = sig("rr_ready", CT)
        relu_ready = sig("relu_ready", CT)
        kk_ready = sig("kk_ready", CT)
        kk_hi_set, kk_lo_set = sig("kk_hi_set", CT), sig("kk_lo_set", CT)
        ff_ready = sig("ff_ready", CT)
        x3_ready = sig("x3_ready", CT)
        x3_hi_set, x3_lo_set = sig("x3_hi_set"), sig("x3_lo_set")
        q_ready = sig("q_ready", CT)
        x3_stored, q_stored = sig("x3_stored"), sig("q_stored")

        readers = {("ymean", ct): (y_centred, ct + 1) for ct in range(CT)} | {"yvar": (y_std, 1)}
        readers |= {("yback", ct): (y_scaled, ct + 1) for ct in range(CT)}
        readers |= {("o", ct): (x2_ready, ct + 1) for ct in range(CT)}
        readers |= {"mean2": (centred3, 1), "var2": (std3, 1)}
        r1 = Results(nc, ctx, "r1_", bank[0:3], readers)
        readers = {(n, ct): (done, ct + 1) for n, done in (("fr", rr_ready), ("fk", relu_ready), ("fv", ff_ready), ("q", q_ready))
                   for ct in range(CT)}
        r2 = Results(nc, ctx, "r2_", bank[3:7], readers)

        kv_w_hi = sig("kv_w_hi", 2)
        kv_w_lo = sig("kv_w_lo", 2)
        h_pads_set = sig("h_pads_set")
        pads_set = sig("pads_set", 6)
        h_in = sig("h_in")
        q_in = [sig(f"q_in{p}") for p in range(2)]
        h_hi_set, h_lo_set, q_hi_set, q_lo_set = (sig(n, 2) for n in ("h_hi_set", "h_lo_set", "q_hi_set", "q_lo_set"))
        mask_ready = sig("mask_ready", 2)
        kv_full = sig("kv_full", 16)
        v_hi_ready, v_done = sig("v_hi_ready", 2 * KT_N), sig("v_done", 2 * KT_N)
        k_hi_ready, k_done = sig("k_hi_ready", 2 * AH), sig("k_done", 2 * AH)
        s_full = sig("s_full", 2 * AH)
        s_masked = sig("s_masked", 2 * AH)
        p_ready = sig("p_ready", 2 * AH)
        t_full = sig("t_full", 2 * AH)
        pT_hi_set = sig("pT_hi_set", 2 * AH)
        pT_ready = sig("pT_ready", 2 * AH)
        pv_done = sig("pv_done", 2 * AH)
        inv_ready = sig("inv_ready", 2)
        o_copied = sig("o_copied", 4)
        o_summed = sig("o_summed", 4)
        o_ready = sig("o_ready", 2)
        oT_full = sig("oT_full", 2)
        oT_ready = sig("oT_ready", 2)
        o_stored = sig("o_stored")

        mlp_w_hi = sig("mlp_w_hi", 2 * W_CHUNKS)
        mlp_w_lo = sig("mlp_w_lo", 2 * W_CHUNKS)
        attn_in = sig("attn_in")
        out_in = sig("out_in")
        resid_ready = sig("resid_ready", CT)
        sq_ready = sig("sq_ready")
        cstd_ready = sig("cstd_ready")
        crstd_ready = sig("crstd_ready")
        mid_ready = sig("mid_ready", CT)
        mid_hi_set = sig("mid_hi_set")
        mid_lo_set = sig("mid_lo_set")
        hid_full = sig("hid_full", FT)
        hid_ready = sig("hid_ready", FT)
        hid_hi_set = sig("hid_hi_set", FT)
        hid_lo_set = sig("hid_lo_set", FT)
        hid_used = sig("hid_used", FT)
        out_ready = sig("out_ready", CT)
        c_out = sig("c_out")
        front_c = {("o", ct): (resid_ready, ct + 1) for ct in range(CT)} | {"ms": (cstd_ready, 1)}
        rf = Results(nc, ctx, "rf", bank[6:8], front_c)

        def runs(x, first):
            return x < PAIR and (x >= 0 or not first)

        block = ctx.enter_context(nc.Block())

        def rows(w):
            return w.rearrange("(c p) n -> p c n", p=P)

        loads = [
            (vec, vecs), (mix1, rows(w_mix1)), (mix2a_s[2], w_mix2[0:P, :]), (mix2b_s[2], w_mix2[P:MIX * MIXR, :]),
            (dec1, rows(w_dec1)), (dec2, w_dec2), (heads_sb, heads), (heads_sum_sb, heads_sum), (heads_back_sb, heads_back),
        ]
        ALL_LOADED = 16 * len(loads)
        PAIRS = SEQS // 2

        @block.sync
        def _(sp):
            def load_x(g):
                sp.wait_ge(ext_ready.sem, ext_ready.at(g, 0))
                sp.dma_start(xa, group_cols(xT, g)).then_inc(x_in.sem, 16)
                sp.dma_start(edge_sb, edgeT[bass.ds(g, 1), :, 1].rearrange("o p c b -> (o p) c b")).then_inc(x_in.sem, 16)

            def store_rec(g):
                for n, ready in enumerate((k_ready, v_ready, r_ready, w_ready, g_ready)):
                    sp.wait_ge(ready.sem, ready.at(g))
                    dst = group_cols(rec_mid[n], g) if n < 4 else group_cols(g_mid, g)
                    sp.dma_start(dst, rec_out[:, n]).then_inc(rec_stored.sem, 16)

            load_x(0)
            for n in range(4):
                sp.dma_start(w_kvrg_s[n][2], rows(w_kvrg[n])).then_inc(weights_in[n].sem, 16)
            with sp.Fori(0, GROUPS - 1) as g:
                load_x(g + 1)
                store_rec(g)
            def load_tile(g, ct):
                sp.dma_start(rec_in[ct], rec_mid[:, ct, :, bass.ds(g * GT, GT)].rearrange("k p n -> p k n")).then_inc(tile_in[ct].sem, 16)
                sp.dma_start(s0_in[ct], s0T[bass.ds(g, 1), :, ct].rearrange("o p q i b -> (o p) q i b")).then_inc(tile_in[ct].sem, 16)

            assert mem_rec_in <= mem_w_v
            sp.wait_ge(rec_stored.sem, 80 * (GROUPS - 1))
            sp.wait_ge(v_ready.sem, v_ready.at(GROUPS - 1))
            for ct in range(CT):
                load_tile(0, ct)
            store_rec(GROUPS - 1)
            sp.wait_ge(rec_stored.sem, 80 * GROUPS)
            for n, src in enumerate([w_off[m] for m in range(4)] + [w_q]):
                sp.dma_start(w_off_s[n][2], rows(src)).then_inc(weights_in[n].sem, 16)

            def rec_io(g, last):
                for ct in range(CT):
                    sp.wait_ge(y_ready.sem, y_ready.at(g, ct + 1))
                    sp.dma_start(y_mid[ct, :, bass.ds(g * GT, GT)], y_out[:, ct % 2, :]).then_inc(y_stored[ct % 2].sem, 16)
                    if not last:
                        load_tile(g + 1, ct)
                    elif ct == 2:
                        for p in range(2):
                            sp.wait_ge(y_stored[p].sem, 32 * (GROUPS - 1))
                        sp.dma_start(y_s[2], group_cols(y_mid, 0)).then_inc(yg_in.sem, 16)

            with sp.Fori(0, GROUPS - 1) as g:
                rec_io(g, False)
            rec_io(GROUPS - 1, True)

            def load_gate(g):
                sp.dma_start(gate, group_cols(g_mid, g)).then_inc(x3_in.sem, 16)

            def load_yg(g):
                sp.wait_ge(x2_ready.sem, x2_ready.at(g, 0))
                for p in range(2):
                    sp.wait_ge(y_stored[p].sem, 16 * CT // 2 * GROUPS)
                sp.dma_start(y_s[2], group_cols(y_mid, g)).then_inc(yg_in.sem, 16)
                load_gate(g)

            def load_x3(g):
                sp.wait_ge(ext3_ready.sem, ext3_ready.at(g, 0))
                sp.dma_start(x_in3, group_cols(xT, g)).then_inc(x3_in.sem, 16)
                sp.dma_start(edge3, edgeT[bass.ds(g, 1), :, 0].rearrange("o p c b -> (o p) c b")).then_inc(x3_in.sem, 16)

            def store_x3(g):
                sp.wait_ge(x3_ready.sem, x3_ready.at(g))
                sp.dma_start(group_cols(x_mid, g), x3_raw).then_inc(x3_stored.sem, 16)

            def store_q(g):
                sp.wait_ge(q_ready.sem, q_ready.at(g))
                sp.dma_start(group_cols(q_mid, g), q_out).then_inc(q_stored.sem, 16)

            def load_h(b):
                sp.dma_start(h_raw[:, :, 0:CTX], ctxT[bass.ds(b, 1)].rearrange("o c p n -> (o p) c n")).then_inc(h_in.sem, 16)
                sp.dma_start(h_raw[:, :, CTX:KEYS], x_mid[:, :, bass.ds(b * LEN, LEN)].rearrange("c p n -> p c n")).then_inc(h_in.sem, 16)

            load_gate(0)
            load_x3(0)
            load_yg(1)
            load_x3(1)
            with sp.Fori(0, GROUPS - 2) as g:
                store_x3(g)
                load_yg(g + 2)
                store_q(g)
                load_x3(g + 2)
            store_x3(GROUPS - 2)
            store_q(GROUPS - 2)
            sp.wait_ge(xk_ready.sem, xk_ready.at(GROUPS - 1))
            sp.dma_start(w_k[2], rows(w_kv[0])).then_inc(weights_in[0].sem, 16)
            sp.dma_start(w_v[2], rows(w_kv[1])).then_inc(weights_in[1].sem, 16)
            sp.wait_ge(x3_stored.sem, 16 * (GROUPS - 1))
            load_h(0)
            store_x3(GROUPS - 1)
            store_q(GROUPS - 1)

            sp.wait_ge(x3_stored.sem, 16 * GROUPS)
            sp.wait_ge(q_stored.sem, 16 * GROUPS)

            def load_q(b, p):
                by_head = q_mid.rearrange("c p n -> (c p) n").rearrange("(h r) n -> r h n", r=AD)
                for m in range(3):
                    sp.dma_start(q_raw[m * AD:(m + 1) * AD], by_head[:, :, bass.ds(b * LEN, LEN)]).then_inc(q_in[p].sem, 16)
                sp.dma_start(mask_i[p][0:LEN, :], mask[bass.ds(b, 1), :].broadcast_to([LEN, CTX])).then_inc(q_in[p].sem, 16)

            load_q(0, 0)
            sp.wait_ge(h_lo_set.sem, 1)
            load_h(1)
            sp.wait_ge(q_lo_set.sem, 1)
            load_q(1, 1)
            sp.dma_start(w_o, rows(w_out)).then_inc(weights_in[2].sem, 16)

            def store_o(b, turn, k):
                sp.wait_ge(oT_ready.sem, oT_ready.at(turn, k))
                sp.dma_start(o_mid[:, :, bass.ds(b * LEN, LEN)].rearrange("c p n -> p c n"), o_T).then_inc(o_stored.sem, 16)

            def load_mlp_w(n):
                c = n // 2
                src = rows(w_mlp1)[:, :, c * C:(c + 1) * C] if n % 2 == 0 else rows(w_mlp2)[:, c * CT:(c + 1) * CT, :]
                sp.dma_start(mlp_w[n][2], src).then_inc(weights_in[n].sem, 16)

            def pair_io(i, first, last):
                for p in range(2):
                    if not last:
                        sp.wait_ge(h_lo_set.sem, h_lo_set.at(i, p + 2))
                        load_h(i * 2 + p + 2)
                    if last and p == 1:
                        sp.wait_ge(kv_full.sem, 8 * SEQS)
                        sp.wait_ge(o_stored.sem, 16 * (SEQS - 2))
                        sp.dma_start(attn, group_cols(o_mid, 0)).then_inc(attn_in.sem, 16)
                        sp.dma_start(res_in, group_cols(x_mid, 0)).then_inc(attn_in.sem, 16)
                        for n in range(EARLY_W):
                            load_mlp_w(n)
                    if p == 1 or not first:
                        store_o(i * 2 + p - 1, i, p)
                    if not last:
                        sp.wait_ge(s_full.sem, s_full.at(i, (p + 1) * AH))
                        sp.wait_ge(q_lo_set.sem, q_lo_set.at(i, p + 2))
                        load_q(i * 2 + p + 2, p)

            pair_io(0, True, False)
            with sp.Fori(1, PAIRS - 1) as i:
                pair_io(i, False, False)
            pair_io(PAIRS - 1, False, True)
            store_o(SEQS - 1, PAIRS, 0)

            sp.wait_ge(o_stored.sem, 16 * SEQS)
            for n in range(EARLY_W, 2 * W_CHUNKS):
                load_mlp_w(n)

            def group_io(g, last):
                sp.wait_ge(c_out.sem, 16 * g)
                sp.dma_start(res_out, group_cols(x_mid, g)).then_inc(out_in.sem, 16)
                if not last:
                    sp.wait_ge(cstd_ready.sem, cstd_ready.at(g))
                    sp.wait_ge(resid_ready.sem, resid_ready.at(g))
                    sp.dma_start(attn, group_cols(o_mid, g + 1)).then_inc(attn_in.sem, 16)
                    sp.dma_start(res_in, group_cols(x_mid, g + 1)).then_inc(attn_in.sem, 16)
                sp.wait_ge(out_ready.sem, out_ready.at(g))
                sp.dma_start(group_cols(out, g), res_out).then_inc(c_out.sem, 16)

            with sp.Fori(0, GROUPS - 1) as g:
                group_io(g, False)
            group_io(GROUPS - 1, True)
            sp.wait_ge(c_out.sem, 16 * GROUPS)

        @block.tensor
        def _(pe):
            mm = nc.tensor.matmul
            pe.wait_ge(consts_set.sem, consts_set.per)

            def exact(ps, weights, moving, first, last):
                mm(ps, weights[0], moving[0], start=first, stop=False)
                mm(ps, weights[1], moving[0], start=False, stop=False)
                return mm(ps, weights[0], moving[1], start=False, stop=last)

            def project(res, g, key, w, ct, src):
                ps = res.claim(pe, g, key)
                cols = slice(ct * P, (ct + 1) * P)
                for kt in range(CT):
                    last = exact(ps[:, 0:GT], (w[0][:, kt, cols], w[1][:, kt, cols]), (src[0][:, kt, :], src[1][:, kt, :]), kt == 0, kt == CT - 1)
                res.filled(last, key)

            def mean_1(g):
                pe.wait_ge(x_in.sem, 32 * g + 32)
                for kt in range(CT):
                    last = mm(bank[7][:, 0:GT], mean_ones, xa[:, kt, :], start=kt == 0, stop=kt == CT - 1)
                last.then_inc(mean_full.sem, 1)

            def var_1(g):
                pe.wait_ge(square_ready.sem, square_ready.at(g))
                for kt in range(CT):
                    last = mm(bank[6][:, 0:GT], mean_ones, scratch[:, kt, :], start=kt == 0, stop=kt == CT - 1)
                last.then_inc(var_full.sem, 1)

            def projections(g, first, last_group):
                pe.wait_ge(mixx_ready.sem, mixx_ready.at(g))
                for key, lo, hi in (("rank4", 0, P), ("rank1", P, MIX * MIXR)):
                    ps = ra.claim(pe, g, key)
                    for kt in range(CT):
                        last = mm(ps[0:hi - lo, 0:GT], mix1[:, kt, lo:hi], scratch[:, kt, :], start=kt == 0, stop=kt == CT - 1)
                    ra.filled(last, key)
                if first:
                    pe.wait_ge(mix2_lo.sem, mix2_lo.per)
                pe.wait_ge(mix_t_lo.sem, mix_t_lo.at(g))
                for j in MIX_ORDER:
                    rows_j = slice(MIXR * (j % 4), MIXR * (j % 4) + MIXR)
                    w, t = (mix2a_s, mix_t4_s) if j < 4 else (mix2b_s, mix_t1_s)
                    for ct in range(CT):
                        ps = ra.claim(pe, g, ("mix", j, ct))
                        cols = slice(ct * P, (ct + 1) * P)
                        ra.filled(exact(ps[:, 0:GT], (w[0][rows_j, cols], w[1][rows_j, cols]), (t[0][rows_j, :], t[1][rows_j, :]), True, True),
                                  ("mix", j, ct))
                for n, name in enumerate("kvrg"):
                    if first:
                        pe.wait_ge(kvrg_lo.sem, n + 1)
                    pe.wait_ge(mixed_lo.sem, mixed_lo.at(g, n + 1))
                    if n == 2:
                        pe.wait_ge(mixed_ready.sem, mixed_ready.at(g))
                        ps = ra.claim(pe, g, "dec1")
                        for kt in range(CT):
                            last = mm(ps[0:DECR, 0:GT], dec1[:, kt, :], mixed_w[:, kt, :], start=kt == 0, stop=kt == CT - 1)
                        ra.filled(last, "dec1")
                        if not last_group:
                            var_1(g + 1)
                    if n == 3:
                        pe.wait_ge(dec_rank.sem, dec_rank.at(g))
                        for ct in range(CT):
                            ps = ra.claim(pe, g, ("dec2", ct))
                            ra.filled(mm(ps[:, 0:GT], dec2[:, ct * P:(ct + 1) * P], dec_t, start=True, stop=True), ("dec2", ct))
                    for ct in range(CT):
                        project(ra, g, (name, ct), w_kvrg_s[n], ct, mixed_s[n])
                    if n == 0 and not last_group:
                        mean_1(g + 1)

            mean_1(0)
            var_1(0)
            pe.wait_ge(loaded.sem, ALL_LOADED)
            projections(0, True, False)
            with pe.Fori(1, GROUPS - 1) as g:
                projections(g, False, False)
            projections(GROUPS - 1, False, True)

            pe.wait_ge(w_ready.sem, w_ready.at(GROUPS - 1))
            pe.wait_ge(g_ready.sem, g_ready.at(GROUPS - 1))

            def recurrence(g, u, first):
                if u < UNITS:
                    ct, q = divmod(u, QUADS)
                    if q == 0:
                        pe.wait_ge(v_lo_set.sem, v_lo_set.at(g, ct + 1))
                    if u > 0 or not first:
                        pe.wait_ge(outer_ready.sem, outer_ready.at(g, u))
                    for i in range(4):
                        rows_i = slice(32 * i, 32 * i + 32)
                        mm(ps_v[:, i, :], pick_r[rows_i, q, :], v_hi2[ct % 2][rows_i, :], start=True, stop=False)
                        last = mm(ps_v[:, i, :], pick_r[rows_i, q, :], v_lo2[ct % 2][rows_i, :], start=False, stop=True)
                    last.then_inc(vals_full.sem, 1)
                    if q == 1:
                        pe.wait_ge(rk_ready.sem, rk_ready.at(g, ct + 1))
                        if ct >= 2 or not first:
                            pe.wait_ge(bonus_ready.sem, bonus_ready.at(g, ct - 1))
                        mm(bank[6 + ct % 2][:, 0:GT], block_ones, rk2[:, ct % 2, :], start=True, stop=True).then_inc(bonus_full.sem, 1)
                x = u - SUM_LAG
                if x < UNITS and (x >= 0 or not first):
                    ct, q = divmod(x, QUADS)
                    pe.wait_ge(weighed.sem, weighed.at(g, x + 1))
                    if q == 0 and (ct >= 2 or not first):
                        pe.wait_ge(y_ready.sem, y_ready.at(g, ct - 1))
                    for i in range(4):
                        row = P - HPT - HPT * (4 * i + q)
                        last = mm(bank[4 + ct % 2][:, 0:GT], window[:, row:row + P], ring[x % RING][:, i, :], start=q == 0 and i == 0, stop=q == 3 and i == 3)
                    last.then_inc(summed.sem, 1)

            for u in range(UNITS):
                recurrence(0, u, True)
            with pe.Fori(1, GROUPS - 1) as g:
                for u in range(UNITS):
                    recurrence(g, u, False)
            for u in range(UNITS + REC_DRAIN):
                recurrence(GROUPS - 1, u, False)

            pe.wait_ge(y_ready.sem, CT * GROUPS)

            def y_mean(g, cts):
                pe.wait_ge(yg_in.sem, 16 * g + 16)
                for ct in cts:
                    ps = r1.claim(pe, g, ("ymean", ct))
                    r1.filled(mm(ps[:, 0:GT], block_ones, y_s[2][:, ct, :], start=True, stop=True), ("ymean", ct))

            def y_var(g):
                ps = r1.claim(pe, g, "yvar")
                for ct in range(CT):
                    pe.wait_ge(y_square.sem, y_square.at(g, ct + 1))
                    last = mm(ps[0:RH, 0:GT], heads_sum_sb[:, ct, :], squares[:, ct, :], start=ct == 0, stop=ct == CT - 1)
                r1.filled(last, "yvar")

            def y_back(g):
                pe.wait_ge(y_rstd.sem, y_rstd.at(g))
                for ct in range(CT):
                    ps = r1.claim(pe, g, ("yback", ct))
                    r1.filled(mm(ps[:, 0:GT], heads_back_sb[:, ct, :], rstd[0:RH, :], start=True, stop=True), ("yback", ct))

            def y_project(g):
                pe.wait_ge(y_lo_set.sem, y_lo_set.at(g))
                for ct in range(CT):
                    project(r1, g, ("o", ct), w_off_s[0], ct, y_s)

            def mean_2(g):
                pe.wait_ge(x2_ready.sem, x2_ready.at(g))
                ps = r1.claim(pe, g, "mean2")
                for kt in range(CT):
                    last = mm(ps[:, 0:GT], mean_ones, x2[:, kt, :], start=kt == 0, stop=kt == CT - 1)
                r1.filled(last, "mean2")

            def var_2(g):
                pe.wait_ge(square3.sem, square3.at(g))
                ps = r1.claim(pe, g, "var2")
                for kt in range(CT):
                    last = mm(ps[:, 0:GT], mean_ones, squares[:, kt, :], start=kt == 0, stop=kt == CT - 1)
                r1.filled(last, "var2")

            def channel_mixing(g, n):
                if n is not None:
                    y_mean(n, (0, 1, 2))
                if g is not None:
                    pe.wait_ge(xrk_lo.sem, xrk_lo.at(g, CT))
                    for ct in range(CT):
                        project(r2, g, ("fr", ct), w_off_s[1], ct, xr_s)
                if n is not None:
                    y_mean(n, (3,))
                if g is not None:
                    pe.wait_ge(xrk_lo.sem, xrk_lo.at(g))
                    for ct in (0, 1):
                        project(r2, g, ("fk", ct), w_off_s[2], ct, xk_s)
                if n is not None:
                    y_var(n)
                if g is not None:
                    for ct in (2, 3):
                        project(r2, g, ("fk", ct), w_off_s[2], ct, xk_s)
                if n is not None:
                    y_back(n)
                if g is not None:
                    pe.wait_ge(kk_lo_set.sem, kk_lo_set.at(g))
                    for ct in range(CT):
                        project(r2, g, ("fv", ct), w_off_s[3], ct, kk_s)
                if g is None:
                    pe.wait_ge(off_lo.sem, 1)
                if n is not None:
                    y_project(n)
                    mean_2(n)
                if g is not None:
                    pe.wait_ge(x3_lo_set.sem, x3_lo_set.at(g))
                    for ct in (0, 1):
                        project(r2, g, ("q", ct), w_off_s[4], ct, kk_s)
                if n is not None:
                    var_2(n)
                if g is not None:
                    for ct in (2, 3):
                        project(r2, g, ("q", ct), w_off_s[4], ct, kk_s)

            channel_mixing(None, 0)
            pe.wait_ge(off_lo.sem, off_lo.per)
            with pe.Fori(0, GROUPS - 1) as g:
                channel_mixing(g, g + 1)
            channel_mixing(GROUPS - 1, None)

            pe.wait_ge(q_ready.sem, CT * GROUPS)
            pe.wait_ge(kv_w_lo.sem, kv_w_lo.per)

            def make_kv(i, p, n, kts):
                m = n // 2
                if kts[0] == 0:
                    if n % 2 == 1:
                        pe.wait_ge(v_done.sem, v_done.at(i, p * KT_N + m))
                    else:
                        pe.wait_ge(k_done.sem, k_done.at(i, p * AH + 4 * m))
                    if n == 0:
                        pe.wait_ge(h_lo_set.sem, h_lo_set.at(i, p + 1))
                ps = bank[6 + n % 2]
                for kt in kts:
                    h = (h_hi[p][:, kt, :], h_lo[p][:, kt, :])
                    if n % 2 == 1:
                        cols = slice(m * KT_W, (m + 1) * KT_W)
                        last = exact(ps[0:KT_W, :], (h[0][:, cols], h[1][:, cols]), (w_v[0][:, kt, :], w_v[1][:, kt, :]), kt == 0, kt == CT - 1)
                    else:
                        cols = slice(m * P, (m + 1) * P)
                        last = exact(ps[:, 0:KPAD], (w_k[0][:, kt, cols], w_k[1][:, kt, cols]), h, kt == 0, kt == CT - 1)
                if kts[-1] == CT - 1:
                    last.then_inc(kv_full.sem, 1)

            for n in range(8):
                make_kv(0, 0, n, (0, 1, 2, 3))

            def attend(i, t, first, last):
                p, h = divmod(t, AH)
                if t < PAIR:
                    pe.wait_ge(k_done.sem, k_done.at(i, t + 1))
                    if h == 0:
                        pe.wait_ge(q_lo_set.sem, q_lo_set.at(i, p + 1))
                    if t >= 2 or not first:
                        pe.wait_ge(s_masked.sem, s_masked.at(i, t - 1))
                    mm(bank[t % 2][0:LEN, 0:KPAD], q_stack[p][:, h, :], k_stack[:, h, :], start=True, stop=True).then_inc(s_full.sem, 1)
                x = t - T_LAG
                if runs(x, first):
                    pe.wait_ge(p_ready.sem, p_ready.at(i, x + 1))
                    if x >= 2 or not first:
                        pe.wait_ge(pT_ready.sem, pT_ready.at(i, x - 1))
                    for k in range(KT_N):
                        done = nc.tensor.transpose(bank[2 + x % 2][0:KT_W, k * LEN:(k + 1) * LEN], probs[x % 4][0:LEN, k * KT_W:(k + 1) * KT_W], ident[0:LEN, 0:LEN])
                    done.then_inc(t_full.sem, 1)
                x = t - PV_LAG
                if runs(x, first):
                    b, h_x = divmod(x, AH)
                    pe.wait_ge(pT_ready.sem, pT_ready.at(i, x + 1))
                    if h_x == 0:
                        pe.wait_ge(v_done.sem, v_done.at(i, (b + 1) * KT_N))
                        if b > 0 or not first:
                            pe.wait_ge(o_summed.sem, o_summed.at(i, 2 * b - 1))
                    if h_x == AH // 2 and (b > 0 or not first):
                        pe.wait_ge(oT_ready.sem, oT_ready.at(i, b))
                    ps = bank[5 - h_x // (AH // 2)][0:LEN, h_x % (AH // 2) * 2 * AD:(h_x % (AH // 2) + 1) * 2 * AD]
                    for k in range(KT_N):
                        mm(ps, pT_hi[x % 4][0:KT_W, k, :], v_all[b % 2][0:KT_W, k, h_x].rearrange("p s d -> p (s d)"), start=k == 0, stop=False)
                        done = mm(ps[:, 0:AD], pT_lo[x % 4][0:KT_W, k, :], v_all[b % 2][0:KT_W, k, h_x, 0, :], start=False, stop=k == KT_N - 1)
                    done.then_inc(pv_done.sem, 1)
                if t < PAIR and (p == 0 or not last):
                    make_kv(i + p, 1 - p, h // 2, (0, 1) if h % 2 == 0 else (2, 3))
                if h == 5 and runs((p - 1) * AH, first):
                    pe.wait_ge(o_ready.sem, o_ready.at(i, p))
                    for ct in range(CT):
                        done = nc.tensor.transpose(bank[4][:, ct * LEN:(ct + 1) * LEN], o_tok[0:LEN, ct * P:(ct + 1) * P], ident[0:LEN, 0:LEN])
                    done.then_inc(oT_full.sem, 1)

            for t in range(PAIR):
                attend(0, t, True, False)
            with pe.Fori(1, PAIRS - 1) as i:
                for t in range(PAIR):
                    attend(i, t, False, False)
            for t in range(PAIR + DRAIN):
                attend(PAIRS - 1, t, False, True)

            await_weights(pe, "kv", 2)
            pe.wait_ge(oT_ready.sem, SEQS)

            def project_out(g):
                pe.wait_ge(attn_in.sem, 32 * g + 32)
                for ct in range(CT):
                    ps = rf.claim(pe, g, ("o", ct))
                    for kt in range(CT):
                        last = mm(ps[:, 0:GT], w_o[:, kt, ct * P:(ct + 1) * P], attn[:, kt, :], start=kt == 0, stop=kt == CT - 1)
                    rf.filled(last, ("o", ct))

            def mean_square(g):
                pe.wait_ge(sq_ready.sem, sq_ready.at(g))
                ps = rf.claim(pe, g, "ms")
                for kt in range(CT):
                    last = mm(ps[:, 0:GT], mean_ones, square_c[:, kt, :], start=kt == 0, stop=kt == CT - 1)
                rf.filled(last, "ms")

            def mlp(g, first, last_group):
                pe.wait_ge(mid_lo_set.sem, mid_lo_set.at(g))
                for f in range(FT + 2):
                    if f < FT:
                        c, cols = f // CT, slice(f % CT * P, (f % CT + 1) * P)
                        if first and f % CT == 0:
                            pe.wait_ge(mlp_w_lo.sem, 2 * c + 1)
                        pe.wait_ge(hid_ready.sem, hid_ready.at(g, max(f - 1, 0)))
                        for kt in range(CT):
                            last = exact(bank[4 + f % 2][:, 0:GT], (w_1[c][0][:, kt, cols], w_1[c][1][:, kt, cols]),
                                         (mid_hi[:, kt, :], mid_lo[:, kt, :]), kt == 0, kt == CT - 1)
                        last.then_inc(hid_full.sem, 1)
                    if f >= 2:
                        e = f - 2
                        if first and e % CT == 0:
                            pe.wait_ge(mlp_w_lo.sem, 2 * (e // CT) + 2)
                        pe.wait_ge(hid_lo_set.sem, hid_lo_set.at(g, e + 1))
                        for ct in range(CT):
                            if e == 0:
                                pe.wait_ge(out_ready.sem, out_ready.at(g, 0))
                            cols = slice(ct * P, (ct + 1) * P)
                            last = exact(bank[ct][:, 0:GT], (w_2[e // CT][0][:, e % CT, cols], w_2[e // CT][1][:, e % CT, cols]),
                                         (hid_hi[e % 4], hid_lo[e % 4]), e == 0, e == FT - 1)
                        last.then_inc(hid_used.sem, 1)
                    if not last_group and f == 3:
                        project_out(g + 1)
                    if not last_group and f == 7:
                        mean_square(g + 1)

            project_out(0)
            mean_square(0)
            mlp(0, True, False)
            with pe.Fori(1, GROUPS - 1) as g:
                mlp(g, False, False)
            mlp(GROUPS - 1, False, True)

        @block.scalar
        def _(act):
            af = nc.scalar.activation
            for dst, src in loads:
                act.dma_start(dst, src).then_inc(loaded.sem, 16)
            act.wait_ge(consts_set.sem, consts_set.per)

            def square_1(g):
                act.wait_ge(centred_ready.sem, centred_ready.at(g))
                af(scratch, xa, ACT.Square).then_inc(square_ready.sem, 1)

            def std_1(g):
                act.wait_ge(var_full.sem, var_full.at(g))
                af(std, bank[6][:, 0:GT], ACT.Sqrt, bias=eps[:, 0:1]).then_inc(std_ready.sem, 1)

            def affine_1(g):
                act.wait_ge(mixed_ready.sem, mixed_ready.at(g, 0))
                af(ext[:, :, :, 0], edge_sb, ACT.Copy).then_inc(ext_ready.sem, 1)
                act.wait_ge(normed.sem, normed.at(g))
                for ct in range(CT):
                    af(ext[:, ct, :, 1:LEN + 1], by_seq(xa[:, ct, :]), ACT.Identity,
                       bias=vcol("ln1_b", ct), scale=vcol("ln1_w", ct)).then_inc(ext_ready.sem, 1)

            def evict(g, name, dst, fn, ready):
                for ct in range(CT):
                    ps = ra.take(act, g, (name, ct))
                    af(dst[:, ct, :], ps[:, 0:GT], fn).then_inc(ready.sem, 1)

            def projections(g, first, last_group):
                ps = ra.take(act, g, "rank4")
                af(mix_t4_s[2], ps[:, 0:GT], ACT.Tanh).then_inc(mix_rank.sem, 1)
                ps = ra.take(act, g, "rank1")
                af(mix_t1_s[2], ps[0:MIXR, 0:GT], ACT.Tanh).then_inc(mix_rank.sem, 1)
                for n, t in enumerate((mix_t4_s, mix_t1_s)):
                    act.wait_ge(mix_rank.sem, mix_rank.at(g, n + 1))
                    af(t[0], t[2], ACT.Copy).then_inc(mix_t_hi.sem, 1)
                for n in range(MIX - 1):
                    if first:
                        await_weights(act, "kvrg", n)
                        af(w_kvrg_s[n][0], w_kvrg_s[n][2], ACT.Copy).then_inc(kvrg_hi.sem, 1)
                    act.wait_ge(mixed_ready.sem, mixed_ready.at(g, n + 1))
                    af(mixed_s[n][0], mixed_s[n][2], ACT.Copy).then_inc(mixed_hi.sem, 1)
                act.wait_ge(rec_stored.sem, 80 * g)
                evict(g, "k", k_sb, ACT.Copy, k_ready)
                if not last_group:
                    square_1(g + 1)
                evict(g, "v", v_sb, ACT.Copy, v_ready)
                ps = ra.take(act, g, "dec1")
                af(dec_t, ps[0:DECR, 0:GT], ACT.Tanh).then_inc(dec_rank.sem, 1)
                if not last_group:
                    std_1(g + 1)
                evict(g, "r", r_sb, ACT.Copy, r_ready)
                if not last_group:
                    affine_1(g + 1)
                for ct in range(CT):
                    ps = ra.take(act, g, ("dec2", ct))
                    af(mixed_w[:, ct, :], ps[:, 0:GT], ACT.Exp, bias=vcol("time_decay", ct)).then_inc(dec_exp.sem, 1)
                for ct in range(CT):
                    act.wait_ge(dec_exp.sem, dec_exp.at(g, ct + 1))
                    af(by_seq(w_sb[:, ct, :])[:, :, 1:LEN], by_seq(mixed_w[:, ct, :])[:, :, 0:LEN - 1],
                       ACT.Exp, scale=-1.0).then_inc(w_ready.sem, 1)
                evict(g, "g", g_sb, ACT.Silu, g_ready)

            square_1(0)
            std_1(0)
            act.wait_ge(loaded.sem, ALL_LOADED)
            affine_1(0)
            for w in (mix2a_s, mix2b_s):
                af(w[0], w[2], ACT.Copy).then_inc(mix2_hi.sem, 1)
            projections(0, True, False)
            with act.Fori(1, GROUPS - 1) as g:
                projections(g, False, False)
            projections(GROUPS - 1, False, True)

            act.wait_ge(g_ready.sem, g_ready.at(GROUPS - 1))
            af(pick_r, pick, ACT.Copy)

            def high_v(g, ct, used):
                act.wait_ge(tile_in[ct].sem, 32 * g + 32)
                act.wait_ge(vals_full.sem, used)
                af(v_hi2[ct % 2], rec_in[ct][:, 1, :], ACT.Copy).then_inc(v_hi_set.sem, 1)

            def recurrence(g, u, first, last):
                ct, q = divmod(u, QUADS)
                act.wait_ge(tile_in[ct].sem, 32 * g + 32)
                if u >= RING or not first:
                    act.wait_ge(summed.sem, summed.at(g, u - RING + 1))
                af(ring[u % RING].rearrange("p j (b l) -> p j b l", b=GB)[:, :, :, 0], s0_in[ct][:, q], ACT.Copy).then_inc(start_state.sem, 1)
                if q == 0 and ct < CT - 1:
                    high_v(g, ct + 1, vals_full.at(g, u))
                elif q == 0 and not last:
                    high_v(g + 1, 0, vals_full.at(g, u))

            high_v(0, 0, 0)
            for u in range(UNITS):
                recurrence(0, u, True, False)
            with act.Fori(1, GROUPS - 1) as g:
                for u in range(UNITS):
                    recurrence(g, u, False, False)
            for n in range(5):
                await_weights(act, "off", n)
                af(w_off_s[n][0], w_off_s[n][2], ACT.Copy).then_inc(off_hi.sem, 1)
            for u in range(UNITS):
                recurrence(GROUPS - 1, u, False, True)

            def split_h(i, p, used):
                act.wait_ge(h_in.sem, 64 * i + 32 * p + 32)
                act.wait_ge(kv_full.sem, used)
                af(h_hi[p], h_raw, ACT.Copy).then_inc(h_hi_set.sem, 1)

            act.wait_ge(y_ready.sem, CT * GROUPS)

            def channel_mixing(g, n):
                def square_y(ct):
                    act.wait_ge(y_centred.sem, y_centred.at(n, ct + 1))
                    af(squares[:, ct, :], y_s[2][:, ct, :], ACT.Square).then_inc(y_square.sem, 1)

                if n is not None:
                    for ct in (0, 1, 2):
                        square_y(ct)
                if g is not None:
                    for ct in range(CT):
                        ps = r2.take(act, g, ("fr", ct))
                        af(rr[:, ct, :], ps[:, 0:GT], ACT.Sigmoid).then_inc(rr_ready.sem, 1)
                if n is not None:
                    square_y(3)
                    ps = r1.take(act, n, "yvar")
                    af(std[0:RH, :], ps[0:RH, 0:GT], ACT.Sqrt, bias=eps[0:RH, 0:1], scale=1.0 / RS).then_inc(y_std.sem, 1)
                if g is not None:
                    for ct in range(CT + 1):
                        if ct < CT:
                            ps = r2.take(act, g, ("fk", ct))
                            af(kk_s[2][:, ct, :], ps[:, 0:GT], ACT.Relu).then_inc(relu_ready.sem, 1)
                        if ct > 0:
                            act.wait_ge(kk_ready.sem, kk_ready.at(g, ct))
                            af(kk_s[0][:, ct - 1, :], kk_s[2][:, ct - 1, :], ACT.Copy).then_inc(kk_hi_set.sem, 1)
                if n is None:
                    for m, w in enumerate((w_k, w_v)):
                        await_weights(act, "kv", m)
                        af(w[0], w[2], ACT.Copy).then_inc(kv_w_hi.sem, 1)
                    act.wait_ge(h_pads_set.sem, 1)
                    split_h(0, 0, 0)
                if n is not None:
                    for ct in range(CT):
                        act.wait_ge(y_gated.sem, y_gated.at(n, ct + 1))
                        af(y_s[0][:, ct, :], y_s[2][:, ct, :], ACT.Copy).then_inc(y_hi_set.sem, 1)
                if g is not None:
                    act.wait_ge(x3_ready.sem, x3_ready.at(g))
                    af(kk_s[0], x3_raw, ACT.Copy).then_inc(x3_hi_set.sem, 1)
                if n is not None:
                    act.wait_ge(centred3.sem, centred3.at(n))
                    af(squares, x_in3, ACT.Square).then_inc(square3.sem, 1)
                if g is not None:
                    act.wait_ge(q_stored.sem, 16 * g)
                    for ct in (0, 1):
                        ps = r2.take(act, g, ("q", ct))
                        af(q_out[:, ct, :], ps[:, 0:GT], ACT.Identity, bias=vcol("q_b", ct)).then_inc(q_ready.sem, 1)
                if n is not None:
                    ps = r1.take(act, n, "var2")
                    af(std, ps[:, 0:GT], ACT.Sqrt, bias=eps[:, 0:1]).then_inc(std3.sem, 1)
                if g is not None:
                    for ct in (2, 3):
                        ps = r2.take(act, g, ("q", ct))
                        af(q_out[:, ct, :], ps[:, 0:GT], ACT.Identity, bias=vcol("q_b", ct)).then_inc(q_ready.sem, 1)
                if n is not None:
                    act.wait_ge(xk_ready.sem, xk_ready.at(n, 0))
                    af(ext3[:, :, :, 0], edge3, ACT.Copy).then_inc(ext3_ready.sem, 1)
                    for ct in range(CT):
                        act.wait_ge(normed3.sem, normed3.at(n, ct + 1))
                        af(ext3[:, ct, :, 1:LEN + 1], by_seq(x_in3[:, ct, :]), ACT.Identity,
                           bias=vcol("ln2_b", ct), scale=vcol("ln2_w", ct)).then_inc(ext3_ready.sem, 1)
                    for m, (x_s, ready) in enumerate(((xr_s, xr_ready), (xk_s, xk_ready))):
                        for ct in range(CT):
                            act.wait_ge(ready.sem, ready.at(n, ct + 1))
                            af(x_s[0][:, ct, :], x_s[2][:, ct, :], ACT.Copy).then_inc(xrk_hi.sem, 1)

            channel_mixing(None, 0)
            with act.Fori(0, GROUPS - 1) as g:
                channel_mixing(g, g + 1)
            channel_mixing(GROUPS - 1, None)

            def split_q(i, p, used):
                act.wait_ge(q_in[p].sem, 64 * i + 64)
                act.wait_ge(s_full.sem, used)
                af(q_stack[p], q_raw, ACT.Copy).then_inc(q_hi_set.sem, 1)

            def high_values(i, p, c, used):
                act.wait_ge(kv_full.sem, kv_full.at(i, p * 8 + 2 * c + 2))
                act.wait_ge(pv_done.sem, used)
                af(v_all[p][0:KT_W, c, :, 0, :], bank[7][0:KT_W, :].rearrange("p (h d) -> p h d", h=AH), ACT.Copy).then_inc(v_hi_ready.sem, 1)

            def high_keys(i, p, ct, heads_k, used):
                act.wait_ge(kv_full.sem, kv_full.at(i, p * 8 + 2 * ct + 1))
                act.wait_ge(s_full.sem, used)
                for a in heads_k:
                    h, rows_a = 4 * ct + a, slice(AD * a, AD * a + AD)
                    bias = vcol("k_b", ct)[rows_a]
                    done = af(k_stack[0:AD, h, :], bank[6][rows_a, 0:KPAD], ACT.Identity, bias=bias)
                    if a % 2 == 0:
                        done = af(k_stack[AD:2 * AD, h, :], bank[6][rows_a, 0:KPAD], ACT.Identity, bias=bias)
                    done.then_inc(k_hi_ready.sem, 1)

            def attend(i, t, first, last):
                p, h = divmod(t, AH)
                if h == 0 and t < PAIR and (p > 0 or not first):
                    high_keys(i, p, 3, (3,), s_full.at(i, p * AH))
                elif h % 4 == 0 and h > 0 and t < PAIR and (p == 0 or not last):
                    high_keys(i + p, 1 - p, h // 4 - 1, (3,), s_full.at(i, t))
                x = t - HI_LAG
                if runs(x, first):
                    act.wait_ge(t_full.sem, t_full.at(i, x + 1))
                    if x >= 4 or not first:
                        act.wait_ge(pv_done.sem, pv_done.at(i, x - 3))
                    af(pT_hi[x % 4][0:KT_W, :, :], bank[2 + x % 2][0:KT_W, 0:KT_N * LEN].rearrange("p (k n) -> p k n", k=KT_N), ACT.Copy).then_inc(pT_hi_set.sem, 1)
                x = t - 1
                if runs(x, first):
                    b, h_x = divmod(x, AH)
                    act.wait_ge(s_masked.sem, s_masked.at(i, x + 1))
                    af(probs[x % 4][0:LEN, 0:KEYS], probs[x % 4][0:LEN, 0:KEYS], ACT.Exp, bias=row_max[0:LEN, h_x:h_x + 1], scale=-1.0,
                       accum_out=row_sum[b % 2][0:LEN, h_x:h_x + 1]).then_inc(p_ready.sem, 1)
                if h == 1 and t < PAIR and (p > 0 or not first):
                    high_values(i, p, 3, 0)
                elif t < PAIR and (p == 0 or not last):
                    if h % 4 >= 2:
                        some = (0,) if h % 4 == 2 else (1, 2)
                        high_keys(i + p, 1 - p, h // 4, some, s_full.at(i, p * AH + h // 4 * 4 + some[-1] + 1))
                    elif h % 4 == 1 and h > 1:
                        high_values(i + p, 1 - p, h // 4 - 1, pv_done.at(i, p * AH))
                if h == 9 and not last:
                    split_h(i + 1, p, kv_full.at(i, p * 8 + 8))
                if h == 7 and t < PAIR and (p == 0 or not last):
                    split_q(i + p, 1 - p, s_full.at(i, p * AH))
                if h == 6 and runs((p - 1) * AH, first):
                    act.wait_ge(oT_full.sem, oT_full.at(i, p))
                    if p > 1 or not first:
                        act.wait_ge(o_stored.sem, 32 * i + 16 * (p - 1))
                    for ct in range(CT):
                        done = af(o_T[:, ct, :], bank[4][:, ct * LEN:(ct + 1) * LEN], ACT.Identity, bias=vcol("v_b", ct))
                    done.then_inc(oT_ready.sem, 1)

            act.wait_ge(x3_stored.sem, 16 * GROUPS)
            act.wait_ge(q_stored.sem, 16 * GROUPS)
            act.wait_ge(pads_set.sem, pads_set.per)
            for c in range(CT):
                high_keys(0, 0, c, (0, 1, 2, 3), 0)
                if c == 1:
                    split_q(0, 0, 0)
                if c == 2:
                    split_h(0, 1, 0)
                high_values(0, 0, c, 0)
            for t in range(PAIR):
                attend(0, t, True, False)
            with act.Fori(1, PAIRS - 1) as i:
                for t in range(PAIR):
                    attend(i, t, False, False)
            for t in range(PAIR + DRAIN):
                attend(PAIRS - 1, t, False, True)


            def norm_c(g):
                act.wait_ge(resid_ready.sem, resid_ready.at(g))
                af(square_c, mid, ACT.Square).then_inc(sq_ready.sem, 1)

            def root_c(g):
                ps = rf.take(act, g, "ms")
                af(std, ps[:, 0:GT], ACT.Sqrt, bias=eps[:, 1:2]).then_inc(cstd_ready.sem, 1)

            def high_w(n):
                w = mlp_w[n]
                await_weights(act, "mlp", n)
                af(w[0], w[2], ACT.Copy).then_inc(mlp_w_hi.sem, 1)

            def high_mid(g):
                act.wait_ge(mid_ready.sem, mid_ready.at(g))
                act.wait_ge(hid_full.sem, hid_full.at(g, 0))
                af(mid_hi, mid, ACT.Copy).then_inc(mid_hi_set.sem, 1)

            def mlp(g, first, last_group):
                for f in range(FT):
                    if first and f % CT == 0:
                        for n in (f // CT * 2, f // CT * 2 + 1):
                            if n >= EARLY_W:
                                high_w(n)
                    act.wait_ge(hid_full.sem, hid_full.at(g, f + 1))
                    act.wait_ge(hid_lo_set.sem, hid_lo_set.at(g, max(f - 3, 0)))
                    af(hid[f % 4], bank[4 + f % 2][:, 0:GT], ACT.Gelu_apprx_tanh, bias=bias1(f)).then_inc(hid_ready.sem, 1)
                    if not last_group and f == 4:
                        norm_c(g + 1)
                    if not last_group and f == 8:
                        root_c(g + 1)
                if not last_group:
                    high_mid(g + 1)

            for n in range(EARLY_W):
                high_w(n)
            norm_c(0)
            root_c(0)
            act.wait_ge(o_stored.sem, 16 * SEQS)
            high_mid(0)
            mlp(0, True, False)
            with act.Fori(1, GROUPS - 1) as g:
                mlp(g, False, False)
            mlp(GROUPS - 1, False, True)

        @block.gpsimd
        def _(pool):
            tt = nc.gpsimd.tensor_tensor
            with pool.Fori(0, GROUPS) as g:
                for n in range(MIX):
                    pool.wait_ge(mix_scaled.sem, mix_scaled.at(g, (n + 1) * CT))
                    m = (mixed_s[n][2] if n < MIX - 1 else mixed_w).rearrange("p c (b l) -> p c b l", b=GB)
                    tt(m, m, ext[:, :, :, 1:LEN + 1], ALU.add).then_inc(mixed_ready.sem, 1)

            def low_v(g, ct):
                pool.wait_ge(v_hi_set.sem, v_hi_set.at(g, ct + 1))
                tt(v_lo2[ct % 2], rec_in[ct][:, 1, :], v_hi2[ct % 2].bitcast(F32), ALU.subtract).then_inc(v_lo_set.sem, 1)

            def recurrence(g, last):
                for u in range(UNITS):
                    ct, q = divmod(u, QUADS)
                    if q == 0 and ct < CT - 1:
                        low_v(g, ct + 1)
                    elif q == 0 and not last:
                        low_v(g + 1, 0)
                    pool.wait_ge(scanned.sem, scanned.at(g, u + 1))
                    tt(ring[u % RING], ring[u % RING], spread(rec_in[ct][:, 2, :], 1, 4), ALU.mult).then_inc(weighed.sem, 1)

            low_v(0, 0)
            with pool.Fori(0, GROUPS - 1) as g:
                recurrence(g, False)
            recurrence(GROUPS - 1, True)

            with pool.Fori(0, GROUPS) as g:
                for ct in range(CT):
                    pool.wait_ge(relu_ready.sem, relu_ready.at(g, ct + 1))
                    tt(kk_s[2][:, ct, :], kk_s[2][:, ct, :], kk_s[2][:, ct, :], ALU.mult).then_inc(kk_ready.sem, 1)

            def split_h(i, p, before):
                pool.wait_ge(h_hi_set.sem, h_hi_set.at(i, p + 1))
                pool.wait_ge(q_lo_set.sem, before)
                tt(h_lo[p], h_raw, h_hi[p].bitcast(F32), ALU.subtract).then_inc(h_lo_set.sem, 1)

            def split_q(i, p, before):
                pool.wait_ge(q_hi_set.sem, q_hi_set.at(i, p + 1))
                pool.wait_ge(h_lo_set.sem, before)
                tt(q_stack[p][AD:2 * AD], q_raw[AD:2 * AD], q_stack[p][AD:2 * AD].bitcast(F32), ALU.subtract).then_inc(q_lo_set.sem, 1)

            def attend(i, p, last_seq, last_pair):
                if not last_pair:
                    split_h(i + 1, p, q_lo_set.at(i, p + 1))
                if not last_seq:
                    split_q(i + p, 1 - p, SEQS if last_pair else h_lo_set.at(i, p + 3))

            split_h(0, 0, 0)
            split_q(0, 0, 1)
            split_h(0, 1, 1)
            with pool.Fori(0, PAIRS - 1) as i:
                attend(i, 0, False, False)
                attend(i, 1, False, False)
            attend(PAIRS - 1, 0, False, True)

            pool.wait_ge(q_lo_set.sem, SEQS)
            with pool.Fori(0, GROUPS) as g:
                for f in range(FT):
                    pool.wait_ge(hid_ready.sem, hid_ready.at(g, f + 1))
                    pool.wait_ge(hid_used.sem, hid_used.at(g, max(f - 3, 0)))
                    tt(hid_hi[f % 4], hid[f % 4], one.broadcast_to([P, GT]), ALU.mult).then_inc(hid_hi_set.sem, 1)

        @block.vector
        def _(dve):
            v = nc.vector
            v.memset(mean_ones[:, :], 1.0 / C).then_inc(consts_set.sem, 1)
            v.memset(eps[:, 0:1], LN_EPS).then_inc(consts_set.sem, 1)
            v.memset(eps[:, 1:2], RMS_EPS).then_inc(consts_set.sem, 1)
            v.memset(one, 1.0).then_inc(consts_set.sem, 1)
            v.memset(rec_out[:, 3], 0.0).then_inc(consts_set.sem, 1)

            def token_shift(dst, src, done):
                v.tensor_tensor(dst.rearrange("p c (b l) -> p c b l", b=GB), src[:, :, :, 0:LEN], src[:, :, :, 1:LEN + 1], ALU.subtract).then_inc(done.sem, 1)

            def mix_in(dst, moved, src, w, done):
                for ct in range(CT):
                    v.scalar_tensor_tensor(by_seq(dst[:, ct, :]), by_seq(moved[:, ct, :]), vcol(w, ct), src[:, ct, :, 1:LEN + 1],
                                           ALU.mult, ALU.add).then_inc(done.sem, 1)

            def centre_1(g):
                dve.wait_ge(mean_full.sem, mean_full.at(g))
                v.tensor_tensor(xa, xa, spread(bank[7][:, 0:GT], 1, CT), ALU.subtract).then_inc(centred_ready.sem, 1)

            def norm_1(g):
                dve.wait_ge(std_ready.sem, std_ready.at(g))
                v.reciprocal(rstd, std).then_inc(rstd_ready.sem, 1)
                dve.wait_ge(rstd_ready.sem, rstd_ready.at(g))
                v.tensor_tensor(xa, xa, spread(rstd, 1, CT), ALU.mult).then_inc(normed.sem, 1)
                dve.wait_ge(ext_ready.sem, ext_ready.at(g))
                token_shift(shift, ext, shift_ready)
                dve.wait_ge(shift_ready.sem, shift_ready.at(g))
                mix_in(scratch, shift, ext, "maa_x", mixx_ready)

            def low_mixed(g, n):
                dve.wait_ge(mixed_hi.sem, mixed_hi.at(g, n + 1))
                v.tensor_tensor(mixed_s[n][1], mixed_s[n][2], mixed_s[n][0].bitcast(F32), ALU.subtract).then_inc(mixed_lo.sem, 1)

            def projections(g, first, last_group):
                for n, t in enumerate((mix_t4_s, mix_t1_s)):
                    dve.wait_ge(mix_t_hi.sem, mix_t_hi.at(g, n + 1))
                    v.tensor_tensor(t[1], t[2], t[0].bitcast(F32), ALU.subtract).then_inc(mix_t_lo.sem, 1)
                for n, j in enumerate(MIX_ORDER):
                    dst = mixed_s[n][2] if n < MIX - 1 else mixed_w
                    if n == MIX - 1:
                        dve.wait_ge(w_ready.sem, w_ready.at(g, 0))
                    for ct in range(CT):
                        ps = ra.take(dve, g, ("mix", j, ct))
                        v.scalar_tensor_tensor(dst[:, ct, :], ps[:, 0:GT], vcol(VECS[5 + j], ct), shift[:, ct, :],
                                               ALU.add, ALU.mult).then_inc(mix_scaled.sem, 1)
                    if first and n < MIX - 1:
                        w = w_kvrg_s[n]
                        dve.wait_ge(kvrg_hi.sem, n + 1)
                        v.tensor_tensor(w[1], w[2], w[0].bitcast(F32), ALU.subtract).then_inc(kvrg_lo.sem, 1)
                    if n >= 2:
                        low_mixed(g, n - 2)
                low_mixed(g, 3)
                if not last_group:
                    centre_1(g + 1)
                    norm_1(g + 1)

            centre_1(0)
            dve.wait_ge(loaded.sem, ALL_LOADED)
            norm_1(0)
            for n, w in enumerate((mix2a_s, mix2b_s)):
                dve.wait_ge(mix2_hi.sem, n + 1)
                v.tensor_tensor(w[1], w[2], w[0].bitcast(F32), ALU.subtract).then_inc(mix2_lo.sem, 1)
            projections(0, True, False)
            with dve.Fori(1, GROUPS - 1) as g:
                projections(g, False, False)
            projections(GROUPS - 1, False, True)

            dve.wait_ge(g_ready.sem, g_ready.at(GROUPS - 1))

            def recurrence(g, u, first):
                ct, q = divmod(u, QUADS)
                if u < UNITS:
                    k, vals, r, w = (rec_in[ct][:, n, :] for n in range(4))
                    if q == 0:
                        dve.wait_ge(tile_in[ct].sem, 32 * g + 32)
                        if ct >= 2 or not first:
                            dve.wait_ge(bonus_full.sem, bonus_full.at(g, ct - 1))
                        v.scalar_tensor_tensor(rk2[:, ct % 2, :], r, vcol("faaaa", ct), k, ALU.mult, ALU.mult).then_inc(rk_ready.sem, 1)
                    states = ring[u % RING].rearrange("p j (b l) -> p j b l", b=GB)
                    dve.wait_ge(vals_full.sem, vals_full.at(g, u + 1))
                    if u >= RING or not first:
                        dve.wait_ge(summed.sem, summed.at(g, u - RING + 1))
                    v.tensor_tensor(states[:, :, :, 1:LEN], spread(by_seq(k)[:, :, 0:LEN - 1], 1, 4),
                                    ps_v.rearrange("p j (b l) -> p j b l", b=GB)[:, :, :, 0:LEN - 1], ALU.mult).then_inc(outer_ready.sem, 1)
                    dve.wait_ge(outer_ready.sem, outer_ready.at(g, u + 1))
                    dve.wait_ge(start_state.sem, start_state.at(g, u + 1))
                    for i in range(4):
                        row = ring[u % RING][:, i, :]
                        last = v.tensor_tensor_scan(row, w, row, 0.0, ALU.mult, ALU.add)
                    last.then_inc(scanned.sem, 1)
                    if q == 2:
                        dve.wait_ge(bonus_full.sem, bonus_full.at(g, ct + 1))
                        v.tensor_tensor(bonus2[:, ct % 2, :], bank[6 + ct % 2][:, 0:GT], vals, ALU.mult).then_inc(bonus_ready.sem, 1)
                c = ct - 1
                if q == 3 and (c >= 0 or not first):
                    dve.wait_ge(summed.sem, summed.at(g, ct * QUADS))
                    dve.wait_ge(bonus_ready.sem, bonus_ready.at(g, ct))
                    if c >= 2 or not first:
                        dve.wait_ge(y_stored[c % 2].sem, 32 * g + 16 * (c // 2))
                    v.tensor_tensor(y_out[:, c % 2, :], bank[4 + c % 2][:, 0:GT], bonus2[:, c % 2, :], ALU.add).then_inc(y_ready.sem, 1)

            for u in range(UNITS):
                recurrence(0, u, True)
            with dve.Fori(1, GROUPS - 1) as g:
                for u in range(UNITS):
                    recurrence(g, u, False)
            for u in range(UNITS + REC_DRAIN):
                recurrence(GROUPS - 1, u, False)


            def low_off(n):
                w = w_off_s[n]
                dve.wait_ge(off_hi.sem, n + 1)
                v.tensor_tensor(w[1], w[2], w[0].bitcast(F32), ALU.subtract).then_inc(off_lo.sem, 1)

            def channel_mixing(g, n):
                if n is not None:
                    for ct in range(CT):
                        ps = r1.take(dve, n, ("ymean", ct))
                        v.scalar_tensor_tensor(y_s[2][:, ct, :], ps[:, 0:GT], -1.0 / RS, y_s[2][:, ct, :], ALU.mult, ALU.add).then_inc(y_centred.sem, 1)
                    if g is None:
                        low_off(0)
                    dve.wait_ge(y_std.sem, y_std.at(n))
                    v.reciprocal(rstd[0:RH, :], std[0:RH, :]).then_inc(y_rstd.sem, 1)
                    if g is None:
                        low_off(1)
                if g is not None:
                    for ct in range(CT):
                        dve.wait_ge(kk_hi_set.sem, kk_hi_set.at(g, ct + 1))
                        v.tensor_tensor(kk_s[1][:, ct, :], kk_s[2][:, ct, :], kk_s[0][:, ct, :].bitcast(F32), ALU.subtract).then_inc(kk_lo_set.sem, 1)
                if n is None:
                    v.memset(h_raw[:, :, KEYS:KPAD], 0.0).then_inc(h_pads_set.sem, 1)
                    for m, w in enumerate((w_k, w_v)):
                        dve.wait_ge(kv_w_hi.sem, m + 1)
                        v.tensor_tensor(w[1], w[2], w[0].bitcast(F32), ALU.subtract).then_inc(kv_w_lo.sem, 1)
                if n is not None:
                    for ct in range(CT):
                        ps = r1.take(dve, n, ("yback", ct))
                        v.scalar_tensor_tensor(y_s[2][:, ct, :], ps[:, 0:GT], vcol("gn_w", ct), y_s[2][:, ct, :], ALU.mult, ALU.mult).then_inc(y_scaled.sem, 1)
                    dve.wait_ge(x3_in.sem, 48 * n + 48)
                    for ct in range(CT):
                        dve.wait_ge(y_scaled.sem, y_scaled.at(n, ct + 1))
                        v.scalar_tensor_tensor(y_s[2][:, ct, :], y_s[2][:, ct, :], vcol("gn_b", ct), gate[:, ct, :], ALU.add, ALU.mult).then_inc(y_gated.sem, 1)
                    for ct in range(CT):
                        dve.wait_ge(y_hi_set.sem, y_hi_set.at(n, ct + 1))
                        v.tensor_tensor(y_s[1][:, ct, :], y_s[2][:, ct, :], y_s[0][:, ct, :].bitcast(F32), ALU.subtract).then_inc(y_lo_set.sem, 1)
                    if g is None:
                        low_off(2)
                if g is not None:
                    for ct in range(CT):
                        ps = r2.take(dve, g, ("fv", ct))
                        dve.wait_ge(rr_ready.sem, rr_ready.at(g, ct + 1))
                        v.tensor_tensor(rr[:, ct, :], ps[:, 0:GT], rr[:, ct, :], ALU.mult).then_inc(ff_ready.sem, 1)
                    dve.wait_ge(x3_stored.sem, 16 * g)
                    for ct in range(CT):
                        dve.wait_ge(ff_ready.sem, ff_ready.at(g, ct + 1))
                        v.tensor_tensor(x3_raw[:, ct, :], x2[:, ct, :], rr[:, ct, :], ALU.add).then_inc(x3_ready.sem, 1)
                    dve.wait_ge(x3_hi_set.sem, x3_hi_set.at(g))
                    v.tensor_tensor(kk_s[1], x3_raw, kk_s[0].bitcast(F32), ALU.subtract).then_inc(x3_lo_set.sem, 1)
                if n is not None:
                    for ct in range(CT):
                        ps = r1.take(dve, n, ("o", ct))
                        v.tensor_tensor(x2[:, ct, :], ps[:, 0:GT], x_in3[:, ct, :], ALU.add).then_inc(x2_ready.sem, 1)
                    dve.wait_ge(x2_ready.sem, x2_ready.at(n))
                    ps = r1.take(dve, n, "mean2")
                    v.tensor_tensor(x_in3, x2, spread(ps[:, 0:GT], 1, CT), ALU.subtract).then_inc(centred3.sem, 1)
                    if g is None:
                        low_off(3)
                        low_off(4)
                    dve.wait_ge(std3.sem, std3.at(n))
                    v.reciprocal(rstd, std).then_inc(rstd3.sem, 1)
                    dve.wait_ge(rstd3.sem, rstd3.at(n))
                    for ct in range(CT):
                        v.tensor_tensor(x_in3[:, ct, :], x_in3[:, ct, :], rstd, ALU.mult).then_inc(normed3.sem, 1)

                    def mix3(x_s, ct, w, done):
                        v.scalar_tensor_tensor(by_seq(x_s[2][:, ct, :]), by_seq(shift3[:, ct, :]), vcol(w, ct), ext3[:, ct, :, 1:LEN + 1],
                                               ALU.mult, ALU.add).then_inc(done.sem, 1)

                    def low3(x_s, m, ct):
                        dve.wait_ge(xrk_hi.sem, xrk_hi.at(n, m * CT + ct + 1))
                        v.tensor_tensor(x_s[1][:, ct, :], x_s[2][:, ct, :], x_s[0][:, ct, :].bitcast(F32), ALU.subtract).then_inc(xrk_lo.sem, 1)

                    if g is None:
                        for p in range(2):
                            dve.wait_ge(y_stored[p].sem, 16 * CT // 2 * GROUPS)
                    for ct in range(CT):
                        dve.wait_ge(ext3_ready.sem, ext3_ready.at(n, ct + 2))
                        v.tensor_tensor(by_seq(shift3[:, ct, :]), ext3[:, ct, :, 0:LEN], ext3[:, ct, :, 1:LEN + 1], ALU.subtract).then_inc(shift3_ready.sem, 1)
                        dve.wait_ge(shift3_ready.sem, shift3_ready.at(n, ct + 1))
                        mix3(xr_s, ct, "fmaa_r", xr_ready)
                    for ct in range(CT):
                        low3(xr_s, 0, ct)
                    for ct in range(CT):
                        mix3(xk_s, ct, "fmaa_k", xk_ready)
                    for ct in range(CT):
                        low3(xk_s, 1, ct)

            channel_mixing(None, 0)
            with dve.Fori(0, GROUPS - 1) as g:
                channel_mixing(g, g + 1)
            channel_mixing(GROUPS - 1, None)

            dve.wait_ge(x3_stored.sem, 16 * GROUPS)
            dve.wait_ge(q_stored.sem, 16 * GROUPS)
            for p in range(2):
                v.memset(mask_f[p][:, CTX:KPAD], 0.0).then_inc(pads_set.sem, 1)
            for t in range(4):
                v.memset(probs[t][:, KEYS:KPAD], 0.0).then_inc(pads_set.sem, 1)
            dve.wait_ge(pads_set.sem, pads_set.per)

            def low_values(i, p, c):
                dve.wait_ge(v_hi_ready.sem, v_hi_ready.at(i, p * KT_N + c + 1))
                v.tensor_tensor(v_all[p][0:KT_W, c, :, 1, :], bank[7][0:KT_W, :].rearrange("p (h d) -> p h d", h=AH),
                                v_all[p][0:KT_W, c, :, 0, :].bitcast(F32), ALU.subtract).then_inc(v_done.sem, 1)

            def low_keys(i, p, ct, heads_k):
                for a in heads_k:
                    h, rows_a = 4 * ct + a, slice(AD * a, AD * a + AD)
                    dve.wait_ge(k_hi_ready.sem, k_hi_ready.at(i, p * AH + h + 1))
                    if a % 2 == 1:
                        v.tensor_copy(k_stack[AD:2 * AD, h, :], k_stack[0:AD, h, :].bitcast(F32))
                    v.scalar_tensor_tensor(k_stack[2 * AD:3 * AD, h, :], bank[6][rows_a, 0:KPAD], k_bias(h), k_stack[0:AD, h, :].bitcast(F32),
                                           ALU.add, ALU.subtract).then_inc(k_done.sem, 1)

            for c in range(CT):
                low_keys(0, 0, c, (0, 1, 2, 3))
                low_values(0, 0, c)

            def mask_scores(i, p):
                dve.wait_ge(q_in[p].sem, 64 * i + 64)
                v.tensor_scalar(mask_f[p][0:LEN, 0:CTX], mask_i[p][0:LEN, :], 0.0, MASKED, ALU.is_equal, ALU.mult).then_inc(mask_ready.sem, 1)

            def attend(i, t, first, last):
                p, h = divmod(t, AH)
                if h == 0 and t < PAIR and (p > 0 or not first):
                    low_keys(i, p, 3, (3,))
                elif h % 4 == 0 and h > 0 and t < PAIR and (p == 0 or not last):
                    low_keys(i + p, 1 - p, h // 4 - 1, (3,))
                if t < PAIR:
                    dve.wait_ge(s_full.sem, s_full.at(i, t + 1))
                    if t >= 4 or not first:
                        dve.wait_ge(t_full.sem, t_full.at(i, t - 3))
                    if h == 0:
                        dve.wait_ge(mask_ready.sem, mask_ready.at(i, p + 1))
                    v.tensor_copy(tick[:, t:t + 1], eps[0:1, 0:1])
                    v.tensor_tensor_reduce(out=probs[t % 4][0:LEN, 0:KEYS], in0=bank[t % 2][0:LEN, 0:KEYS], in1=mask_f[p][0:LEN, 0:KEYS],
                                           scale=-1.0 / AD, scalar=3.0e38, op0=ALU.add, op1=ALU.min,
                                           accum_out=row_max[0:LEN, h:h + 1]).then_inc(s_masked.sem, 1)
                if h == 12 and t < PAIR:
                    if p > 0 or not first:
                        dve.wait_ge(oT_full.sem, oT_full.at(i, p))
                    dve.wait_ge(pv_done.sem, pv_done.at(i, t - PV_LAG))
                    sum_heads(0, i, p * 2 + 1)
                if h == 4 and runs((p - 1) * AH, first):
                    dve.wait_ge(pv_done.sem, pv_done.at(i, p * AH))
                    sum_heads(1, i, p * 2)
                    dve.wait_ge(o_summed.sem, o_summed.at(i, p * 2))
                    dve.wait_ge(inv_ready.sem, inv_ready.at(i, p))
                    heads_o = o_tok[0:LEN, :].rearrange("p (h d) -> p h d", h=AH)
                    v.tensor_tensor(heads_o, heads_o, spread(row_inv[0:LEN, :], 2, AD), ALU.mult).then_inc(o_ready.sem, 1)
                x = t - LO_LAG
                if runs(x, first):
                    dve.wait_ge(pT_hi_set.sem, pT_hi_set.at(i, x + 1))
                    v.tensor_tensor(pT_lo[x % 4][0:KT_W, :, :], bank[2 + x % 2][0:KT_W, 0:KT_N * LEN].rearrange("p (k n) -> p k n", k=KT_N),
                                    pT_hi[x % 4][0:KT_W, :, :].bitcast(F32), ALU.subtract).then_inc(pT_ready.sem, 1)
                if h == 1 and t < PAIR and (p > 0 or not first):
                    low_values(i, p, 3)
                elif t < PAIR and (p == 0 or not last):
                    if h % 4 >= 2:
                        low_keys(i + p, 1 - p, h // 4, (0,) if h % 4 == 2 else (1, 2))
                    elif h % 4 == 1 and h > 1:
                        low_values(i + p, 1 - p, h // 4 - 1)
                if h == 12 and t < PAIR and (p == 0 or not last):
                    mask_scores(i + p, 1 - p)
                if h == 2 and runs((p - 1) * AH, first):
                    dve.wait_ge(p_ready.sem, p_ready.at(i, p * AH))
                    v.reciprocal(row_inv[0:LEN, :], row_sum[(p - 1) % 2][0:LEN, :]).then_inc(inv_ready.sem, 1)

            def sum_heads(half, i, k):
                parts = bank[5 - half][0:LEN, :].rearrange("p (h s d) -> p h s d", h=AH // 2, s=2)
                dst = o_tok[0:LEN, half * C // 2:(half + 1) * C // 2].rearrange("p (h d) -> p h d", h=AH // 2)
                v.tensor_copy(dst, parts[:, :, 0, :]).then_inc(o_copied.sem, 1)
                dve.wait_ge(o_copied.sem, o_copied.at(i, k))
                v.tensor_tensor(dst, dst, parts[:, :, 1, :], ALU.add).then_inc(o_summed.sem, 1)

            mask_scores(0, 0)
            for t in range(PAIR):
                attend(0, t, True, False)
            with dve.Fori(1, PAIRS - 1) as i:
                for t in range(PAIR):
                    attend(i, t, False, False)
            for t in range(PAIR + DRAIN):
                attend(PAIRS - 1, t, False, True)

            def low_w(n):
                dve.wait_ge(mlp_w_hi.sem, n + 1)
                v.tensor_tensor(mlp_w[n][1], mlp_w[n][2], mlp_w[n][0].bitcast(F32), ALU.subtract).then_inc(mlp_w_lo.sem, 1)

            def residual(g):
                dve.wait_ge(attn_in.sem, 32 * g + 32)
                for ct in range(CT):
                    ps = rf.take(dve, g, ("o", ct))
                    v.scalar_tensor_tensor(mid[:, ct, :], ps[:, 0:GT], vcol("out_b", ct), res_in[:, ct, :], ALU.add, ALU.add).then_inc(resid_ready.sem, 1)

            def norm_c(g):
                dve.wait_ge(cstd_ready.sem, cstd_ready.at(g))
                v.reciprocal(rstd, std).then_inc(crstd_ready.sem, 1)
                dve.wait_ge(crstd_ready.sem, crstd_ready.at(g))
                for ct in range(CT):
                    v.scalar_tensor_tensor(mid[:, ct, :], mid[:, ct, :], vcol("postnorm_w", ct), rstd, ALU.mult, ALU.mult).then_inc(mid_ready.sem, 1)

            def low_mid(g):
                dve.wait_ge(mid_hi_set.sem, mid_hi_set.at(g))
                v.tensor_tensor(mid_lo, mid, mid_hi.bitcast(F32), ALU.subtract).then_inc(mid_lo_set.sem, 1)

            def mlp(g, first, last_group):
                for f in range(FT):
                    if first and f % CT == 0:
                        for n in (f // CT * 2, f // CT * 2 + 1):
                            if n >= EARLY_W:
                                low_w(n)
                    dve.wait_ge(hid_hi_set.sem, hid_hi_set.at(g, f + 1))
                    v.tensor_tensor(hid_lo[f % 4], hid[f % 4], hid_hi[f % 4].bitcast(F32), ALU.subtract).then_inc(hid_lo_set.sem, 1)
                    if not last_group and f == 3:
                        residual(g + 1)
                    if not last_group and f == 8:
                        norm_c(g + 1)
                if not last_group:
                    low_mid(g + 1)
                dve.wait_ge(hid_used.sem, hid_used.at(g))
                dve.wait_ge(out_in.sem, 16 * g + 16)
                for ct in range(CT):
                    v.scalar_tensor_tensor(res_out[:, ct, :], bank[ct][:, 0:GT], vcol("mlp_b2", ct), res_out[:, ct, :], ALU.add, ALU.add).then_inc(out_ready.sem, 1)

            low_w(0)
            residual(0)
            for n in range(1, EARLY_W):
                low_w(n)
            norm_c(0)
            dve.wait_ge(o_stored.sem, 16 * SEQS)
            low_mid(0)
            mlp(0, True, False)
            with dve.Fori(1, GROUPS - 1) as g:
                mlp(g, False, False)
            mlp(GROUPS - 1, False, True)


def head_constants():
    row = np.arange(P)
    head, chan = row % HPT, row // HPT
    same = (head[:, None] == head[None, :]).astype(np.float32)
    pick = (same[:, None, :] * (chan[:, None, None] % 4 == np.arange(4)[None, :, None])).astype(np.float32)
    window = np.zeros((P, 2 * P - HPT), np.float32)
    window[row, P - HPT + head] = 1
    heads = np.concatenate([np.eye(P, dtype=np.float32), same, pick.reshape(P, -1), window], 1)
    heads_sum = np.zeros((P, CT, RH), np.float32)
    for ct in range(CT):
        heads_sum[row, ct, ct * HPT + head] = 1
    heads_back = np.ascontiguousarray(heads_sum.transpose(2, 1, 0))
    return heads, heads_sum, heads_back


def kernel(**inputs):
    import concourse.bacc as bacc
    from concourse.bass_utils import run_bass_kernel_spmd

    a = {k: np.asarray(v) for k, v in inputs.items()}
    l0 = {k[len("L0_xattn_"):]: v for k, v in a.items() if k.startswith("L0_")}
    l1 = {k[len("L1_xattn_"):]: v for k, v in a.items() if k.startswith("L1_")}

    def channels(x):
        return x.transpose(2, 0, 1).reshape(CT, P, -1)

    def tiles(x):
        return x.reshape(-1, P).T

    ctx = a["ctx_2048"]
    kv_w = l1["kv_w"].reshape(C, C, 2)
    kv_b = l1["kv_b"].reshape(C, 2)

    def by_row(x, axis):
        x = np.moveaxis(x, axis, 0)
        x = x.reshape(CT, HPT, RS, -1).transpose(0, 2, 1, 3).reshape(x.shape)
        return np.moveaxis(x, 0, axis)

    named = {**l0, **l1, "k_b": kv_b[:, 0], "v_b": kv_b[:, 1], "faaaa": l0["faaaa"].reshape(C)}
    for n in ("time_decay", "faaaa", "gn_w", "gn_b"):
        named[n] = by_row(named[n], 0)
    heads, heads_sum, heads_back = head_constants()
    s0 = ctx[:, 2:2 + RS].reshape(GROUPS, GB, CT, HPT, RS, 4, 4).transpose(0, 4, 3, 2, 6, 5, 1).reshape(GROUPS, P, CT, QUADS, 4, GB)
    edge = ctx[:, 0:2].reshape(GROUPS, GB, 2, CT, P).transpose(0, 4, 2, 3, 1)
    arrays = {
        "xT": channels(a["x"]), "ctxT": ctx.transpose(0, 2, 1).reshape(SEQS, CT, P, CTX), "mask": a["mask_BxS2_ik0"],
        "edgeT": edge, "s0T": s0,
        "vecs": np.concatenate([tiles(named[n]) for n in VECS] + [tiles(l1["mlp_b1"]), np.tile(kv_b[:, 0].reshape(AH, AD).T, (P // AD, 1))], 1),
        "w_mix1": l0["maa_w1"], "w_mix2": l0["maa_w2"].reshape(MIX * MIXR, C),
        "w_dec1": l0["decay_w1"], "w_dec2": by_row(l0["decay_w2"], 1),
        "w_kvrg": np.stack([by_row(l0[n].T, 1) for n in ("Wk", "Wv", "Wr", "Wg")]),
        "w_off": np.stack([by_row(l0["Wo"].T, 0)] + [l0[n].T for n in ("fWr", "fWk", "fWv")]),
        "w_q": l1["q_w"], "w_kv": kv_w.transpose(2, 0, 1), "w_out": l1["out_w"],
        "w_mlp1": l1["mlp_w1"], "w_mlp2": l1["mlp_w2"],
        "heads": heads, "heads_sum": heads_sum, "heads_back": heads_back,
    }
    arrays = {k: np.ascontiguousarray(v) for k, v in arrays.items()}
    nc = bacc.Bacc("TRN2", target_bir_lowering=False, num_devices=1)
    args = {k: nc.dram_tensor(k, v.shape, mybir.dt.from_np(v.dtype), kind="ExternalInput").ap() for k, v in arrays.items()}
    out = nc.dram_tensor("out", [CT, P, TOK], F32, kind="ExternalOutput").ap()
    rwkv_perceiver(nc, **args, out=out)
    r = run_bass_kernel_spmd(nc, [arrays], core_ids=[0])
    got = r.results[0]["out"]
    return np.ascontiguousarray(got.reshape(C, SEQS, LEN).transpose(1, 2, 0))
```
